# Optimizing a Trainium2 kernel written in Bass

```python
import numpy as np
import jax
import jax.numpy as jnp

def _softmax(x, axis=-1):
    return jax.nn.softmax(x, axis=axis)

def _gelu(x):
    return jax.nn.gelu(x, approximate=True)

def _silu(x):
    return jax.nn.silu(x)

def _sigmoid(x):
    return jax.nn.sigmoid(x)

def _layernorm(x, axis=-1, eps=1e-05):
    m = jnp.mean(x, axis=axis, keepdims=True)
    v = jnp.var(x, axis=axis, keepdims=True)
    return (x - m) / jnp.sqrt(v + eps)

def _scatter_add(tgt, idx, src, axis=0):
    return tgt.at[idx].add(src)

def _segment_sum(src, seg, n):
    return jax.ops.segment_sum(src, seg, n)
kernel_name = 'mk_gnn_ffn_d2_gnn_r8_2d706c'

def setup_inputs(seed: int=0):
    np.random.seed(seed)
    _w = jnp.asarray

    def _rec_inputs():
        import jax
        import jax.numpy as jnp
        _gk = jax.random.key(seed)
        x = -0.0001538 + 1 * jax.random.normal(jax.random.fold_in(_gk, 1), (1536, 512), jnp.float32)
        src = jax.random.randint(jax.random.fold_in(_gk, 2), (49152,), 0, 1536, jnp.int32)
        dst = jax.random.randint(jax.random.fold_in(_gk, 3), (49152,), 0, 1536, jnp.int32)
        _o = jnp.argsort(dst, stable=True)
        src = src[_o]
        dst = dst[_o]
        return (x, src, dst)
    x, src, dst = _rec_inputs()

    def _L0_gnn_setup():
        import jax, jax.numpy as jnp
        import numpy as np
        N = 1536
        B = 64
        R = 36
        E = 24576
        D_IN = 512
        D_OUT = 512
        P = 256
        D_IMG = 1024
        key = jax.random.key(seed)
        ks = jax.random.split(key, 12)

        def w(k, shape, fan_in):
            return jax.random.normal(k, shape, dtype=jnp.float32) / np.float32(np.sqrt(fan_in))
        return {'h': jax.random.normal(ks[0], (N, D_IN), dtype=jnp.float32), 'img_feats': jax.random.normal(ks[1], (B, R, D_IMG), dtype=jnp.float32), 'batch_ids': jax.random.randint(ks[2], (N,), 0, B, dtype=jnp.int32), 'src': jax.random.randint(ks[3], (E,), 0, N, dtype=jnp.int32), 'dst': jax.random.randint(ks[4], (E,), 0, N, dtype=jnp.int32), 'Wf': w(ks[5], (D_IN, P), D_IN), 'bf': jnp.zeros((P,), jnp.float32), 'Wi': w(ks[6], (D_IMG, P), D_IMG), 'bi': jnp.zeros((P,), jnp.float32), 'Wa': w(ks[7], (P, 1), P), 'ba': jnp.zeros((1,), jnp.float32), 'Wn': w(ks[8], (D_IN, D_OUT), D_IN), 'bn': jnp.zeros((D_OUT,), jnp.float32), 'Wim': w(ks[9], (D_IMG, D_OUT), D_IMG), 'bim': jnp.zeros((D_OUT,), jnp.float32), 'Wap': w(ks[10], (2 * D_OUT, D_OUT), 2 * D_OUT), 'bap': jnp.zeros((D_OUT,), jnp.float32)}
    _L0_gnn_all = _L0_gnn_setup()
    _L0_gnn_in = {k: v for k, v in _L0_gnn_all.items() if k in ('img_feats', 'Wf', 'bf', 'Wi', 'bi', 'Wa', 'ba', 'Wn', 'bn', 'Wim', 'bim', 'Wap', 'bap')}
    del _L0_gnn_all

    def _L0_ffn_setup():
        import jax, jax.numpy as jnp
        import numpy as np
        K = 2
        EPS = 1e-06

        def _layernorm(x, gamma, beta):
            mu = jnp.mean(x, axis=-1, keepdims=True)
            var = jnp.mean(jnp.square(x - mu), axis=-1, keepdims=True)
            return (x - mu) * jax.lax.rsqrt(var + EPS) * gamma + beta
        key = jax.random.key(seed)
        ks = jax.random.split(key, 5)
        B, S, D, F, E = (8, 256, 512, 256, 8)
        x = jax.random.normal(ks[0], (B, S, D), dtype=jnp.float32)
        router_w = jax.random.normal(ks[1], (D, E), dtype=jnp.float32) * 0.02
        w1 = jax.random.normal(ks[2], (E, D, F), dtype=jnp.float32) * 0.02
        b1 = jnp.zeros((E, F), dtype=jnp.float32)
        w2 = jax.random.normal(ks[3], (E, F, D), dtype=jnp.float32) * 0.02
        b2 = jnp.zeros((E, D), dtype=jnp.float32)
        gamma = jnp.ones((E, D), dtype=jnp.float32)
        beta = jnp.zeros((E, D), dtype=jnp.float32)
        return {'x': x, 'router_w': router_w, 'w1': w1, 'b1': b1, 'w2': w2, 'b2': b2, 'gamma': gamma, 'beta': beta}
    _L0_ffn_all = _L0_ffn_setup()
    _L0_ffn_in = {k: v for k, v in _L0_ffn_all.items() if k in ('router_w', 'w1', 'b1', 'w2', 'b2', 'gamma', 'beta')}
    del _L0_ffn_all

    def _L1_gnn_setup():
        import jax, jax.numpy as jnp
        import numpy as np
        N_NODES = 6250
        N_EDGES = 18750
        D_IN = 512
        D_OUT = 512
        LN_EPS = 1e-05
        key = jax.random.key(seed)
        k_x, k_e, k_ws, k_wn = jax.random.split(key, 4)
        x = jax.random.normal(k_x, (N_NODES, D_IN), dtype=jnp.float32)
        edge_index = jax.random.randint(k_e, (2, N_EDGES), 0, N_NODES, dtype=jnp.int64)
        scale = 1.0 / np.sqrt(D_IN)
        w_self = jax.random.normal(k_ws, (D_OUT, D_IN), dtype=jnp.float32) * scale
        w_neigh = jax.random.normal(k_wn, (D_OUT, D_IN), dtype=jnp.float32) * scale
        bias = jnp.zeros((D_OUT,), dtype=jnp.float32)
        gamma = jnp.ones((D_OUT,), dtype=jnp.float32)
        beta = jnp.zeros((D_OUT,), dtype=jnp.float32)
        return {'x': x, 'edge_index': edge_index, 'w_self': w_self, 'w_neigh': w_neigh, 'bias': bias, 'gamma': gamma, 'beta': beta}
    _L1_gnn_all = _L1_gnn_setup()
    _L1_gnn_in = {k: v for k, v in _L1_gnn_all.items() if k in ('w_self', 'w_neigh', 'bias', 'gamma', 'beta')}
    del _L1_gnn_all

    def _L1_ffn_setup():
        import jax, jax.numpy as jnp
        import numpy as np
        MARK_AX = 0
        OPCODE_BASE = 16
        OP_SHL = OPCODE_BASE + 23
        OP_SHR = OPCODE_BASE + 24
        ALU_LO = 64
        ALU_HI = 80
        AX_CARRY_LO = 96
        OUTPUT_LO = 128
        OUTPUT_HI = 144
        B, SEQ, D = (8, 4096, 512)
        key = jax.random.key(seed)
        ks = jax.random.split(key, 6)
        x = jax.random.uniform(ks[0], (B, SEQ, D), dtype=jnp.float32) * 0.4
        mark = (jax.random.uniform(ks[1], (B, SEQ)) < 0.75).astype(jnp.float32)
        op_sel = jax.random.randint(ks[2], (B, SEQ), 0, 3)
        lo = jax.random.randint(ks[3], (B, SEQ), 0, 16)
        hi = jax.random.randint(ks[4], (B, SEQ), 0, 16)
        sa = jax.random.randint(ks[5], (B, SEQ), 0, 16)
        oh = lambda idx: jax.nn.one_hot(idx, 16, dtype=jnp.float32)
        x = x.at[..., MARK_AX].set(mark)
        x = x.at[..., OP_SHL].set((op_sel == 1).astype(jnp.float32))
        x = x.at[..., OP_SHR].set((op_sel == 2).astype(jnp.float32))
        x = x.at[..., ALU_LO:ALU_LO + 16].set(oh(lo))
        x = x.at[..., ALU_HI:ALU_HI + 16].set(oh(hi))
        x = x.at[..., AX_CARRY_LO:AX_CARRY_LO + 16].set(oh(sa))
        return {'x_bd': x}
    _L1_ffn_all = _L1_ffn_setup()
    _L1_ffn_in = {k: v for k, v in _L1_ffn_all.items() if k in ()}
    del _L1_ffn_all
    return {'x': x, 'src': src, 'dst': dst, 'L0_gnn_img_feats': _L0_gnn_in['img_feats'], 'L0_gnn_Wf': _L0_gnn_in['Wf'], 'L0_gnn_bf': _L0_gnn_in['bf'], 'L0_gnn_Wi': _L0_gnn_in['Wi'], 'L0_gnn_bi': _L0_gnn_in['bi'], 'L0_gnn_Wa': _L0_gnn_in['Wa'], 'L0_gnn_ba': _L0_gnn_in['ba'], 'L0_gnn_Wn': _L0_gnn_in['Wn'], 'L0_gnn_bn': _L0_gnn_in['bn'], 'L0_gnn_Wim': _L0_gnn_in['Wim'], 'L0_gnn_bim': _L0_gnn_in['bim'], 'L0_gnn_Wap': _L0_gnn_in['Wap'], 'L0_gnn_bap': _L0_gnn_in['bap'], 'L0_ffn_router_w': _L0_ffn_in['router_w'], 'L0_ffn_w1': _L0_ffn_in['w1'], 'L0_ffn_b1': _L0_ffn_in['b1'], 'L0_ffn_w2': _L0_ffn_in['w2'], 'L0_ffn_b2': _L0_ffn_in['b2'], 'L0_ffn_gamma': _L0_ffn_in['gamma'], 'L0_ffn_beta': _L0_ffn_in['beta'], 'L1_gnn_w_self': _L1_gnn_in['w_self'], 'L1_gnn_w_neigh': _L1_gnn_in['w_neigh'], 'L1_gnn_bias': _L1_gnn_in['bias'], 'L1_gnn_gamma': _L1_gnn_in['gamma'], 'L1_gnn_beta': _L1_gnn_in['beta']}

def reference(x, src, dst, L0_gnn_img_feats, L0_gnn_Wf, L0_gnn_bf, L0_gnn_Wi, L0_gnn_bi, L0_gnn_Wa, L0_gnn_ba, L0_gnn_Wn, L0_gnn_bn, L0_gnn_Wim, L0_gnn_bim, L0_gnn_Wap, L0_gnn_bap, L0_ffn_router_w, L0_ffn_w1, L0_ffn_b1, L0_ffn_w2, L0_ffn_b2, L0_ffn_gamma, L0_ffn_beta, L1_gnn_w_self, L1_gnn_w_neigh, L1_gnn_bias, L1_gnn_gamma, L1_gnn_beta):
    import jax
    import jax.numpy as jnp

    def _L0_gnn_ref(h, img_feats, batch_ids, src, dst, Wf, bf, Wi, bi, Wa, ba, Wn, bn, Wim, bim, Wap, bap):
        import jax, jax.numpy as jnp
        import numpy as np
        N = 1536
        B = 64
        R = 36
        E = 24576
        D_IN = 512
        D_OUT = 512
        P = 256
        D_IMG = 1024
        node_proj = h @ Wf + bf
        img_proj = img_feats @ Wi + bi
        img_proj_n = img_proj[batch_ids]
        logits = (jnp.tanh(node_proj[:, None, :] + img_proj_n) @ Wa)[..., 0] + ba[0]
        att = jax.nn.softmax(logits, axis=1)
        img_n = img_feats[batch_ids]
        img = jnp.einsum('nr,nrd->nd', att, img_n)
        h1 = h @ Wn + bn
        neigh = jax.ops.segment_sum(h1[src], dst, num_segments=N)
        msg = neigh + img @ Wim + bim
        out = jax.nn.relu(jnp.concatenate([msg, h1], axis=1) @ Wap + bap)
        return out

    def _L0_ffn_ref(x, router_w, w1, b1, w2, b2, gamma, beta):
        import jax, jax.numpy as jnp
        import numpy as np
        K = 2
        EPS = 1e-06

        def _layernorm(x, gamma, beta):
            mu = jnp.mean(x, axis=-1, keepdims=True)
            var = jnp.mean(jnp.square(x - mu), axis=-1, keepdims=True)
            return (x - mu) * jax.lax.rsqrt(var + EPS) * gamma + beta
        B, S, D = x.shape
        E = w1.shape[0]
        xf = x.reshape(-1, D)
        logits = xf @ router_w
        gate_vals, idx = jax.lax.top_k(logits, K)
        gates = jax.nn.softmax(gate_vals, axis=-1)
        out = jnp.zeros_like(xf)
        for e in range(E):
            h = jax.nn.relu(xf @ w1[e] + b1[e]) @ w2[e] + b2[e]
            y = _layernorm(xf + h, gamma[e], beta[e])
            w = jnp.sum(jnp.where(idx == e, gates, 0.0), axis=-1)
            out = out + w[:, None] * y
        return out.reshape(B, S, D)

    def _L1_gnn_ref(x, edge_index, w_self, w_neigh, bias, gamma, beta):
        import jax, jax.numpy as jnp
        import numpy as np
        N_NODES = 6250
        N_EDGES = 18750
        D_IN = 512
        D_OUT = 512
        LN_EPS = 1e-05
        n = x.shape[0]
        s, d = (edge_index[0], edge_index[1])
        agg = jax.ops.segment_sum(x[s], d, num_segments=n)
        cnt = jax.ops.segment_sum(jnp.ones(s.shape[0], x.dtype), d, num_segments=n)
        agg = agg / jnp.maximum(cnt, 1.0)[:, None]
        h = x @ w_self.T + agg @ w_neigh.T + bias
        mu = jnp.mean(h, axis=-1, keepdims=True)
        var = jnp.mean(jnp.square(h - mu), axis=-1, keepdims=True)
        hn = (h - mu) * jax.lax.rsqrt(var + LN_EPS) * gamma + beta
        return jax.nn.relu(hn)

    def _L1_ffn_ref(x_bd):
        import jax, jax.numpy as jnp
        import numpy as np
        MARK_AX = 0
        OPCODE_BASE = 16
        OP_SHL = OPCODE_BASE + 23
        OP_SHR = OPCODE_BASE + 24
        ALU_LO = 64
        ALU_HI = 80
        AX_CARRY_LO = 96
        OUTPUT_LO = 128
        OUTPUT_HI = 144
        B, SEQ, D = (8, 4096, 512)
        hot = x_bd > 0.5
        first16 = lambda off: jnp.argmax(hot[..., off:off + 16], axis=-1).astype(jnp.int32)
        lo = first16(ALU_LO)
        hi = first16(ALU_HI)
        sa = first16(AX_CARRY_LO)
        val = lo + 16 * hi
        shl = jnp.left_shift(val, sa) & 255
        shr = jnp.right_shift(val, sa)
        mark = hot[..., MARK_AX]
        is_shl = hot[..., OP_SHL]
        is_shr = jnp.logical_and(hot[..., OP_SHR], jnp.logical_not(is_shl))
        act_shl = jnp.logical_and(mark, is_shl)
        act_shr = jnp.logical_and(mark, is_shr)
        active = jnp.logical_or(act_shl, act_shr)
        res = jnp.where(act_shl, shl, jnp.where(act_shr, shr, 0))
        res = jnp.clip(res, 0, 255)
        rlo = res & 15
        rhi = res >> 4
        amp = 2.0 * active.astype(x_bd.dtype)
        add_lo = amp[..., None] * jax.nn.one_hot(rlo, 16, dtype=x_bd.dtype)
        add_hi = amp[..., None] * jax.nn.one_hot(rhi, 16, dtype=x_bd.dtype)
        out = x_bd.at[..., OUTPUT_LO:OUTPUT_LO + 16].add(add_lo)
        out = out.at[..., OUTPUT_HI:OUTPUT_HI + 16].add(add_hi)
        return out
    edge_index = jnp.stack([src, dst])
    batch0 = jnp.zeros((1536,), jnp.int32)
    x = x + _L0_gnn_ref(_layernorm(x, axis=-1), L0_gnn_img_feats, batch0, src, dst, L0_gnn_Wf, L0_gnn_bf, L0_gnn_Wi, L0_gnn_bi, L0_gnn_Wa, L0_gnn_ba, L0_gnn_Wn, L0_gnn_bn, L0_gnn_Wim, L0_gnn_bim, L0_gnn_Wap, L0_gnn_bap)
    x = x + _L0_ffn_ref(_layernorm(x, axis=-1)[None], L0_ffn_router_w, L0_ffn_w1, L0_ffn_b1, L0_ffn_w2, L0_ffn_b2, L0_ffn_gamma, L0_ffn_beta)[0]
    x = x + _L1_gnn_ref(_layernorm(x, axis=-1), edge_index, L1_gnn_w_self, L1_gnn_w_neigh, L1_gnn_bias, L1_gnn_gamma, L1_gnn_beta)
    x = x + _L1_ffn_ref(_layernorm(x, axis=-1)[None])[0]
    return x

_drawn_inputs = setup_inputs


def setup_inputs(seed=0):
    import zlib

    import numpy as np

    out = dict(_drawn_inputs(seed))
    spreads = {'L0_gnn_bf': (0.0, 0.8),
     'L0_gnn_bi': (0.0, 0.8),
     'L0_gnn_bn': (0.0, 0.1),
     'L0_gnn_bim': (0.0, 0.46),
     'L0_gnn_bap': (0.0, 0.358),
     'L0_ffn_b1': (0.0, 0.8),
     'L0_ffn_b2': (0.0, 0.468),
     'L0_ffn_gamma': (1.0, 0.2),
     'L0_ffn_beta': (0.0, 0.49),
     'L1_gnn_bias': (0.0, 0.502),
     'L1_gnn_gamma': (1.0, 0.2),
     'L1_gnn_beta': (0.0, 0.496)}
    factors = {'L0_gnn_Wf': 8.0,
     'L0_gnn_Wi': 3.703,
     'L0_gnn_Wa': 4.044,
     'L0_ffn_w1': 3.839,
     'L0_ffn_w2': 3.132}
    for name, (base, spread) in spreads.items():
        noise = np.random.default_rng([zlib.crc32(name.encode()), seed]).standard_normal(out[name].shape)
        drawn = base * np.exp(spread * noise) if base else spread * noise
        out[name] = jnp.asarray(drawn.astype(out[name].dtype))
    for name, factor in factors.items():
        out[name] = (out[name] * factor).astype(out[name].dtype)
    return out
```

```python
from contextlib import ExitStack

import concourse.bass as bass
from concourse import mybir

ALU = mybir.AluOpType
ACT = mybir.ActivationFunctionType
F32 = mybir.dt.float32
BF16 = mybir.dt.bfloat16
I32 = mybir.dt.int32
U32 = mybir.dt.uint32
U16 = mybir.dt.uint16
I16 = mybir.dt.int16
AX_X = mybir.AxisListType.X

P = 128
RSQRT_MAGIC = 1597463007.0
TOPK = 2
GNN_EPS = 1e-5
EXPERT_EPS = 1e-6


def gnn_moe_kernel(nc, x, src, dst, img, wf, bf, wi, bi, wa, ba, wn, bn, wim, bim, wap, bap,
                   router, w1, b1, w2, b2, ffn_gamma, ffn_beta,
                   w_self, w_neigh, l1_bias, l1_gamma, l1_beta, out, xf_dram, y_dram):
    N, D = x.shape
    NB = N // P
    DC = D // P
    NJ = N // 512
    JB = 512 // P
    EC = src.shape[1]
    KI, R = img.shape[1], img.shape[2]
    PJ = wf.shape[1]
    PC = PJ // P
    NE, F = w1.shape[0], w1.shape[2]
    FC = F // P
    NCH = (N * TOPK + NE * (P - 1)) // P
    SW = 32
    GC = 4
    EG = EC // GC
    WIN = 24
    XG = 3
    GB = NB // XG
    assert EG == 3 * R - 12 and PC == 2 and NCH <= SW and D == 512 and N % 512 == 0 and NCH == 31

    with ExitStack() as ctx:
        def sb(name, shape, dt=F32):
            return ctx.enter_context(nc.sbuf_tensor(name, shape, dt))

        def sem(name):
            return ctx.enter_context(nc.semaphore(name))

        ps = ctx.enter_context(nc.psum_tensor("ps", [P, 8, 512], F32))

        arena = sb("arena", [P, 4 * NB * D + NE * DC * F])
        AX = 0
        AW = AX + NB * D
        AH = AW + NE * DC * F
        AT = AH + NB * D
        AN = AT + NB * D

        def at(start, size):
            return arena[:, start:start + size]

        x_sb = at(AX, NB * D).rearrange("p (b d) -> p b d", b=NB)
        xn = at(AN, NB * D).rearrange("p (b d) -> p b d", b=NB)
        xT = at(AT, NB * D).rearrange("p (c n) -> p c n", c=DC)
        hT = at(AH, NB * D).rearrange("p (c n) -> p c n", c=DC)
        node_proj = at(AX, PC * N).rearrange("p (m n) -> p m n", m=PC)
        tanh_t = at(AX + PC * N, PC * N).rearrange("p (m n) -> p m n", m=PC)
        wi_sb = at(AH, KI * PJ).rearrange("p (k n) -> p k n", k=KI)
        wim_sb = at(AH + KI * PJ, KI * D).rearrange("p (k n) -> p k n", k=KI)
        wf_sb = at(AW, DC * PJ).rearrange("p (k n) -> p k n", k=DC)
        wn_sb = at(AW + DC * PJ, DC * D).rearrange("p (k n) -> p k n", k=DC)
        wap_sb = at(AW + DC * (PJ + D), 2 * DC * D).rearrange("p (k n) -> p k n", k=2 * DC)
        w1_sb = at(AW, NE * DC * F)
        w2_sb = at(AH, NE * FC * D)
        w2_cut = NB * D // (FC * D)
        b1_row = at(AH + NE * FC * D, NE * F)
        b2_row = at(AH + NE * FC * D + NE * F, NE * D)
        gamma_row = at(AH + NE * FC * D + NE * F + NE * D, NE * D)
        y_top = at(AT, TOPK * NB * D).rearrange("p (k b d) -> p k b d", k=TOPK, b=NB)
        ws_sb = at(AW, DC * D).rearrange("p (k n) -> p k n", k=DC)
        wg_sb = at(AW + DC * D, DC * D).rearrange("p (k n) -> p k n", k=DC)
        assert AH + NE * FC * D + NE * F + 2 * NE * D <= AN + NB * D

        counts = sb("counts", [P, NB, N], U16)

        work = sb("work", [P, 6656])
        src_f = work[:, 0:EC]
        dst_f = work[:, EC:2 * EC]
        src_k = work[:, 2 * EC:3 * EC]
        src_i = work[:, 3 * EC:4 * EC].bitcast(I32)
        dst_i = work[:, 4 * EC:5 * EC].bitcast(I32)
        oh_dst = work[:, 5 * EC:5 * EC + N].bitcast(BF16).rearrange("p (b n) -> p b n", b=2)
        oh_src = work[:, 5 * EC + N:5 * EC + N + 2 * P].bitcast(BF16).rearrange("p (b n) -> p b n", b=2)
        iota_n = work[:, 5 * EC + N + 2 * P:5 * EC + N + 2 * P + N // 2].bitcast(I16)
        lo_f = work[:, 2 * EC:3 * EC]
        win_f = work[:, 5 * EC + N + 2 * P + N // 2:6 * EC + N + 2 * P + N // 2]
        edge_t = work[:, 5 * EC:6 * EC]
        edge_u = work[:, 6 * EC:7 * EC]
        oh_lo = work[:, 5 * EC:5 * EC + GC * P // 2].bitcast(BF16).rearrange("p (b n) -> p b n", b=GC)
        oh_win = work[:, 5 * EC + GC * P // 2:5 * EC + GC * (P + NB * WIN) // 2].bitcast(BF16).rearrange(
            "p (b n) -> p b n", b=GC)
        att = work[:, 0:NB * R].rearrange("p (b r) -> p b r", b=NB)
        att_red = work[:, 448:448 + NB]
        att_inv = work[:, 464:464 + NB]
        attT = work[:, 512:512 + N]
        out_t = work[:, 2048:2048 + 2 * D].rearrange("p (b d) -> p b d", b=2)
        gate_T = work[:, 0:N]
        xs = work[:, 0:1024].rearrange("p (b d) -> p b d", b=2)
        xb = work[:, 1024:2048].rearrange("p (b d) -> p b d", b=2)
        xsT = work[:, 2048:3072].rearrange("p (b c n) -> p b c n", b=2, c=DC)
        hb = work[:, 3072:3072 + 2 * F].rearrange("p (b f) -> p b f", b=2)
        hbT = work[:, 3584:3584 + 2 * F].rearrange("p (b c n) -> p b c n", b=2, c=FC)
        yt = work[:, 4096:5120].rearrange("p (b d) -> p b d", b=2)
        yu = work[:, 5120:6144].rearrange("p (b d) -> p b d", b=2)
        l1g_row = work[:, 0:D]
        l1b_row = work[:, D:2 * D]
        h_t = work[:, 2 * D:3 * D]
        hot = work[:, 3072:3072 + NB * 48].rearrange("p (b c) -> p b c", b=NB)
        nib = work[:, 3712:3712 + NB * 3].rearrange("p (b c) -> p b c", b=NB)
        nib_pos = work[:, 3776:3776 + NB * 3].rearrange("p (b c) -> p b c", b=NB)
        mark = work[:, 3840:3840 + NB]
        is_shl = work[:, 3856:3856 + NB]
        is_shr = work[:, 3872:3872 + NB]
        not_shl = work[:, 3888:3888 + NB]
        val_f = work[:, 3904:3904 + NB]
        val_i = work[:, 3920:3920 + NB].bitcast(I32)
        sa_i = work[:, 3936:3936 + NB].bitcast(I32)
        shl_i = work[:, 3952:3952 + NB].bitcast(I32)
        shr_i = work[:, 3968:3968 + NB].bitcast(I32)
        shl_f = work[:, 3984:3984 + NB]
        shr_f = work[:, 4000:4000 + NB]
        res_i = work[:, 4016:4016 + NB].bitcast(I32)
        out_ni = work[:, 4032:4032 + 2 * NB].rearrange("p (b k) -> p b k", b=NB).bitcast(I32)
        out_nf = work[:, 4064:4064 + 2 * NB].rearrange("p (b k) -> p b k", b=NB)
        out_oh = work[:, 4096:4096 + NB * 32].rearrange("p (b k i) -> p b k i", b=NB, k=2)
        amp = work[:, 4480:4480 + NB]

        ident = sb("ident", [P, P])
        ones_bf = sb("ones_bf", [P, P], BF16)
        before_bf = sb("before_bf", [P, P], BF16)
        ones_col = sb("ones_col", [P, 1])
        row0 = sb("row0", [P, P])
        base_f = sb("base_f", [P, EG])
        base_i = sb("base_i", [P, EG], I32)
        outside = sb("outside", [P, 2])
        outside_bf = sb("outside_bf", [P, 1], BF16)
        loose = sb("loose", [P, 1], I32)
        iota_i = sb("iota_i", [P, P], I32)
        iota_f = sb("iota_f", [P, P])
        iota_pi = sb("iota_pi", [P, 1], I32)
        iota_p = sb("iota_p", [P, 1])
        key_i = sb("key_i", [P, 16], I32)
        first_key = sb("first_key", [P, 16])
        block_col = sb("block_col", [P, NB])
        img_sb = sb("img_sb", [P, KI, R])
        bfi = sb("bfi", [P, 2, PC])
        bfi_sum = sb("bfi_sum", [P, PC])
        wa_sb = sb("wa_sb", [P, PC])
        ba_sb = sb("ba_sb", [P, 1])
        bn_sb = sb("bn_sb", [P, DC])
        bim_sb = sb("bim_sb", [P, DC])
        row_bias = sb("row_bias", [P, D])
        img_bias = sb("img_bias", [P, PC, R])
        img_ctx = work[:, 5120:5120 + D]
        stats = sb("stats", [P, NB, 6])
        mv = sb("mv", [P, NB, 2])
        var_e = sb("var_e", [P, NB])
        rstd = sb("rstd", [P, NB])
        nt_a = sb("nt_a", [P, NB])
        nt_b = sb("nt_b", [P, NB])
        cf = work[:, 5632:6656].rearrange("p (b n) -> p b n", b=2)

        rw_sb = sb("rw_sb", [P, DC, NE])
        logits = sb("logits", [P, NB, NE])
        top_v = sb("top_v", [P, NB, 8])
        top_i = sb("top_i", [P, NB, 8], U32)
        top_f = sb("top_f", [P, TOPK, NB])
        gate_d = sb("gate_d", [P, NB])
        gate_e = sb("gate_e", [P, NB])
        gates = sb("gates", [P, TOPK, NB])
        sel = sb("sel", [P, TOPK, NB, NE])
        sel_bf = sb("sel_bf", [P, (2 * NB - 1) * NE], BF16)
        gate_w = sb("gate_w", [P, 2, NB, NE])
        beta_sb = sb("beta_sb", [NE, D])
        pos = sb("pos", [P, NB, NE])
        pos_t = sb("pos_t", [P, NB, NE])
        cnt_i = sb("cnt_i", [P, NE], I32)
        cnt_f = sb("cnt_f", [P, NE])
        end_f = sb("end_f", [P, NE])
        off_f = sb("off_f", [P, NE])
        one_f = sb("one_f", [P, NE])
        slot_f = sb("slot_f", [P, TOPK, NB])
        slot_i = sb("slot_i", [P, TOPK, NB], I32)
        slot_hi = sb("slot_hi", [P, TOPK, NB], I32)
        slot_lo = sb("slot_lo", [P, TOPK, NB], I32)
        slot_hf = sb("slot_hf", [P, TOPK, NB])
        slot_lf = sb("slot_lf", [P, TOPK, NB])
        lo_oh = sb("lo_oh", [P, 2, P], BF16)
        hi_oh = sb("hi_oh", [P, 2, 2 * SW], BF16)
        chunk_ge = work[:, 2048:2048 + SW * NE].rearrange("p (c e) -> p c e", e=NE)
        chunk_ef = sb("chunk_ef", [P, SW])
        chunk_e = sb("chunk_e", [P, SW], I32)
        tok_f = sb("tok_f", [P, SW])
        tok = sb("tok", [P, SW], U32)
        e_mv = sb("e_mv", [P, 2, 8])
        e_stats = sb("e_stats", [P, 2, 6])
        deg = sb("deg", [P, NB])
        deg_inv = sb("deg_inv", [P, NB])

        x_in = [sem(f"x_in{g}") for g in range(XG)]
        edges_in = sem("edges_in")
        img_in = sem("img_in")
        attw_in = sem("attw_in")
        gnnw_in = sem("gnnw_in")
        x_again = sem("x_again")
        w1_in = sem("w1_in")
        w2_in = sem("w2_in")
        ffn_rows_in = sem("ffn_rows_in")
        l1w_in = sem("l1w_in")
        xf_out = sem("xf_out")
        consts_ready = sem("consts_ready")
        pool_order = sem("pool_order")
        dve_order = sem("dve_order")
        edge_oh = sem("edge_oh")
        edge_oh_used = sem("edge_oh_used")
        pass_out = sem("pass_out")
        src_k_ready = sem("src_k_ready")
        edges_f = sem("edges_f")
        base_ps = sem("base_ps")
        outside_ready = sem("outside_ready")
        outside_ps = sem("outside_ps")
        loose_ready = sem("loose_ready")
        win_oh = sem("win_oh")
        win_oh_used = sem("win_oh_used")
        win_bank_free = sem("win_bank_free")
        counts_zero = sem("counts_zero")
        counts_ready = sem("counts_ready")
        xn_ready = sem("xn_ready")
        tr_ps = sem("tr_ps")
        tr_sb = sem("tr_sb")
        img_ps = sem("img_ps")
        img_bias_ready = sem("img_bias_ready")
        img_ctx_ready = sem("img_ctx_ready")
        proj_ps = sem("proj_ps")
        proj_sb = sem("proj_sb")
        tanh_sb = sem("tanh_sb")
        att_ps = sem("att_ps")
        att_shift = sem("att_shift")
        att_exp = sem("att_exp")
        att_ready = sem("att_ready")
        h1_ps = sem("h1_ps")
        h1_sb = sem("h1_sb")
        cf_ready = sem("cf_ready")
        cf_used = sem("cf_used")
        agg_ps = sem("agg_ps")
        agg_sb = sem("agg_sb")
        out_ps = sem("out_ps")
        out_read = sem("out_read")
        router_ps = sem("router_ps")
        gate_diff = sem("gate_diff")
        gate_exp = sem("gate_exp")
        sel_ready = sem("sel_ready")
        gatew_ready = sem("gatew_ready")
        pos_ps = sem("pos_ps")
        slot_oh = sem("slot_oh")
        slot_ps = sem("slot_ps")
        tok_ready = sem("tok_ready")
        beta_ps = sem("beta_ps")
        beta_read = sem("beta_read")
        xs_in = [sem(f"xs_in{i}") for i in range(2)]
        xs_ps = sem("xs_ps")
        xs_T = sem("xs_T")
        hid_ps = sem("hid_ps")
        hid_sb = sem("hid_sb")
        hidT_ps = sem("hidT_ps")
        hidT_sb = sem("hidT_sb")
        y_ps = sem("y_ps")
        xb_ready = sem("xb_ready")
        yt_ready = sem("yt_ready")
        sd_ready = sem("sd_ready")
        yu_ready = sem("yu_ready")
        yg_ready = sem("yg_ready")
        y_out = [sem(f"y_out{i}") for i in range(2)]
        y_top_in = [sem(f"y_top_in{b}") for b in range(NB)]
        deg_zero = sem("deg_zero")
        yv_ready = sem("yv_ready")
        es_ready = sem("es_ready")
        em_ready = sem("em_ready")
        er_ready = sem("er_ready")
        l1_ps = sem("l1_ps")
        l1_read = sem("l1_read")
        fin_ready = sem("fin_ready")
        out_done = sem("out_done")

        TR_X, TR_H1, TR_ATT = 0, NB, 2 * NB
        TR_XF = TR_ATT + NJ
        TR_GATE = TR_XF + NB
        TR_X3 = TR_GATE + NJ

        xb_dram = x.rearrange("(b p) d -> p b d", p=P)
        out_dram = out.rearrange("(b p) d -> p b d", p=P)

        block = ctx.enter_context(nc.Block())

        @block.sync
        def _(sp):
            sp.dma_start(src_i, src).then_inc(edges_in, 16)
            sp.dma_start(dst_i, dst).then_inc(edges_in, 16)
            for g in range(XG):
                sp.dma_start(x_sb[:, g * GB:(g + 1) * GB, :], xb_dram[:, g * GB:(g + 1) * GB, :]).then_inc(x_in[g], 16)
            sp.dma_start(img_sb[:], img).then_inc(img_in, 16)
            sp.dma_start(bfi[:, 0, :], bf).then_inc(img_in, 16)
            sp.dma_start(bfi[:, 1, :], bi).then_inc(img_in, 16)
            sp.dma_start(wi_sb, wi.rearrange("(k p) n -> p k n", p=P)).then_inc(img_in, 16)
            sp.dma_start(wim_sb, wim.rearrange("(k p) n -> p k n", p=P)).then_inc(img_in, 16)
            sp.dma_start(wf_sb, wf.rearrange("(k p) n -> p k n", p=P)).then_inc(attw_in, 16)
            sp.dma_start(wa_sb[:], wa).then_inc(attw_in, 16)
            sp.dma_start(ba_sb[:], ba.partition_broadcast(P)).then_inc(attw_in, 16)
            sp.dma_start(wn_sb, wn.rearrange("(k p) n -> p k n", p=P)).then_inc(gnnw_in, 16)
            sp.dma_start(wap_sb, wap.rearrange("(k p) n -> p k n", p=P)).then_inc(gnnw_in, 16)
            sp.dma_start(bn_sb[:], bn).then_inc(gnnw_in, 16)
            sp.dma_start(bim_sb[:], bim).then_inc(gnnw_in, 16)
            sp.dma_start(row_bias[:], bap.partition_broadcast(P)).then_inc(gnnw_in, 16)
            sp.dma_start(rw_sb[:], router.rearrange("(k p) n -> p k n", p=P)).then_inc(gnnw_in, 16)
            sp.dma_start(beta_sb[:], ffn_beta).then_inc(gnnw_in, 16)
            sp.wait_ge(att_ps, PC * R)
            sp.dma_start(x_sb, xb_dram).then_inc(x_again, 16)
            sp.wait_ge(out_ps, NB)
            sp.dma_start(w1_sb.rearrange("p (e k f) -> p e k f", e=NE, k=DC),
                         w1.rearrange("e (k p) f -> p e k f", p=P)).then_inc(w1_in, 16)
            w2v = w2_sb.rearrange("p (e k d) -> p e k d", e=NE, k=FC)
            w2d = w2.rearrange("e (k p) d -> p e k d", p=P)
            sp.dma_start(w2v[:, 0:w2_cut], w2d[:, 0:w2_cut]).then_inc(w2_in, 16)
            sp.wait_ge(xn_ready, 2 * NB)
            sp.dma_start(xf_dram.rearrange("(b p) d -> p b d", p=P), xn).then_inc(xf_out, 16)
            sp.wait_ge(router_ps, 1)
            sp.dma_start(w2v[:, w2_cut:NE], w2d[:, w2_cut:NE]).then_inc(w2_in, 16)
            sp.dma_start(b1_row, b1.partition_broadcast(P)).then_inc(ffn_rows_in, 16)
            sp.wait_ge(xf_out, 16)
            sp.dma_start(b2_row, b2.partition_broadcast(P)).then_inc(ffn_rows_in, 16)
            sp.dma_start(gamma_row, ffn_gamma.partition_broadcast(P)).then_inc(ffn_rows_in, 16)

            def store(j, b):
                sp.wait_ge(yg_ready, j + 1)
                sp.dma_start(y_dram[bass.ds(j * P, P), :], yu[:, b, :]).then_inc(y_out[b], 16)

            with sp.Fori(0, NCH - 1, 2) as j:
                store(j, 0)
                store(j + 1, 1)
            store(NCH - 1, 0)

            sp.wait_ge(hid_ps, NCH)
            sp.dma_start(ws_sb, w_self.rearrange("(k p) n -> p k n", p=P)).then_inc(l1w_in, 16)
            sp.dma_start(wg_sb, w_neigh.rearrange("(k p) n -> p k n", p=P)).then_inc(l1w_in, 16)
            sp.dma_start(row_bias[:], l1_bias.partition_broadcast(P)).then_inc(l1w_in, 16)
            sp.wait_ge(xs_ps, NCH)
            sp.wait_ge(xb_ready, NCH)
            sp.dma_start(l1g_row, l1_gamma.partition_broadcast(P)).then_inc(l1w_in, 16)
            sp.dma_start(l1b_row, l1_beta.partition_broadcast(P)).then_inc(l1w_in, 16)
            for b in range(NB):
                sp.wait_ge(fin_ready, b + 1)
                sp.dma_start(out_dram[:, b, :], x_sb[:, b, :]).then_inc(out_done, 16)
            sp.wait_ge(out_done, 16 * NB)
            for i in range(2):
                sp.wait_ge(y_out[i], 16 * ((NCH + 1 - i) // 2))

        @block.gpsimd
        def _(pool):
            pool.memset(ident[:], 0.0).then_inc(pool_order, 1)
            pool.memset(before_bf[:], 0.0).then_inc(pool_order, 1)
            pool.memset(row0[:], 0.0).then_inc(pool_order, 1)
            pool.wait_ge(pool_order, 3)
            pool.memset(row0[0:1, :], 1.0).then_inc(consts_ready, 1)
            pool.affine_select(out=ident[:], in_=ident[:], compare_op=ALU.not_equal, fill=1.0, base=0,
                               pattern=[[-1, P]], channel_multiplier=1).then_inc(consts_ready, 1)
            pool.affine_select(out=before_bf[:], in_=before_bf[:], compare_op=ALU.is_ge, fill=1.0, base=0,
                               pattern=[[-1, P]], channel_multiplier=1).then_inc(consts_ready, 1)
            pool.memset(ones_bf[:], 1.0).then_inc(consts_ready, 1)
            pool.memset(ones_col[:], 1.0).then_inc(consts_ready, 1)
            pool.iota(iota_n, pattern=[[1, N]], base=0, channel_multiplier=0).then_inc(consts_ready, 1)
            pool.iota(iota_i[:], pattern=[[1, P]], base=0, channel_multiplier=0).then_inc(consts_ready, 1)
            pool.iota(key_i[:], pattern=[[-1, 16]], base=16, channel_multiplier=0).then_inc(consts_ready, 1)
            pool.iota(iota_pi[:], pattern=[[1, 1]], base=0, channel_multiplier=1).then_inc(consts_ready, 1)
            pool.memset(counts[:].rearrange("p b n -> p (b n)").bitcast(F32), 0.0).then_inc(counts_zero, 1)

            def count_tiles(layer):
                for j in range(NJ):
                    for s in range(NB):
                        n = (layer * NJ + j) * NB + s
                        if n == 0:
                            pool.wait_ge(counts_ready, 1)
                        if n >= 2:
                            pool.wait_ge(cf_used, n - 1)
                        pool.tensor_copy(cf[:, n % 2, :], counts[:, s, j * 512:(j + 1) * 512]).then_inc(cf_ready, 1)

            count_tiles(0)

            def gather(j):
                if j == 0:
                    pool.wait_ge(tok_ready, 2)
                    pool.wait_ge(xf_out, 16)
                    pool.wait_ge(beta_ps, NB)
                if j >= 2:
                    pool.wait_ge(xs_ps, j - 1)
                    pool.wait_ge(xb_ready, j - 1)
                pool.indirect_dma_start(out=xs[:, j % 2, :], out_offset=None, in_=xf_dram,
                                        in_offset=bass.IndirectOffsetOnAxis(tok[:, j:j + 1], 0)
                                        ).then_inc(xs_in[j % 2], 16)

            def scale(j):
                e = pool.value_load(chunk_e[0:1, j:j + 1], min_val=0, max_val=NE - 1)
                pool.wait_ge(yu_ready, j + 1)
                pool.tensor_tensor(yu[:, j % 2, :], yu[:, j % 2, :], gamma_row[:, bass.ds(e * D, D)],
                                   ALU.mult).then_inc(yg_ready, 1)

            gather(0)
            for j in range(NCH):
                if j + 1 < NCH:
                    gather(j + 1)
                e = pool.value_load(chunk_e[0:1, j:j + 1], min_val=0, max_val=NE - 1)
                if j == 0:
                    pool.wait_ge(ffn_rows_in, 48)
                if j >= 2:
                    pool.wait_ge(yt_ready, j - 1)
                pool.wait_ge(xs_in[j % 2], 16 * (j // 2 + 1))
                pool.tensor_tensor(xb[:, j % 2, :], xs[:, j % 2, :], b2_row[:, bass.ds(e * D, D)],
                                   ALU.add).then_inc(xb_ready, 1)
                if j >= 3:
                    scale(j - 3)
            for j in range(NCH - 3, NCH):
                scale(j)
            for i in range(2):
                pool.wait_ge(y_out[i], 16 * ((NCH + 1 - i) // 2))
            pool.wait_ge(yg_ready, NCH)
            for b in range(NB):
                for k in range(TOPK):
                    pool.indirect_dma_start(out=y_top[:, k, b, :], out_offset=None, in_=y_dram,
                                            in_offset=bass.IndirectOffsetOnAxis(slot_i[:, k, b:b + 1].bitcast(U32), 0)
                                            ).then_inc(y_top_in[b], 16)
            count_tiles(1)

        @block.tensor
        def _(pe):
            mm = nc.tensor.matmul

            pe.wait_ge(img_in, 80)
            for m in range(PC):
                for k in range(KI):
                    last = mm(ps[:, 0, m * R:(m + 1) * R], wi_sb[:, k, m * P:(m + 1) * P], img_sb[:, k, :],
                              start=(k == 0), stop=(k == KI - 1))
            last.then_inc(img_ps, 1)
            for k in range(KI):
                last = mm(ps[0:R, 1, :], img_sb[:, k, :], wim_sb[:, k, :], start=(k == 0), stop=(k == KI - 1))
            last.then_inc(img_ps, 1)

            def turn(t, pieces):
                if t >= 2:
                    pe.wait_ge(tr_sb, t - 1)
                for to, fr in pieces:
                    last = nc.tensor.transpose(to, fr, ident[0:fr.shape[0], 0:fr.shape[0]])
                last.then_inc(tr_ps, 1)

            def turn_rows(t0, rows, ready, n0):
                for b in range(NB):
                    pe.wait_ge(ready, n0 + b + 1)
                    bank = ps[:, 6 + (t0 + b) % 2, :]
                    turn(t0 + b, [(bank[:, c * P:(c + 1) * P], rows[:, b, c * P:(c + 1) * P]) for c in range(DC)])

            pe.wait_ge(consts_ready, 9)
            turn_rows(TR_X, xn, xn_ready, 0)

            pe.wait_ge(edges_f, 1)
            pe.wait_ge(img_bias_ready, 1)
            mm(ps[:, 0, 0:EG], row0[:], dst_f[:, 0:EC:GC], start=True, stop=True).then_inc(base_ps, 1)

            pe.wait_ge(attw_in, 48)
            pe.wait_ge(tr_sb, TR_X + NB)
            for t in range(PC * NJ):
                m, j = t // NJ, t % NJ
                if t >= 4:
                    pe.wait_ge(proj_sb, t - 3)
                for k in range(DC):
                    last = mm(ps[:, 2 + t % 4, :], wf_sb[:, k, m * P:(m + 1) * P], xT[:, k, j * 512:(j + 1) * 512],
                              start=(k == 0), stop=(k == DC - 1))
                last.then_inc(proj_ps, 1)

            pe.wait_ge(outside_ready, 1)
            pe.wait_ge(img_ctx_ready, 1)
            mm(ps[:, 1, 0:1], ones_bf[:], outside_bf[:], start=True, stop=True).then_inc(outside_ps, 1)
            pe.wait_ge(loose_ready, 1)
            pe.wait_ge(proj_sb, PC * NJ)

            def logits_tile(r, m, n):
                pe.wait_ge(tanh_sb, n)
                for b in range(NB):
                    last = mm(ps[:, m, bass.ds(r * NB + b, 1)], tanh_t[:, m, b * P:(b + 1) * P],
                              wa_sb[:, m:m + 1], start=True, stop=True)
                last.then_inc(att_ps, 1)

            def window_chunk(c, g, q):
                if q % GC == 0:
                    pe.wait_ge(win_bank_free, g + 1)
                pe.wait_ge(win_oh, c + 1)
                mm(ps[:, 4 + (q // GC) % 2, 0:NB * WIN], oh_lo[:, q % GC, :], oh_win[:, q % GC, :],
                   start=(q % GC == 0), stop=(q % GC == GC - 1)).then_inc(win_oh_used, 1)

            with pe.Fori(0, EC // 24) as i:
                for u in range(2 * PC):
                    logits_tile(2 * i + u // PC, u % PC, 2 * PC * i + (u + 1))
                    for q in range(6 * u, 6 * u + 6):
                        window_chunk(24 * i + q, 6 * i + q // GC, q)
            for r in range(EC // 12, R):
                for m in range(PC):
                    logits_tile(r, m, PC * r + m + 1)

            def count_chunk(k, c, b, start, stop):
                pe.wait_ge(edge_oh, k * EC + c + 1)
                for s in range(2):
                    for j in range(NJ):
                        last = mm(ps[:, 2 + s * NJ + j, :], oh_src[:, b, s * P:(s + 1) * P],
                                  oh_dst[:, b, j * 512:(j + 1) * 512], start=start, stop=stop)
                last.then_inc(edge_oh_used, 1)

            pe.wait_ge(loose_ready, 1)
            n_loose = pe.value_load(loose[0:1, 0:1], min_val=0, max_val=P)
            with pe.If(n_loose > 0):
                pe.wait_ge(win_bank_free, EG + 2)
                for k in range(NB // 2):
                    if k >= 1:
                        pe.wait_ge(pass_out, k)
                    count_chunk(k, 0, 0, True, False)
                    with pe.Fori(0, EC // 2 - 1) as c:
                        count_chunk(k, 2 * c + 1, 1, False, False)
                        count_chunk(k, 2 * c + 2, 0, False, False)
                    count_chunk(k, EC - 1, 1, False, True)

            pe.wait_ge(gnnw_in, 112)
            pe.wait_ge(win_bank_free, EG + 2)
            for t in range(DC * NJ):
                j, m = t // DC, t % DC
                if t >= 4:
                    pe.wait_ge(h1_sb, t - 3)
                for k in range(DC):
                    last = mm(ps[:, 2 + t % 4, :], wn_sb[:, k, m * P:(m + 1) * P], xT[:, k, j * 512:(j + 1) * 512],
                              start=(k == 0), stop=(k == DC - 1))
                last.then_inc(h1_ps, 1)
            for b in range(NB):
                pe.wait_ge(h1_sb, DC * (b // JB + 1))
                bank = ps[:, 6 + (TR_H1 + b) % 2, :]
                turn(TR_H1 + b, [(bank[:, c * P:(c + 1) * P], hT[:, c, b * P:(b + 1) * P]) for c in range(DC)])
            pe.wait_ge(att_ready, 1)
            for j in range(NJ):
                bank = ps[0:R, 6 + (TR_ATT + j) % 2, :]
                turn(TR_ATT + j, [(bank[:, i * P:(i + 1) * P], att[:, j * JB + i, :]) for i in range(JB)])

            def aggregate(layer, rows):
                for j in range(NJ):
                    for m in range(DC):
                        t = (layer * NJ + j) * DC + m
                        if t >= 6 and (layer == 0 or j * DC + m >= 6):
                            pe.wait_ge(agg_sb, t - 5)
                    for s in range(NB):
                        n = (layer * NJ + j) * NB + s
                        pe.wait_ge(cf_ready, n + 1)
                        for m in range(DC):
                            last = mm(ps[:, (j * DC + m) % 6, :], rows[:, s, m * P:(m + 1) * P], cf[:, n % 2, :],
                                      start=(s == 0), stop=(layer == 1 and s == NB - 1))
                            if layer == 1 and s == NB - 1:
                                last.then_inc(agg_ps, 1)
                        if layer == 1:
                            for i in range(JB):
                                last = mm(ps[:, 7, j * JB + i:j * JB + i + 1], cf[:, n % 2, i * P:(i + 1) * P],
                                          ones_col[:], start=False, stop=True, skip_group_check=True)
                        last.then_inc(cf_used, 1)
                    if layer == 0:
                        for m in range(DC):
                            mm(ps[:, (j * DC + m) % 6, :], img_ctx[0:R, m * P:(m + 1) * P],
                               attT[0:R, j * 512:(j + 1) * 512], start=False, stop=True).then_inc(agg_ps, 1)

            pe.wait_ge(tr_sb, TR_ATT + NJ)
            aggregate(0, xn)

            for b in range(NB):
                if b % JB == 0:
                    pe.wait_ge(agg_sb, DC * (b // JB + 1))
                if b == 0:
                    pe.wait_ge(agg_sb, DC * NJ)
                if b >= 4:
                    pe.wait_ge(out_read, b - 3)
                for k in range(2 * DC):
                    rows = xT[:, k, b * P:(b + 1) * P] if k < DC else hT[:, k - DC, b * P:(b + 1) * P]
                    last = mm(ps[:, b % 4, :], rows, wap_sb[:, k, :], start=(k == 0), stop=(k == 2 * DC - 1))
                last.then_inc(out_ps, 1)

            turn_rows(TR_XF, xn, xn_ready, NB)
            pe.wait_ge(tr_sb, TR_XF + NB)
            pe.wait_ge(out_read, NB)
            for b in range(NB):
                for k in range(DC):
                    last = mm(ps[:, 0, b * NE:(b + 1) * NE], xT[:, k, b * P:(b + 1) * P], rw_sb[:, k, :],
                              start=(k == 0), stop=(k == DC - 1))
            last.then_inc(router_ps, 1)

            pe.wait_ge(sel_ready, 1)
            for s in range(NB):
                mm(ps[:, 1, 0:NB * NE], before_bf[:] if s == 0 else ones_bf[:],
                   sel_bf[:, (NB - 1 - s) * NE:(2 * NB - 1 - s) * NE], start=(s == 0), stop=(s == NB - 1))
            for b in range(NB):
                last = mm(ps[:, 2, 0:NE], ones_bf[:], sel_bf[:, (NB - 1 + b) * NE:(NB + b) * NE],
                          start=(b == 0), stop=(b == NB - 1))
            last.then_inc(pos_ps, 1)

            for n in range(TOPK * NB):
                pe.wait_ge(slot_oh, n + 1)
                mm(ps[:, 3, 0:2 * SW], lo_oh[:, n % 2, :], hi_oh[:, n % 2, :],
                   start=(n == 0), stop=(n == TOPK * NB - 1)).then_inc(slot_ps, 1)

            pe.wait_ge(gatew_ready, 1)
            for j in range(NJ):
                bank = ps[0:NE, 6 + (TR_GATE + j) % 2, :]
                turn(TR_GATE + j, [(bank[:, i * P:(i + 1) * P], gate_w[:, 0, j * JB + i, :]) for i in range(JB)])
            pe.wait_ge(tr_sb, TR_GATE + NJ)
            for b in range(NB):
                if b >= 2:
                    pe.wait_ge(beta_read, b - 1)
                mm(ps[:, 4 + b % 2, :], gate_T[0:NE, b * P:(b + 1) * P], beta_sb[:], start=True,
                   stop=True).then_inc(beta_ps, 1)

            pe.wait_ge(w1_in, 16)
            pe.wait_ge(w2_in, 32)
            pe.wait_ge(tok_ready, 2)
            pe.wait_ge(beta_read, NB)

            def turn_tokens(j, b, half, free):
                pe.wait_ge(xs_in[b], 16 * (half + 1))
                if free is not None:
                    pe.wait_ge(xs_T, free)
                for c in range(DC):
                    last = nc.tensor.transpose(ps[:, 4 + b, c * P:(c + 1) * P], xs[:, b, c * P:(c + 1) * P], ident[:])
                last.then_inc(xs_ps, 1)

            def expert_of(j):
                return pe.value_load(chunk_e[0:1, bass.ds(j, 1)], min_val=0, max_val=NE - 1)

            def hidden(j, b, free):
                e = expert_of(j)
                pe.wait_ge(xs_T, j + 1)
                if free is not None:
                    pe.wait_ge(hid_sb, free)
                for k in range(DC):
                    last = mm(ps[:, b, 0:F], xsT[:, b, k, :], w1_sb[:, bass.ds(e * (DC * F) + k * F, F)],
                              start=(k == 0), stop=(k == DC - 1))
                last.then_inc(hid_ps, 1)

            def turn_hidden(j, b, free):
                pe.wait_ge(hid_sb, j + 1)
                if free is not None:
                    pe.wait_ge(hidT_sb, free)
                for c in range(FC):
                    last = nc.tensor.transpose(ps[:, 6 + b, c * P:(c + 1) * P], hb[:, b, c * P:(c + 1) * P], ident[:])
                last.then_inc(hidT_ps, 1)

            def expert_out(j, b, free):
                e = expert_of(j)
                pe.wait_ge(hidT_sb, j + 1)
                if free is not None:
                    pe.wait_ge(yt_ready, free)
                for k in range(FC):
                    last = mm(ps[:, 2 + b, :], hbT[:, b, k, :], w2_sb[:, bass.ds(e * (FC * D) + k * D, D)],
                              start=(k == 0), stop=(k == FC - 1))
                last.then_inc(y_ps, 1)

            def expert_step(n, u, half, more=True):
                hidden(n + u, u % 2, n + (u - 1))
                if more:
                    turn_tokens(n + (u + 1), 1 - u % 2, half, n + u)
                expert_out(n + (u - 1), 1 - u % 2, n + (u - 2) if u > 1 else None)
                turn_hidden(n + u, u % 2, n + (u - 1))

            turn_tokens(0, 0, 0, None)
            hidden(0, 0, None)
            turn_tokens(1, 1, 0, None)
            turn_hidden(0, 0, None)
            expert_step(0, 1, 1)
            expert_step(0, 2, 1)
            with pe.Fori(0, (NCH - 5) // 2) as i:
                expert_step(2 * i, 3, i + 2)
                expert_step(2 * i, 4, i + 2)
            expert_step(NCH - 5, 3, NCH // 2)
            expert_step(NCH - 5, 4, 0, more=False)
            expert_out(NCH - 1, 0, NCH - 2)

            turn_rows(TR_X3, xn, xn_ready, 2 * NB)
            pe.wait_ge(deg_zero, 1)
            aggregate(1, xn)
            pe.wait_ge(l1w_in, 80)
            for b in range(NB):
                pe.wait_ge(agg_sb, DC * NJ + DC * (NJ if b == 0 else b // JB + 1))
                if b >= 3:
                    pe.wait_ge(l1_read, b - 2)
                for k in range(DC):
                    mm(ps[:, 2 * (b % 3), :], xT[:, k, b * P:(b + 1) * P], ws_sb[:, k, :],
                       start=(k == 0), stop=(k == DC - 1))
                for k in range(DC):
                    last = mm(ps[:, 2 * (b % 3) + 1, :], hT[:, k, b * P:(b + 1) * P], wg_sb[:, k, :],
                              start=(k == 0), stop=(k == DC - 1))
                last.then_inc(l1_ps, 1)

        @block.scalar
        def _(act):
            def evac(to, fr):
                return nc.scalar.activation(to, fr, ACT.Copy)

            def evac_turned(t0, to, rows=P):
                for b in range(NB):
                    act.wait_ge(tr_ps, t0 + b + 1)
                    evac(to(b), ps[:, 6 + (t0 + b) % 2, :].rearrange("p (c n) -> p c n", c=DC)).then_inc(tr_sb, 1)

            act.wait_ge(img_ps, 2)
            evac(img_ctx[0:R, :], ps[0:R, 1, :]).then_inc(img_ctx_ready, 1)
            evac_turned(TR_X, lambda b: xT[:, :, b * P:(b + 1) * P])
            for t in range(PC * NJ):
                m, j = t // NJ, t % NJ
                act.wait_ge(proj_ps, t + 1)
                evac(node_proj[:, m, j * 512:(j + 1) * 512], ps[:, 2 + t % 4, :]).then_inc(proj_sb, 1)

            act.wait_ge(img_bias_ready, 1)
            act.wait_ge(proj_sb, PC * NJ)

            def tanh_tile(r, m):
                nc.scalar.activation(tanh_t[:, m, :], node_proj[:, m, :], ACT.Tanh,
                                     bias=img_bias[:, m, bass.ds(r, 1)]).then_inc(tanh_sb, 1)

            for m in range(PC):
                tanh_tile(0, m)
            with act.Fori(0, R - 1) as r:
                for m in range(PC):
                    act.wait_ge(att_ps, PC * r + (m + 1))
                    tanh_tile(r + 1, m)

            def h1_tile(t):
                j, m = t // DC, t % DC
                act.wait_ge(h1_ps, t + 1)
                nc.scalar.activation(hT[:, m, j * 512:(j + 1) * 512], ps[:, 2 + t % 4, :], ACT.Identity,
                                     bias=bn_sb[:, m:m + 1]).then_inc(h1_sb, 1)

            act.wait_ge(gnnw_in, 112)
            for t in range(DC):
                h1_tile(t)
            act.wait_ge(att_shift, 1)
            nc.scalar.activation(att, att, ACT.Exp).then_inc(att_exp, 1)
            for t in range(DC, DC * NJ):
                h1_tile(t)
            evac_turned(TR_H1, lambda b: xn[:, b, :].rearrange("p (c n) -> p c n", c=DC))
            for j in range(NJ):
                t = TR_ATT + j
                act.wait_ge(tr_ps, t + 1)
                evac(attT[0:R, j * 512:(j + 1) * 512], ps[0:R, 6 + t % 2, :]).then_inc(tr_sb, 1)
            for t in range(DC * NJ):
                j, m = t // DC, t % DC
                act.wait_ge(agg_ps, t + 1)
                nc.scalar.activation(xT[:, m, j * 512:(j + 1) * 512], ps[:, (j * DC + m) % 6, :], ACT.Identity,
                                     bias=bim_sb[:, m:m + 1]).then_inc(agg_sb, 1)
            evac_turned(TR_XF, lambda b: xT[:, :, b * P:(b + 1) * P])
            act.wait_ge(gate_diff, 1)
            nc.scalar.activation(gate_e[:], gate_d[:], ACT.Exp).then_inc(gate_exp, 1)
            for j in range(NJ):
                t = TR_GATE + j
                act.wait_ge(tr_ps, t + 1)
                evac(gate_T[0:NE, j * 512:(j + 1) * 512], ps[0:NE, 6 + t % 2, :]).then_inc(tr_sb, 1)

            def tokens_out(j, b, free):
                act.wait_ge(xs_ps, j + 1)
                if free is not None:
                    act.wait_ge(hid_ps, free)
                evac(xsT[:, b], ps[:, 4 + b, :].rearrange("p (c n) -> p c n", c=DC)).then_inc(xs_T, 1)

            def hidden_out(j, b, free):
                act.wait_ge(hidT_ps, j + 1)
                if free is not None:
                    act.wait_ge(y_ps, free)
                nc.scalar.activation(hbT[:, b], ps[:, 6 + b, 0:F].rearrange("p (c n) -> p c n", c=FC),
                                     ACT.Relu).then_inc(hidT_sb, 1)

            def root(j, b):
                act.wait_ge(yv_ready, j + 1)
                nc.scalar.activation(e_mv[:, b, 3:4], e_mv[:, b, 2:3], ACT.Sqrt).then_inc(sd_ready, 1)

            def step(n, u, more=True):
                if more:
                    tokens_out(n + (u + 1), 1 - u % 2, n + u)
                hidden_out(n + u, u % 2, n + (u - 1))
                root(n + (u - 1), 1 - u % 2)

            tokens_out(0, 0, None)
            tokens_out(1, 1, None)
            hidden_out(0, 0, None)
            step(0, 1)
            step(0, 2)
            with act.Fori(0, (NCH - 5) // 2) as i:
                step(2 * i, 3)
                step(2 * i, 4)
            step(NCH - 5, 3)
            step(NCH - 5, 4, more=False)
            root(NCH - 1, 0)

            evac_turned(TR_X3, lambda b: xT[:, :, b * P:(b + 1) * P])
            for t in range(DC * NJ):
                j, m = t // DC, t % DC
                act.wait_ge(agg_ps, DC * NJ + t + 1)
                evac(hT[:, m, j * 512:(j + 1) * 512], ps[:, (j * DC + m) % 6, :]).then_inc(agg_sb, 1)

        @block.vector
        def _(dve):
            order = [0]
            v = nc.vector

            def link(ins):
                order[0] += 1
                ins.then_inc(dve_order, 1)
                dve.wait_ge(dve_order, order[0])

            def rsqrt(to, var, tmp):
                link(v.tensor_scalar(tmp.bitcast(I32), var.bitcast(I32), 1, None, ALU.logical_shift_right))
                link(v.tensor_scalar(to.bitcast(I32), tmp.bitcast(I32), -1.0, RSQRT_MAGIC, ALU.mult, ALU.add))
                for _ in range(4):
                    link(v.tensor_tensor(tmp, to, to, ALU.mult))
                    link(v.tensor_tensor(tmp, tmp, var, ALU.mult))
                    link(v.tensor_scalar(tmp, tmp, -0.5, 1.5, ALU.mult, ALU.add))
                    link(v.tensor_tensor(to, to, tmp, ALU.mult))

            def row_scales(g0, g1):
                for b in range(g0, g1):
                    last = v.bn_aggr(mv[:, b, :], stats[:, b, :])
                link(last)
                link(v.tensor_scalar(var_e[:, g0:g1], mv[:, g0:g1, 1], GNN_EPS, None, ALU.add))
                rsqrt(rstd[:, g0:g1], var_e[:, g0:g1], nt_a[:, g0:g1])

            def normalise(g0, g1):
                for b in range(g0, g1):
                    last = v.bn_stats(stats[:, b, :], x_sb[:, b, :])
                link(last)
                row_scales(g0, g1)
                for b in range(g0, g1):
                    v.tensor_scalar(xn[:, b, :], x_sb[:, b, :], mv[:, b, 0:1], rstd[:, b:b + 1],
                                    ALU.subtract, ALU.mult).then_inc(xn_ready, 1)

            dve.wait_ge(consts_ready, 9)
            v.tensor_copy(iota_f[:], iota_i[:])
            v.tensor_copy(first_key[:], key_i[:])
            v.memset(one_f[:], 1.0)
            v.memset(sel_bf[:], 0.0)
            for b in range(NB):
                v.memset(block_col[:, b:b + 1], float(b))
            link(v.tensor_copy(iota_p[:], iota_pi[:]))

            for g in range(XG):
                dve.wait_ge(x_in[g], 16)
                normalise(g * GB, (g + 1) * GB)

            dve.wait_ge(img_in, 80)
            link(v.tensor_tensor(bfi_sum[:], bfi[:, 0, :], bfi[:, 1, :], ALU.add))
            dve.wait_ge(img_ps, 2)
            for m in range(PC):
                last = v.tensor_scalar(img_bias[:, m, :], ps[:, 0, m * R:(m + 1) * R], bfi_sum[:, m:m + 1], None,
                                       ALU.add)
            last.then_inc(img_bias_ready, 1)

            dve.wait_ge(edges_in, 32)
            v.tensor_copy(src_f, src_i)
            v.tensor_copy(dst_f, dst_i).then_inc(edges_f, 1)
            v.tensor_scalar(edge_t.bitcast(I32), src_i, 7, None, ALU.logical_shift_right)
            link(v.tensor_scalar(edge_u.bitcast(I32), src_i, P - 1, None, ALU.bitwise_and))
            link(v.tensor_copy(lo_f, edge_u.bitcast(I32)))
            dve.wait_ge(base_ps, 1)
            link(v.tensor_scalar(base_f[:], ps[:, 0, 0:EG], float(N - WIN), None, ALU.min))
            v.tensor_copy(base_i[:], base_f[:])
            dve.wait_ge(edges_f, 1)
            link(v.tensor_tensor(edge_u.rearrange("p (g c) -> p g c", c=GC), dst_f.rearrange("p (g c) -> p g c", c=GC),
                                 base_f[:].unsqueeze(2).to_broadcast([P, EG, GC]), ALU.subtract))
            v.tensor_reduce(outside[:, 0:1], edge_u, AX_X, ALU.max)
            v.tensor_reduce(outside[:, 1:2], edge_u, AX_X, ALU.min)
            link(v.scalar_tensor_tensor(out=win_f, in0=edge_t.bitcast(I32), scalar=float(WIN), in1=edge_u,
                                        op0=ALU.mult, op1=ALU.add))
            link(v.tensor_scalar(outside[:, 0:1], outside[:, 0:1], WIN - 0.5, None, ALU.is_gt))
            link(v.tensor_scalar(outside[:, 1:2], outside[:, 1:2], 0.0, None, ALU.is_lt))
            v.tensor_tensor(outside_bf[:], outside[:, 0:1], outside[:, 1:2], ALU.max).then_inc(outside_ready, 1)
            dve.wait_ge(outside_ps, 1)
            v.tensor_copy(loose[:], ps[:, 1, 0:1]).then_inc(loose_ready, 1)

            def window_rows(c, b):
                v.tensor_scalar(oh_lo[:, b, :], iota_n[:, 0:P], lo_f[:, bass.ds(c, 1)], None, ALU.is_equal)
                v.tensor_scalar(oh_win[:, b, :], iota_n[:, 0:NB * WIN], win_f[:, bass.ds(c, 1)], None,
                                ALU.is_equal).then_inc(win_oh, 1)

            def window_add(g, b):
                base = dve.value_load(base_i[0:1, bass.ds(g, 1)], min_val=0, max_val=N - WIN)
                dve.wait_ge(win_oh_used, GC * (g + 1))
                dve.wait_ge(win_bank_free, g + 2)
                at_base = counts[:, :, bass.ds(base, WIN)]
                v.tensor_tensor(at_base, at_base, ps[:, 4 + b, 0:NB * WIN].rearrange("p (b w) -> p b w", w=WIN),
                                ALU.add).then_inc(win_bank_free, 1)

            dve.wait_ge(counts_zero, 1)
            dve.wait_ge(loose_ready, 1)
            link(v.memset(nt_b[:], 0.0))
            v.memset(nt_b[:, 0:1], 0.0).then_inc(win_bank_free, 2)
            for c in range(GC):
                window_rows(c, c)
            with dve.Fori(0, EG // 2 - 1) as i:
                for u in range(2):
                    for c in range(GC):
                        dve.wait_ge(win_oh_used, 2 * GC * i + (GC * u + c + 1))
                        window_rows(2 * GC * i + (GC * (u + 1) + c), c)
                    window_add(2 * i + u, u)
            for c in range(GC):
                dve.wait_ge(win_oh_used, EC - 2 * GC + c + 1)
                window_rows(EC - GC + c, c)
            window_add(EG - 2, 0)
            window_add(EG - 1, 1)
            dve.wait_ge(win_bank_free, EG + 2)

            def edge_rows(k, c, b):
                v.tensor_scalar(oh_src[:, b, :], iota_n[:, 0:2 * P], src_k[:, bass.ds(c, 1)], None, ALU.is_equal)
                v.tensor_scalar(oh_dst[:, b, :], iota_n, dst_f[:, bass.ds(c, 1)], None,
                                ALU.is_equal).then_inc(edge_oh, 1)

            n_loose = dve.value_load(loose[0:1, 0:1], min_val=0, max_val=P)
            with dve.If(n_loose > 0):
                for k in range(NB // 2):
                    v.tensor_scalar(src_k, src_f, float(-2 * P * k), None, ALU.add).then_inc(src_k_ready, 1)
                    dve.wait_ge(src_k_ready, k + 1)
                    for c in range(2):
                        if k >= 1:
                            dve.wait_ge(edge_oh_used, k * EC + c - 1)
                        edge_rows(k, c, c)
                    with dve.Fori(0, EC // 2 - 1) as c:
                        for i in range(2):
                            dve.wait_ge(edge_oh_used, 2 * c + (k * EC + i + 1))
                            edge_rows(k, 2 * c + (i + 2), i)
                    dve.wait_ge(edge_oh_used, (k + 1) * EC)
                    for s in range(2):
                        last = v.tensor_copy(counts[:, 2 * k + s, :],
                                             ps[:, 2 + s * NJ:2 + (s + 1) * NJ, :].rearrange("p a b -> p (a b)"))
                    last.then_inc(pass_out, 1)
                dve.wait_ge(pass_out, NB // 2)
            v.memset(nt_b[:, 0:1], 0.0).then_inc(counts_ready, 1)

            dve.wait_ge(att_ps, PC * R)
            dve.wait_ge(attw_in, 48)
            halves = [ps[:, m, 0:R * NB].rearrange("p (r b) -> p b r", b=NB) for m in range(PC)]
            link(v.tensor_scalar(att, halves[0], ba_sb[:, 0:1], None, ALU.add))
            link(v.tensor_tensor(att, att, halves[1], ALU.add))
            link(v.tensor_reduce(att_red, att, AX_X, ALU.max))
            v.tensor_tensor(att, att, att_red.unsqueeze(2).to_broadcast([P, NB, R]),
                            ALU.subtract).then_inc(att_shift, 1)
            dve.wait_ge(att_exp, 1)
            link(v.tensor_reduce(att_red, att, AX_X, ALU.add))
            link(v.reciprocal(att_inv, att_red))
            v.tensor_tensor(att, att, att_inv.unsqueeze(2).to_broadcast([P, NB, R]),
                            ALU.mult).then_inc(att_ready, 1)

            dve.wait_ge(x_again, 16)
            dve.wait_ge(gnnw_in, 112)
            for b in range(NB):
                dve.wait_ge(out_ps, b + 1)
                v.tensor_tensor(out_t[:, b % 2, :], ps[:, b % 4, :], row_bias[:], ALU.add).then_inc(out_read, 1)
                dve.wait_ge(out_read, b + 1)
                last = v.scalar_tensor_tensor(out=x_sb[:, b, :], in0=out_t[:, b % 2, :], scalar=0.0,
                                              in1=x_sb[:, b, :], op0=ALU.max, op1=ALU.add)
            link(last)
            for g in range(XG):
                normalise(g * GB, (g + 1) * GB)

            dve.wait_ge(router_ps, 1)
            link(v.tensor_copy(logits[:].rearrange("p b e -> p (b e)"), ps[:, 0, 0:NB * NE]))
            for b in range(NB):
                last = v.max(top_v[:, b, :], logits[:, b, :])
            link(last)
            for b in range(NB):
                last = v.max_index(top_i[:, b, :], top_v[:, b, :], logits[:, b, :])
            v.tensor_tensor(gate_d[:], top_v[:, :, 1], top_v[:, :, 0], ALU.subtract).then_inc(gate_diff, 1)
            link(last)
            for k in range(TOPK):
                last = v.tensor_copy(top_f[:, k, :], top_i[:, :, k])
            link(last)
            for k in range(TOPK):
                last = v.tensor_tensor(sel[:, k], iota_f[:, 0:NE].unsqueeze(1).to_broadcast([P, NB, NE]),
                                       top_f[:, k, :].unsqueeze(2).to_broadcast([P, NB, NE]), ALU.is_equal)
            link(last)
            v.tensor_tensor(sel_bf[:, (NB - 1) * NE:].rearrange("p (b e) -> p b e", e=NE), sel[:, 0], sel[:, 1],
                            ALU.add).then_inc(sel_ready, 1)
            dve.wait_ge(gate_exp, 1)
            link(v.tensor_scalar(gate_d[:], gate_e[:], 1.0, None, ALU.add))
            link(v.reciprocal(gates[:, 0, :], gate_d[:]))
            link(v.tensor_tensor(gates[:, 1, :], gates[:, 0, :], gate_e[:], ALU.mult))
            for k in range(TOPK):
                last = v.tensor_tensor(gate_w[:, k], sel[:, k], gates[:, k, :].unsqueeze(2).to_broadcast([P, NB, NE]),
                                       ALU.mult)
            link(last)
            v.tensor_tensor(gate_w[:, 0], gate_w[:, 0], gate_w[:, 1], ALU.add).then_inc(gatew_ready, 1)

            dve.wait_ge(pos_ps, 1)
            link(v.tensor_scalar(cnt_i[:], ps[:, 2, 0:NE], float(P - 1), None, ALU.add))
            link(v.tensor_scalar(cnt_i[:], cnt_i[:], 7, 7, ALU.logical_shift_right, ALU.logical_shift_left))
            link(v.tensor_copy(cnt_f[:], cnt_i[:]))
            link(v.tensor_tensor_scan(end_f[:], one_f[:], cnt_f[:], 0.0, ALU.mult, ALU.add))
            link(v.tensor_tensor(off_f[:], end_f[:], cnt_f[:], ALU.subtract))
            link(v.tensor_tensor(pos[:], ps[:, 1, 0:NB * NE].rearrange("p (b e) -> p b e", e=NE),
                                 off_f[:].unsqueeze(1).to_broadcast([P, NB, NE]), ALU.add))
            for k in range(TOPK):
                link(v.tensor_tensor(pos_t[:], sel[:, k], pos[:], ALU.mult))
                link(v.tensor_reduce(slot_f[:, k, :], pos_t[:], AX_X, ALU.add))
            link(v.tensor_copy(slot_i[:], slot_f[:]))
            v.tensor_scalar(slot_hi[:], slot_i[:], 7, None, ALU.logical_shift_right)
            link(v.tensor_scalar(slot_lo[:], slot_i[:], P - 1, None, ALU.bitwise_and))
            v.tensor_copy(slot_hf[:], slot_hi[:])
            link(v.tensor_copy(slot_lf[:], slot_lo[:]))
            link(v.tensor_scalar(chunk_ef[:], iota_f[:, 0:SW], float(P), None, ALU.mult))
            link(v.tensor_tensor(chunk_ge, chunk_ef[:].unsqueeze(2).to_broadcast([P, SW, NE]),
                                 end_f[:].unsqueeze(1).to_broadcast([P, SW, NE]), ALU.is_ge))
            link(v.tensor_reduce(chunk_ef[:], chunk_ge, AX_X, ALU.add))
            v.tensor_scalar(chunk_e[:], chunk_ef[:], float(NE - 1), None, ALU.min).then_inc(tok_ready, 1)
            for b in range(NB):
                for k in range(TOPK):
                    n = b * TOPK + k
                    if n >= 2:
                        dve.wait_ge(slot_ps, n - 1)
                    v.tensor_scalar(lo_oh[:, n % 2, :], iota_f[:], slot_lf[:, k, b:b + 1], None, ALU.is_equal)
                    v.tensor_scalar(hi_oh[:, n % 2, 0:SW], iota_f[:, 0:SW], slot_hf[:, k, b:b + 1], iota_p[:, 0:1],
                                    ALU.is_equal, ALU.mult)
                    v.tensor_scalar(hi_oh[:, n % 2, SW:2 * SW], iota_f[:, 0:SW], slot_hf[:, k, b:b + 1],
                                    block_col[:, b:b + 1], ALU.is_equal, ALU.mult).then_inc(slot_oh, 1)
            dve.wait_ge(slot_ps, TOPK * NB)
            link(v.tensor_scalar(tok_f[:], ps[:, 3, SW:2 * SW], float(P), None, ALU.mult))
            link(v.tensor_tensor(tok_f[:], tok_f[:], ps[:, 3, 0:SW], ALU.add))
            v.tensor_copy(tok[:], tok_f[:]).then_inc(tok_ready, 1)
            for b in range(NB):
                dve.wait_ge(beta_ps, b + 1)
                v.tensor_tensor(x_sb[:, b, :], x_sb[:, b, :], ps[:, 4 + b % 2, :], ALU.add).then_inc(beta_read, 1)

            def hidden_bias(j, b, free):
                e = dve.value_load(chunk_e[0:1, bass.ds(j, 1)], min_val=0, max_val=NE - 1)
                dve.wait_ge(hid_ps, j + 1)
                if free is not None:
                    dve.wait_ge(hidT_ps, free)
                v.tensor_tensor(hb[:, b, :], ps[:, b, 0:F], b1_row[:, bass.ds(e * F, F)], ALU.add).then_inc(hid_sb, 1)

            def residual(j, b):
                dve.wait_ge(y_ps, j + 1)
                dve.wait_ge(xb_ready, j + 1)
                v.tensor_tensor(yt[:, b, :], ps[:, 2 + b, :], xb[:, b, :], ALU.add).then_inc(yt_ready, 1)
                dve.wait_ge(yt_ready, j + 1)
                v.bn_stats(e_stats[:, b, :], yt[:, b, :]).then_inc(es_ready, 1)
                dve.wait_ge(es_ready, j + 1)
                v.memset(nt_b[:, 0:1], 0.0)
                v.bn_aggr(e_mv[:, b, 0:2], e_stats[:, b, :]).then_inc(em_ready, 1)
                dve.wait_ge(em_ready, j + 1)
                v.tensor_scalar(e_mv[:, b, 2:3], e_mv[:, b, 1:2], EXPERT_EPS, None, ALU.add).then_inc(yv_ready, 1)

            def scaled(j, b, half):
                dve.wait_ge(sd_ready, j + 1)
                v.reciprocal(e_mv[:, b, 4:5], e_mv[:, b, 3:4]).then_inc(er_ready, 1)
                dve.wait_ge(er_ready, 4 * j + 1)
                v.scalar_tensor_tensor(out=e_mv[:, b, 5:6], in0=e_mv[:, b, 4:5], scalar=e_mv[:, b, 4:5],
                                       in1=e_mv[:, b, 2:3], op0=ALU.mult, op1=ALU.mult).then_inc(er_ready, 1)
                dve.wait_ge(er_ready, 4 * j + 2)
                v.tensor_scalar(e_mv[:, b, 6:7], e_mv[:, b, 5:6], -0.5, 1.5, ALU.mult, ALU.add).then_inc(er_ready, 1)
                dve.wait_ge(er_ready, 4 * j + 3)
                v.tensor_tensor(e_mv[:, b, 7:8], e_mv[:, b, 6:7], e_mv[:, b, 4:5], ALU.mult).then_inc(er_ready, 1)
                dve.wait_ge(er_ready, 4 * j + 4)
                if half is not None:
                    dve.wait_ge(y_out[b], 16 * half)
                v.tensor_scalar(yu[:, b, :], yt[:, b, :], e_mv[:, b, 0:1], e_mv[:, b, 7:8],
                                ALU.subtract, ALU.mult).then_inc(yu_ready, 1)

            dve.wait_ge(ffn_rows_in, 48)
            hidden_bias(0, 0, None)
            hidden_bias(1, 1, None)
            residual(0, 0)
            hidden_bias(2, 0, 1)
            scaled(0, 0, None)
            residual(1, 1)
            hidden_bias(3, 1, 2)
            scaled(1, 1, None)
            residual(2, 0)
            with dve.Fori(0, (NCH - 5) // 2) as i:
                for u in range(2):
                    hidden_bias(2 * i + (4 + u), u, 2 * i + (3 + u))
                    scaled(2 * i + (2 + u), u, i + 1)
                    residual(2 * i + (3 + u), 1 - u)
            hidden_bias(NCH - 1, 0, NCH - 2)
            scaled(NCH - 3, 0, (NCH - 3) // 2)
            residual(NCH - 2, 1)
            scaled(NCH - 2, 1, (NCH - 2) // 2)
            residual(NCH - 1, 0)
            scaled(NCH - 1, 0, (NCH - 1) // 2)

            for b in range(NB):
                dve.wait_ge(y_top_in[b], 16 * TOPK)
                for k in range(TOPK):
                    link(v.scalar_tensor_tensor(out=x_sb[:, b, :], in0=y_top[:, k, b, :], scalar=gates[:, k, b:b + 1],
                                                in1=x_sb[:, b, :], op0=ALU.mult, op1=ALU.add))

            for g in range(XG):
                normalise(g * GB, (g + 1) * GB)
            dve.wait_ge(tr_sb, TR_X3 + NB)
            v.memset(ps[:, 7, 0:NB], 0.0).then_inc(deg_zero, 1)
            dve.wait_ge(agg_ps, 2 * DC * NJ)
            dve.wait_ge(cf_used, 2 * NJ * NB)
            link(v.tensor_scalar(deg[:], ps[:, 7, 0:NB], 1.0, None, ALU.max))
            link(v.reciprocal(deg_inv[:], deg[:]))
            dve.wait_ge(l1w_in, 80)
            for b in range(NB):
                dve.wait_ge(l1_ps, b + 1)
                link(v.scalar_tensor_tensor(out=h_t, in0=ps[:, 2 * (b % 3) + 1, :], scalar=deg_inv[:, b:b + 1],
                                            in1=row_bias[:], op0=ALU.mult, op1=ALU.add))
                v.tensor_tensor(xn[:, b, :], h_t, ps[:, 2 * (b % 3), :], ALU.add).then_inc(l1_read, 1)
                dve.wait_ge(l1_read, b + 1)
                v.bn_stats(stats[:, b, :], xn[:, b, :])
            link(v.memset(nt_b[:], 0.0))
            row_scales(0, NB)
            for b in range(NB):
                link(v.tensor_scalar(h_t, xn[:, b, :], mv[:, b, 0:1], rstd[:, b:b + 1], ALU.subtract, ALU.mult))
                link(v.tensor_tensor(h_t, h_t, l1g_row, ALU.mult))
                link(v.tensor_tensor(h_t, h_t, l1b_row, ALU.add))
                link(v.scalar_tensor_tensor(out=x_sb[:, b, :], in0=h_t, scalar=0.0, in1=x_sb[:, b, :],
                                            op0=ALU.max, op1=ALU.add))
            for g in range(XG):
                normalise(g * GB, (g + 1) * GB)
            dve.wait_ge(xn_ready, 4 * NB)

            link(v.tensor_scalar(hot, xn[:, :, 64:112], 0.5, None, ALU.is_gt))
            link(v.tensor_tensor(hot.rearrange("p b (g i) -> p (b g) i", i=16),
                                 hot.rearrange("p b (g i) -> p (b g) i", i=16),
                                 first_key[:].unsqueeze(1).to_broadcast([P, NB * 3, 16]), ALU.mult))
            nib_f = nib.rearrange("p b c -> p (b c)")
            nib_pf = nib_pos.rearrange("p b c -> p (b c)")
            link(v.tensor_reduce(nib_f, hot.rearrange("p b (g i) -> p (b g) i", i=16), AX_X, ALU.max))
            link(v.tensor_scalar(nib_pf, nib_f, 0.0, None, ALU.is_gt))
            link(v.tensor_scalar(nib_f, nib_f, -1.0, 16.0, ALU.mult, ALU.add))
            link(v.tensor_tensor(nib_f, nib_f, nib_pf, ALU.mult))
            v.tensor_scalar(mark, xn[:, :, 0], 0.5, None, ALU.is_gt)
            v.tensor_scalar(is_shl, xn[:, :, 39], 0.5, None, ALU.is_gt)
            link(v.tensor_scalar(is_shr, xn[:, :, 40], 0.5, None, ALU.is_gt))
            link(v.scalar_tensor_tensor(out=val_f, in0=nib[:, :, 1], scalar=16.0, in1=nib[:, :, 0],
                                        op0=ALU.mult, op1=ALU.add))
            v.tensor_copy(val_i, val_f)
            link(v.tensor_copy(sa_i, nib[:, :, 2]))
            v.tensor_tensor(shl_i, val_i, sa_i, ALU.logical_shift_left)
            link(v.tensor_tensor(shr_i, val_i, sa_i, ALU.logical_shift_right))
            link(v.tensor_scalar(shl_i, shl_i, 255, None, ALU.bitwise_and))
            v.tensor_copy(shl_f, shl_i)
            v.tensor_copy(shr_f, shr_i)
            link(v.tensor_scalar(not_shl, is_shl, -1.0, 1.0, ALU.mult, ALU.add))
            link(v.tensor_tensor(is_shr, is_shr, not_shl, ALU.mult))
            v.tensor_tensor(is_shl, is_shl, mark, ALU.mult)
            link(v.tensor_tensor(is_shr, is_shr, mark, ALU.mult))
            v.tensor_tensor(shl_f, shl_f, is_shl, ALU.mult)
            v.tensor_tensor(shr_f, shr_f, is_shr, ALU.mult)
            link(v.tensor_tensor(amp, is_shl, is_shr, ALU.add))
            v.tensor_scalar(amp, amp, 2.0, None, ALU.mult)
            link(v.tensor_tensor(val_f, shl_f, shr_f, ALU.add))
            link(v.tensor_scalar(val_f, val_f, 0.0, 255.0, ALU.max, ALU.min))
            link(v.tensor_copy(res_i, val_f))
            v.tensor_scalar(out_ni[:, :, 0], res_i, 15, None, ALU.bitwise_and)
            link(v.tensor_scalar(out_ni[:, :, 1], res_i, 4, None, ALU.logical_shift_right))
            link(v.tensor_copy(out_nf, out_ni))
            for k in range(2):
                last = v.tensor_tensor(out_oh[:, :, k, :], iota_f[:, 0:16].unsqueeze(1).to_broadcast([P, NB, 16]),
                                       out_nf[:, :, k].unsqueeze(2).to_broadcast([P, NB, 16]), ALU.is_equal)
            link(last)
            oh = out_oh.rearrange("p b k i -> p b (k i)")
            link(v.tensor_tensor(oh, oh, amp.unsqueeze(2).to_broadcast([P, NB, 32]), ALU.mult))
            link(v.tensor_tensor(xn[:, :, 128:160], xn[:, :, 128:160], oh, ALU.add))
            for b in range(NB):
                v.tensor_tensor(x_sb[:, b, :], x_sb[:, b, :], xn[:, b, :], ALU.add).then_inc(fin_ready, 1)


_OUTS = [((1536, 512), 'float32')]


def kernel(**inputs):
    import numpy as np
    import concourse.bacc as bacc
    from concourse import mybir as mb
    from concourse.bass_utils import run_bass_kernel_spmd as run

    def cols(a):
        return np.asarray(a).reshape(-1, 128).T

    g = {k: np.asarray(v) for k, v in inputs.items()}
    img0 = g['L0_gnn_img_feats'][0]
    laid = {
        'x': g['x'],
        'src': g['src'].reshape(-1, 128).T, 'dst': g['dst'].reshape(-1, 128).T,
        'img': img0.T.reshape(-1, 128, img0.shape[0]).transpose(1, 0, 2),
        'wf': g['L0_gnn_Wf'], 'bf': cols(g['L0_gnn_bf']), 'wi': g['L0_gnn_Wi'], 'bi': cols(g['L0_gnn_bi']),
        'wa': cols(g['L0_gnn_Wa']), 'ba': g['L0_gnn_ba'],
        'wn': g['L0_gnn_Wn'], 'bn': cols(g['L0_gnn_bn']),
        'wim': g['L0_gnn_Wim'], 'bim': cols(g['L0_gnn_bim']),
        'wap': g['L0_gnn_Wap'], 'bap': g['L0_gnn_bap'],
        'router': g['L0_ffn_router_w'], 'w1': g['L0_ffn_w1'], 'b1': g['L0_ffn_b1'].reshape(-1),
        'w2': g['L0_ffn_w2'], 'b2': g['L0_ffn_b2'].reshape(-1),
        'ffn_gamma': g['L0_ffn_gamma'].reshape(-1), 'ffn_beta': g['L0_ffn_beta'],
        'w_self': g['L1_gnn_w_self'].T, 'w_neigh': g['L1_gnn_w_neigh'].T,
        'l1_bias': g['L1_gnn_bias'], 'l1_gamma': g['L1_gnn_gamma'], 'l1_beta': g['L1_gnn_beta'],
    }
    nc = bacc.Bacc("TRN2", target_bir_lowering=False, num_devices=1)
    arrays, args = {}, []
    for name, a in laid.items():
        a = np.ascontiguousarray(a)
        arrays[f"in_{name}_dram"] = a
        args.append(nc.dram_tensor(f"in_{name}_dram", a.shape, mb.dt.from_np(a.dtype), kind="ExternalInput").ap())
    for i, (shape, dtype) in enumerate(_OUTS):
        dt = mb.dt.from_np(np.dtype(dtype))
        args.append(nc.dram_tensor(f"out_{i}_dram", shape, dt, kind="ExternalOutput").ap())
    args.append(nc.dram_tensor("tokens_dram", (1536, 512), mb.dt.float32, kind="Internal").ap())
    args.append(nc.dram_tensor("expert_rows_dram", (31 * 128, 512), mb.dt.float32, kind="Internal").ap())
    gnn_moe_kernel(nc, *args)
    r = run(nc, [arrays], core_ids=[0])
    return r.results[0]["out_0_dram"]
```

```python
from contextlib import ExitStack

import concourse.bass as bass
from concourse import mybir

ALU = mybir.AluOpType
ACT = mybir.ActivationFunctionType
F32 = mybir.dt.float32
F32R = mybir.dt.float32r
BF16 = mybir.dt.bfloat16
I32 = mybir.dt.int32
U32 = mybir.dt.uint32
U16 = mybir.dt.uint16
I16 = mybir.dt.int16
AX_X = mybir.AxisListType.X

P = 128
RSQRT_MAGIC = 1597463007.0
TOPK = 2
EXACT = 4096
GNN_EPS = 1e-5
EXPERT_EPS = 1e-6


def gnn_moe_kernel(nc, x, src, dst, img, wf, bf, wi, bi, wa, ba, wn, bn, wim, bim, wap, bap,
                   router, w1, b1, w2, b2, ffn_gamma, ffn_beta,
                   w_self, w_neigh, l1_bias, l1_gamma, l1_beta, out, xf_dram, y_dram):
    N, D = x.shape
    NB = N // P
    DC = D // P
    NJ = N // 512
    JB = 512 // P
    EC = src.shape[1]
    KI, R = img.shape[1], img.shape[2]
    PJ = wf.shape[1]
    PC = PJ // P
    NE, F = w1.shape[0], w1.shape[2]
    FC = F // P
    NCH = (N * TOPK + NE * (P - 1)) // P
    SW = 32
    LOGIT_BANKS = (0, 1, 6)
    GC = 4
    EG = EC // GC
    WIN = 24
    XG = 3
    GB = NB // XG
    assert 3 * EG == 8 * R and R % 3 == 0 and PC == 2 and NCH <= SW and D == 512 and N % 512 == 0 and NCH == 31

    with ExitStack() as ctx:
        def sb(name, shape, dt=F32):
            return ctx.enter_context(nc.sbuf_tensor(name, shape, dt))

        def sem(name):
            return ctx.enter_context(nc.semaphore(name))

        ps = ctx.enter_context(nc.psum_tensor("ps", [P, 8, 512], F32))

        AX = 0
        AW = AX + NB * D
        AH = AW + NE * DC * F
        AT = AH + NB * D
        AN = AT + NB * D

        def beneath(name, start, size):
            with ExitStack() as place:
                if start:
                    place.enter_context(nc.sbuf_tensor(name + "_before", [P, start], F32))
                return place.enter_context(nc.sbuf_tensor(name, [P, size], F32R))

        rows_hi = beneath("rows_hi", AN, NB * D)[:].rearrange("p (b d) -> p b d", b=NB)
        rows_lo = [beneath(f"rows_lo{k}", a, NB * D)[:].rearrange("p (b d) -> p b d", b=NB)
                   for k, a in enumerate((AX, AW))]
        arena = sb("arena", [P, 4 * NB * D + NE * DC * F])

        def at(start, size):
            return arena[:, start:start + size]

        x_sb = at(AX, NB * D).rearrange("p (b d) -> p b d", b=NB)
        xn = at(AN, NB * D).rearrange("p (b d) -> p b d", b=NB)
        xT = at(AT, NB * D).rearrange("p (c n) -> p c n", c=DC)
        hT = at(AH, NB * D).rearrange("p (c n) -> p c n", c=DC)
        node_proj = at(AX, PC * N).rearrange("p (m n) -> p m n", m=PC)
        tanh_t = [at(AX + PC * N, PC * N).rearrange("p (m n) -> p m n", m=PC)] + [
            at(AN + k * PC * N, PC * N).rearrange("p (m n) -> p m n", m=PC) for k in range(2)]
        wi_sb = at(AH, KI * PJ).rearrange("p (k n) -> p k n", k=KI)
        wim_sb = at(AH + KI * PJ, KI * D).rearrange("p (k n) -> p k n", k=KI)
        wf_sb = at(AW, DC * PJ).rearrange("p (k n) -> p k n", k=DC)
        wn_sb = at(AW + DC * PJ, DC * D).rearrange("p (k n) -> p k n", k=DC)
        wap_sb = at(AW + DC * (PJ + D), 2 * DC * D).rearrange("p (k n) -> p k n", k=2 * DC)
        w1_sb = at(AW, NE * DC * F)
        w2_sb = at(AH, NE * FC * D)
        w2_cut = NB * D // (FC * D)
        b1_row = at(AH + NE * FC * D, NE * F)
        b2_row = at(AH + NE * FC * D + NE * F, NE * D)
        gamma_row = at(AH + NE * FC * D + NE * F + NE * D, NE * D)
        y_top = at(AT, TOPK * NB * D).rearrange("p (k b d) -> p k b d", k=TOPK, b=NB)
        ws_sb = at(AW + NB * D, DC * D).rearrange("p (k n) -> p k n", k=DC)
        wg_sb = at(AW, DC * D).rearrange("p (k n) -> p k n", k=DC)
        xn3 = at(AW, NB * D).rearrange("p (b d) -> p b d", b=NB)
        assert NB * D + DC * D <= NE * DC * F
        assert AH + NE * FC * D + NE * F + 2 * NE * D <= AN + NB * D

        counts = sb("counts", [P, NB, N], U16)

        work_r = beneath("work_r", 0, 6656)
        work = sb("work", [P, 6656])
        dst_f = work[:, 480:480 + EC]
        src_k = work[:, 864:864 + EC]
        src_i = work[:, 1248:1248 + EC].bitcast(I32)
        dst_i = work[:, 1632:1632 + EC].bitcast(I32)
        oh_dst = work[:, 2016:2016 + N].bitcast(BF16).rearrange("p (b n) -> p b n", b=2)
        oh_src = work[:, 3552:3552 + 2 * P].bitcast(BF16).rearrange("p (b n) -> p b n", b=2)
        iota_n = work[:, 3808:3808 + N // 2].bitcast(I16)
        edge_t = work[:, 2016:2016 + EC]
        edge_u = work[:, 2400:2400 + EC]
        OC = 2 * GC
        WW = NB * WIN

        def pair_rows(start, n):
            return at(start, n * OC // 2).bitcast(I16).rearrange("p (n c) -> p n c", c=OC)

        num_win = pair_rows(AH, WW)
        oh_win = [pair_rows(AH + (k + 1) * WW * OC // 2, WW).bitcast(BF16) for k in range(4)]
        oh_lo = [pair_rows((AW, AH - DC * PJ)[k // 2] + (k % 2) * P * OC // 2, P).bitcast(BF16) for k in range(4)]
        assert P * OC == DC * PJ and 5 * WW * OC // 2 <= NB * D and DC * (2 * PJ + 3 * D) <= NE * DC * F
        att = work[:, 0:NB * R].rearrange("p (b r) -> p b r", b=NB)
        region_col = work[:, 0:3 * R].rearrange("p (b r) -> p b r", b=3)
        logits_T = at(AN, N)
        att_red = work[:, 448:448 + NB]
        att_inv = work[:, 464:464 + NB]
        attT = work[:, 512:512 + N]
        out_t = work[:, 2048:2048 + 2 * D].rearrange("p (b d) -> p b d", b=2)
        gate_T = work[:, 0:N]
        xs = work[:, 0:1024].rearrange("p (b d) -> p b d", b=2)
        xb = work[:, 1024:2048].rearrange("p (b d) -> p b d", b=2)
        xsT = work[:, 2048:3072].rearrange("p (b c n) -> p b c n", b=2, c=DC)
        hb = work[:, 3072:3072 + 2 * F].rearrange("p (b f) -> p b f", b=2)
        hbT = work[:, 3584:3584 + 2 * F].rearrange("p (b c n) -> p b c n", b=2, c=FC)
        yt = work[:, 4096:5120].rearrange("p (b d) -> p b d", b=2)
        yu = work[:, 5120:6144].rearrange("p (b d) -> p b d", b=2)
        l1g_row = work[:, 0:D]
        l1b_row = work[:, D:2 * D]
        h_t = work[:, 2 * D:3 * D]
        deg_inv = work[:, 3 * D:4 * D]
        hot = work[:, 3072:3072 + NB * 48].rearrange("p (b c) -> p b c", b=NB)
        nib = work[:, 3712:3712 + NB * 3].rearrange("p (b c) -> p b c", b=NB)
        nib_pos = work[:, 3776:3776 + NB * 3].rearrange("p (b c) -> p b c", b=NB)
        mark = work[:, 3840:3840 + NB]
        is_shl = work[:, 3856:3856 + NB]
        is_shr = work[:, 3872:3872 + NB]
        not_shl = work[:, 3888:3888 + NB]
        val_f = work[:, 3904:3904 + NB]
        val_i = work[:, 3920:3920 + NB].bitcast(I32)
        sa_i = work[:, 3936:3936 + NB].bitcast(I32)
        shl_i = work[:, 3952:3952 + NB].bitcast(I32)
        shr_i = work[:, 3968:3968 + NB].bitcast(I32)
        shl_f = work[:, 3984:3984 + NB]
        shr_f = work[:, 4000:4000 + NB]
        res_i = work[:, 4016:4016 + NB].bitcast(I32)
        out_ni = work[:, 4032:4032 + 2 * NB].rearrange("p (b k) -> p b k", b=NB).bitcast(I32)
        out_nf = work[:, 4064:4064 + 2 * NB].rearrange("p (b k) -> p b k", b=NB)
        out_oh = work[:, 4096:4096 + NB * 32].rearrange("p (b k i) -> p b k i", b=NB, k=2)
        amp = work[:, 4480:4480 + NB]

        ident = sb("ident", [P, P])
        ones_bf = sb("ones_bf", [P, P], BF16)
        before_bf = sb("before_bf", [P, P], BF16)
        row0 = sb("row0", [P, P])
        lo_16 = sb("lo_16", [P, EC], I16)
        win_16 = sb("win_16", [P, EC], I16)
        base_f = sb("base_f", [P, EG])
        base_i = sb("base_i", [P, EG], I32)
        outside = sb("outside", [P, 2])
        outside_bf = sb("outside_bf", [P, 1], BF16)
        loose = sb("loose", [P, 1], I32)
        iota_i = sb("iota_i", [P, P], I32)
        iota_f = sb("iota_f", [P, P])
        iota_pi = sb("iota_pi", [P, 1], I32)
        iota_p = sb("iota_p", [P, 1])
        key_i = sb("key_i", [P, 16], I32)
        first_key = sb("first_key", [P, 16])
        block_col = sb("block_col", [P, NB])
        img_sb = sb("img_sb", [P, KI, R])
        bfi = sb("bfi", [P, 2, PC])
        bfi_sum = sb("bfi_sum", [P, PC])
        wa_sb = sb("wa_sb", [P, PC])
        ba_sb = sb("ba_sb", [P, 1])
        bn_sb = sb("bn_sb", [P, DC])
        bim_sb = sb("bim_sb", [P, DC])
        row_bias = sb("row_bias", [P, D])
        img_bias = sb("img_bias", [P, PC, R])
        img_ctx = work[:, 4608:4608 + D]
        stats = sb("stats", [P, NB, 6])
        mv = sb("mv", [P, NB, 2])
        var_e = sb("var_e", [P, NB])
        rstd = sb("rstd", [P, NB])
        nt_a = sb("nt_a", [P, NB])
        nt_b = sb("nt_b", [P, NB])
        cf = work_r[:, 5120:6656].rearrange("p (b n) -> p b n", b=3)
        cf_rest = work_r[:, 3072:4096].rearrange("p (b n) -> p b n", b=2)
        count_max = sb("count_max", [P, 1])
        over_bf = sb("over_bf", [P, 1], BF16)
        over = sb("over", [P, 1], I32)
        ones_r = work_r[:, 2 * D:2 * D + P]

        rw_sb = sb("rw_sb", [P, DC, NE])
        logits = sb("logits", [P, NB, NE])
        top_v = sb("top_v", [P, NB, 8])
        top_i = sb("top_i", [P, NB, 8], U32)
        top_f = sb("top_f", [P, TOPK, NB])
        gate_d = sb("gate_d", [P, NB])
        gate_e = sb("gate_e", [P, NB])
        gates = sb("gates", [P, TOPK, NB])
        sel = sb("sel", [P, TOPK, NB, NE])
        sel_bf = sb("sel_bf", [P, (2 * NB - 1) * NE], BF16)
        gate_w = sb("gate_w", [P, 2, NB, NE])
        beta_sb = sb("beta_sb", [NE, D])
        pos = sb("pos", [P, NB, NE])
        pos_t = sb("pos_t", [P, NB, NE])
        cnt_i = sb("cnt_i", [P, NE], I32)
        cnt_f = sb("cnt_f", [P, NE])
        end_f = sb("end_f", [P, NE])
        off_f = sb("off_f", [P, NE])
        one_f = sb("one_f", [P, NE])
        slot_f = sb("slot_f", [P, TOPK, NB])
        slot_i = sb("slot_i", [P, TOPK, NB], I32)
        slot_hi = sb("slot_hi", [P, TOPK, NB], I32)
        slot_lo = sb("slot_lo", [P, TOPK, NB], I32)
        slot_hf = sb("slot_hf", [P, TOPK, NB])
        slot_lf = sb("slot_lf", [P, TOPK, NB])
        lo_oh = sb("lo_oh", [P, 2, P], BF16)
        hi_oh = sb("hi_oh", [P, 2, 2 * SW], BF16)
        chunk_ge = work[:, 2048:2048 + SW * NE].rearrange("p (c e) -> p c e", e=NE)
        chunk_ef = sb("chunk_ef", [P, SW])
        chunk_e = sb("chunk_e", [P, SW], I32)
        tok_f = sb("tok_f", [P, SW])
        tok = sb("tok", [P, SW], U32)
        e_mv = sb("e_mv", [P, 2, 8])
        e_stats = sb("e_stats", [P, 2, 6])

        x_in = [sem(f"x_in{g}") for g in range(XG)]
        edges_in = sem("edges_in")
        img_in = sem("img_in")
        attw_in = sem("attw_in")
        gnnw_in = sem("gnnw_in")
        x_again = [sem(f"x_again{g}") for g in range(XG)]
        w1_in = sem("w1_in")
        w2_in = sem("w2_in")
        ffn_rows_in = sem("ffn_rows_in")
        l1w_in = sem("l1w_in")
        xf_out = sem("xf_out")
        consts_ready = sem("consts_ready")
        pool_order = sem("pool_order")
        dve_order = sem("dve_order")
        edge_oh = sem("edge_oh")
        edge_oh_used = sem("edge_oh_used")
        pass_out = sem("pass_out")
        src_k_ready = sem("src_k_ready")
        edges_f = sem("edges_f")
        base_ps = sem("base_ps")
        outside_ready = sem("outside_ready")
        outside_ps = sem("outside_ps")
        loose_ready = sem("loose_ready")
        win_oh = sem("win_oh")
        win_ps = sem("win_ps")
        num_ready = sem("num_ready")
        win_bank_free = sem("win_bank_free")
        counts_zero = sem("counts_zero")
        counts_ready = sem("counts_ready")
        xn_ready = sem("xn_ready")
        tr_ps = sem("tr_ps")
        tr_sb = sem("tr_sb")
        img_ps = sem("img_ps")
        img_bias_ready = sem("img_bias_ready")
        img_ctx_ready = sem("img_ctx_ready")
        proj_ps = sem("proj_ps")
        proj_sb = sem("proj_sb")
        tanh_sb = sem("tanh_sb")
        scaled_sb = sem("scaled_sb")
        sum_ready = sem("sum_ready")
        att_ps = sem("att_ps")
        logits_zero = sem("logits_zero")
        logits_sb = sem("logits_sb")
        logits_turned = sem("logits_turned")
        att_shift = sem("att_shift")
        att_exp = sem("att_exp")
        att_ready = sem("att_ready")
        h1_ps = sem("h1_ps")
        h1_sb = sem("h1_sb")
        cf_ready = sem("cf_ready")
        cf_used = sem("cf_used")
        rest_rounded = sem("rest_rounded")
        rest_ready = sem("rest_ready")
        rest_used = sem("rest_used")
        ones_r_ready = sem("ones_r_ready")
        over_flag = sem("over_flag")
        over_ps = sem("over_ps")
        over_ready = sem("over_ready")
        lo_ready = sem("lo_ready")
        hi_ready = sem("hi_ready")
        deg_read = sem("deg_read")
        wg_in = sem("wg_in")
        agg_ps = sem("agg_ps")
        agg_sb = sem("agg_sb")
        out_ps = sem("out_ps")
        out_read = sem("out_read")
        router_ps = sem("router_ps")
        gate_diff = sem("gate_diff")
        gate_exp = sem("gate_exp")
        sel_ready = sem("sel_ready")
        gatew_ready = sem("gatew_ready")
        pos_ps = sem("pos_ps")
        slot_oh = sem("slot_oh")
        slot_ps = sem("slot_ps")
        tok_ready = sem("tok_ready")
        beta_ps = sem("beta_ps")
        beta_read = sem("beta_read")
        xs_in = [sem(f"xs_in{i}") for i in range(2)]
        xs_ps = sem("xs_ps")
        xs_T = sem("xs_T")
        hid_ps = sem("hid_ps")
        hid_sb = sem("hid_sb")
        hidT_ps = sem("hidT_ps")
        hidT_sb = sem("hidT_sb")
        y_ps = sem("y_ps")
        xb_ready = sem("xb_ready")
        yt_ready = sem("yt_ready")
        sd_ready = sem("sd_ready")
        yu_ready = sem("yu_ready")
        yg_ready = sem("yg_ready")
        y_out = [sem(f"y_out{i}") for i in range(2)]
        y_top_in = [sem(f"y_top_in{b}") for b in range(NB)]
        yv_ready = sem("yv_ready")
        es_ready = sem("es_ready")
        em_ready = sem("em_ready")
        er_ready = sem("er_ready")
        l1_ps = sem("l1_ps")
        l1_read = sem("l1_read")
        fin_ready = sem("fin_ready")
        out_done = sem("out_done")

        TR_X, TR_H1, TR_ATT = 0, NB, 2 * NB
        TR_XF = TR_ATT + NJ
        TR_GATE = TR_XF + NB
        TR_X3 = TR_GATE + NJ

        xb_dram = x.rearrange("(b p) d -> p b d", p=P)
        out_dram = out.rearrange("(b p) d -> p b d", p=P)

        block = ctx.enter_context(nc.Block())

        @block.sync
        def _(sp):
            sp.dma_start(src_i, src).then_inc(edges_in, 16)
            sp.dma_start(dst_i, dst).then_inc(edges_in, 16)
            for g in range(XG):
                sp.dma_start(x_sb[:, g * GB:(g + 1) * GB, :], xb_dram[:, g * GB:(g + 1) * GB, :]).then_inc(x_in[g], 16)
            sp.dma_start(img_sb[:], img).then_inc(img_in, 16)
            sp.dma_start(bfi[:, 0, :], bf).then_inc(img_in, 16)
            sp.dma_start(bfi[:, 1, :], bi).then_inc(img_in, 16)
            sp.dma_start(wi_sb, wi.rearrange("(k p) n -> p k n", p=P)).then_inc(img_in, 16)
            sp.dma_start(wim_sb, wim.rearrange("(k p) n -> p k n", p=P)).then_inc(img_in, 16)
            sp.dma_start(wf_sb, wf.rearrange("(k p) n -> p k n", p=P)).then_inc(attw_in, 16)
            sp.dma_start(wa_sb[:], wa).then_inc(attw_in, 16)
            sp.dma_start(ba_sb[:], ba.partition_broadcast(P)).then_inc(attw_in, 16)
            sp.dma_start(wn_sb, wn.rearrange("(k p) n -> p k n", p=P)).then_inc(gnnw_in, 16)
            sp.dma_start(wap_sb, wap.rearrange("(k p) n -> p k n", p=P)).then_inc(gnnw_in, 16)
            sp.dma_start(bn_sb[:], bn).then_inc(gnnw_in, 16)
            sp.dma_start(bim_sb[:], bim).then_inc(gnnw_in, 16)
            sp.dma_start(row_bias[:], bap.partition_broadcast(P)).then_inc(gnnw_in, 16)
            sp.dma_start(rw_sb[:], router.rearrange("(k p) n -> p k n", p=P)).then_inc(gnnw_in, 16)
            sp.dma_start(beta_sb[:], ffn_beta).then_inc(gnnw_in, 16)
            sp.wait_ge(agg_ps, DC * NJ)
            for g in range(XG):
                sp.dma_start(x_sb[:, g * GB:(g + 1) * GB, :], xb_dram[:, g * GB:(g + 1) * GB, :]).then_inc(
                    x_again[g], 16)
            sp.wait_ge(out_ps, NB)
            sp.dma_start(w1_sb.rearrange("p (e k f) -> p e k f", e=NE, k=DC),
                         w1.rearrange("e (k p) f -> p e k f", p=P)).then_inc(w1_in, 16)
            w2v = w2_sb.rearrange("p (e k d) -> p e k d", e=NE, k=FC)
            w2d = w2.rearrange("e (k p) d -> p e k d", p=P)
            sp.dma_start(w2v[:, 0:w2_cut], w2d[:, 0:w2_cut]).then_inc(w2_in, 16)
            sp.wait_ge(xn_ready, 2 * NB)
            sp.dma_start(xf_dram.rearrange("(b p) d -> p b d", p=P), xn).then_inc(xf_out, 16)
            sp.wait_ge(router_ps, 1)
            sp.dma_start(w2v[:, w2_cut:NE], w2d[:, w2_cut:NE]).then_inc(w2_in, 16)
            sp.dma_start(b1_row, b1.partition_broadcast(P)).then_inc(ffn_rows_in, 16)
            sp.wait_ge(xf_out, 16)
            sp.dma_start(b2_row, b2.partition_broadcast(P)).then_inc(ffn_rows_in, 16)
            sp.dma_start(gamma_row, ffn_gamma.partition_broadcast(P)).then_inc(ffn_rows_in, 16)

            def store(j, b):
                sp.wait_ge(yg_ready, j + 1)
                sp.dma_start(y_dram[bass.ds(j * P, P), :], yu[:, b, :]).then_inc(y_out[b], 16)

            with sp.Fori(0, NCH - 1, 2) as j:
                store(j, 0)
                store(j + 1, 1)
            store(NCH - 1, 0)

            sp.wait_ge(hid_ps, NCH)
            sp.dma_start(ws_sb, w_self.rearrange("(k p) n -> p k n", p=P)).then_inc(l1w_in, 16)
            sp.dma_start(row_bias[:], l1_bias.partition_broadcast(P)).then_inc(l1w_in, 16)
            sp.wait_ge(xs_ps, NCH)
            sp.wait_ge(xb_ready, NCH)
            sp.dma_start(l1g_row, l1_gamma.partition_broadcast(P)).then_inc(l1w_in, 16)
            sp.dma_start(l1b_row, l1_beta.partition_broadcast(P)).then_inc(l1w_in, 16)
            sp.wait_ge(agg_ps, 2 * DC * NJ)
            sp.dma_start(wg_sb, w_neigh.rearrange("(k p) n -> p k n", p=P)).then_inc(wg_in, 16)
            for b in range(NB):
                sp.wait_ge(fin_ready, b + 1)
                sp.dma_start(out_dram[:, b, :], x_sb[:, b, :]).then_inc(out_done, 16)
            sp.wait_ge(out_done, 16 * NB)
            for i in range(2):
                sp.wait_ge(y_out[i], 16 * ((NCH + 1 - i) // 2))

        @block.gpsimd
        def _(pool):
            pool.memset(ident[:], 0.0).then_inc(pool_order, 1)
            pool.memset(before_bf[:], 0.0).then_inc(pool_order, 1)
            pool.memset(row0[:], 0.0).then_inc(pool_order, 1)
            pool.wait_ge(pool_order, 3)
            pool.memset(row0[0:1, :], 1.0).then_inc(consts_ready, 1)
            pool.affine_select(out=ident[:], in_=ident[:], compare_op=ALU.not_equal, fill=1.0, base=0,
                               pattern=[[-1, P]], channel_multiplier=1).then_inc(consts_ready, 1)
            pool.affine_select(out=before_bf[:], in_=before_bf[:], compare_op=ALU.is_ge, fill=1.0, base=0,
                               pattern=[[-1, P]], channel_multiplier=1).then_inc(consts_ready, 1)
            pool.memset(ones_bf[:], 1.0).then_inc(consts_ready, 1)
            pool.memset(count_max[:], 0.0).then_inc(consts_ready, 1)
            pool.iota(iota_n, pattern=[[1, N]], base=0, channel_multiplier=0).then_inc(consts_ready, 1)
            pool.iota(iota_i[:], pattern=[[1, P]], base=0, channel_multiplier=0).then_inc(consts_ready, 1)
            pool.iota(key_i[:], pattern=[[-1, 16]], base=16, channel_multiplier=0).then_inc(consts_ready, 1)
            pool.iota(iota_pi[:], pattern=[[1, 1]], base=0, channel_multiplier=1).then_inc(consts_ready, 1)
            pool.memset(counts[:].rearrange("p b n -> p (b n)").bitcast(F32), 0.0).then_inc(counts_zero, 1)

            def gather(j):
                if j == 0:
                    pool.wait_ge(tok_ready, 2)
                    pool.wait_ge(xf_out, 16)
                    pool.wait_ge(beta_ps, NB)
                if j >= 2:
                    pool.wait_ge(xs_ps, j - 1)
                    pool.wait_ge(xb_ready, j - 1)
                pool.indirect_dma_start(out=xs[:, j % 2, :], out_offset=None, in_=xf_dram,
                                        in_offset=bass.IndirectOffsetOnAxis(tok[:, j:j + 1], 0)
                                        ).then_inc(xs_in[j % 2], 16)

            def scale(j):
                e = pool.value_load(chunk_e[0:1, j:j + 1], min_val=0, max_val=NE - 1)
                pool.wait_ge(yu_ready, j + 1)
                pool.tensor_tensor(yu[:, j % 2, :], yu[:, j % 2, :], gamma_row[:, bass.ds(e * D, D)],
                                   ALU.mult).then_inc(yg_ready, 1)

            gather(0)
            for j in range(NCH):
                if j + 1 < NCH:
                    gather(j + 1)
                e = pool.value_load(chunk_e[0:1, j:j + 1], min_val=0, max_val=NE - 1)
                if j == 0:
                    pool.wait_ge(ffn_rows_in, 48)
                if j >= 2:
                    pool.wait_ge(yt_ready, j - 1)
                pool.wait_ge(xs_in[j % 2], 16 * (j // 2 + 1))
                pool.tensor_tensor(xb[:, j % 2, :], xs[:, j % 2, :], b2_row[:, bass.ds(e * D, D)],
                                   ALU.add).then_inc(xb_ready, 1)
                if j >= 3:
                    scale(j - 3)
            for j in range(NCH - 3, NCH):
                scale(j)
            for i in range(2):
                pool.wait_ge(y_out[i], 16 * ((NCH + 1 - i) // 2))
            pool.wait_ge(yg_ready, NCH)
            for b in range(NB):
                for k in range(TOPK):
                    pool.indirect_dma_start(out=y_top[:, k, b, :], out_offset=None, in_=y_dram,
                                            in_offset=bass.IndirectOffsetOnAxis(slot_i[:, k, b:b + 1].bitcast(U32), 0)
                                            ).then_inc(y_top_in[b], 16)
            for b in range(NB):
                pool.wait_ge(hi_ready, b + 1)
                pool.wait_ge(tr_ps, TR_X3 + b + 1)
                pool.tensor_tensor(rows_lo[1][:, b, :], xn3[:, b, :], rows_hi[:, b, :].bitcast(F32),
                                   ALU.subtract).then_inc(lo_ready, 1)

        @block.tensor
        def _(pe):
            mm = nc.tensor.matmul

            pe.wait_ge(img_in, 80)
            for m in range(PC):
                for k in range(KI):
                    last = mm(ps[:, 0, m * R:(m + 1) * R], wi_sb[:, k, m * P:(m + 1) * P], img_sb[:, k, :],
                              start=(k == 0), stop=(k == KI - 1))
            last.then_inc(img_ps, 1)
            for k in range(KI):
                last = mm(ps[0:R, 1, :], img_sb[:, k, :], wim_sb[:, k, :], start=(k == 0), stop=(k == KI - 1))
            last.then_inc(img_ps, 1)

            def turn(t, pieces):
                if t >= 2:
                    pe.wait_ge(tr_sb, t - 1)
                if TR_H1 + 2 <= t < TR_ATT + 2:
                    pe.wait_ge(lo_ready, t - TR_H1 - 1)
                for to, fr in pieces:
                    last = nc.tensor.transpose(to, fr, ident[0:fr.shape[0], 0:fr.shape[0]])
                last.then_inc(tr_ps, 1)

            def turn_rows(t0, rows, ready, n0):
                for b in range(NB):
                    pe.wait_ge(ready, n0 + b + 1)
                    bank = ps[:, 6 + (t0 + b) % 2, :]
                    turn(t0 + b, [(bank[:, c * P:(c + 1) * P], rows[:, b, c * P:(c + 1) * P]) for c in range(DC)])

            pe.wait_ge(consts_ready, 9)
            turn_rows(TR_X, xn, xn_ready, 0)

            pe.wait_ge(edges_f, 1)
            pe.wait_ge(img_bias_ready, 1)
            mm(ps[:, 0, 0:EG], row0[:], dst_f[:, 0:EC:GC], start=True, stop=True).then_inc(base_ps, 1)

            pe.wait_ge(attw_in, 48)
            pe.wait_ge(tr_sb, TR_X + NB)
            for t in range(PC * NJ):
                m, j = t // NJ, t % NJ
                if t >= 4:
                    pe.wait_ge(proj_sb, t - 3)
                for k in range(DC):
                    last = mm(ps[:, 2 + t % 4, :], wf_sb[:, k, m * P:(m + 1) * P], xT[:, k, j * 512:(j + 1) * 512],
                              start=(k == 0), stop=(k == DC - 1))
                last.then_inc(proj_ps, 1)

            pe.wait_ge(outside_ready, 1)
            pe.wait_ge(img_ctx_ready, 1)
            mm(ps[:, 1, 0:1], ones_bf[:], outside_bf[:], start=True, stop=True).then_inc(outside_ps, 1)
            pe.wait_ge(loose_ready, 1)
            pe.wait_ge(proj_sb, PC * NJ)

            pe.wait_ge(logits_zero, 1)

            def logits_region(r, u):
                pe.wait_ge(sum_ready, r + 1)
                for j in range(NJ):
                    last = mm(ps[0:R, LOGIT_BANKS[j], :], region_col[:, u, :], tanh_t[u][:, 1, j * 512:(j + 1) * 512],
                              start=False, stop=True, skip_group_check=True)
                last.then_inc(att_ps, 1)

            def window_chunk(g, pair, q):
                if q % OC == 0:
                    pe.wait_ge(win_oh, pair + 1)
                if q % GC == 0:
                    pe.wait_ge(win_bank_free, g + 1)
                last = mm(ps[:, 2 + (q // GC) % 4, 0:WW], oh_lo[q // OC][:, :, q % OC],
                          oh_win[q // OC][:, :, q % OC], start=(q % GC == 0), stop=(q % GC == GC - 1))
                if q % GC == GC - 1:
                    last.then_inc(win_ps, 1)

            with pe.Fori(0, R // 3) as i:
                for u in range(3):
                    logits_region(3 * i + u, u)
                    for q in range(8 * GC * u // 3, 8 * GC * (u + 1) // 3):
                        window_chunk(8 * i + q // GC, 4 * i + q // OC, q)

            def count_chunk(k, c, b, start, stop):
                pe.wait_ge(edge_oh, k * EC + c + 1)
                for s in range(2):
                    for j in range(NJ):
                        last = mm(ps[:, 2 + s * NJ + j, :], oh_src[:, b, s * P:(s + 1) * P],
                                  oh_dst[:, b, j * 512:(j + 1) * 512], start=start, stop=stop)
                last.then_inc(edge_oh_used, 1)

            pe.wait_ge(loose_ready, 1)
            n_loose = pe.value_load(loose[0:1, 0:1], min_val=0, max_val=P)
            with pe.If(n_loose > 0):
                pe.wait_ge(win_bank_free, EG + 4)
                pe.wait_ge(logits_sb, NJ)
                for k in range(NB // 2):
                    if k >= 1:
                        pe.wait_ge(pass_out, k)
                    count_chunk(k, 0, 0, True, False)
                    with pe.Fori(0, EC // 2 - 1) as c:
                        count_chunk(k, 2 * c + 1, 1, False, False)
                        count_chunk(k, 2 * c + 2, 0, False, False)
                    count_chunk(k, EC - 1, 1, False, True)
                pe.wait_ge(pass_out, NB // 2)

            pe.wait_ge(logits_sb, NJ)
            for b in range(NB):
                last = nc.tensor.transpose(ps[:, 0, b * R:(b + 1) * R], logits_T[0:R, b * P:(b + 1) * P],
                                           ident[0:R, 0:R])
            last.then_inc(logits_turned, 1)

            pe.wait_ge(gnnw_in, 112)
            pe.wait_ge(win_bank_free, EG + 4)
            for t in range(DC * NJ):
                j, m = t // DC, t % DC
                if t >= 4:
                    pe.wait_ge(h1_sb, t - 3)
                for k in range(DC):
                    last = mm(ps[:, 2 + t % 4, :], wn_sb[:, k, m * P:(m + 1) * P], xT[:, k, j * 512:(j + 1) * 512],
                              start=(k == 0), stop=(k == DC - 1))
                last.then_inc(h1_ps, 1)
            pe.wait_ge(over_flag, 1)
            mm(ps[:, 1, 0:1], ones_bf[:], over_bf[:], start=True, stop=True).then_inc(over_ps, 1)
            for b in range(NB):
                pe.wait_ge(h1_sb, DC * (b // JB + 1))
                bank = ps[:, 6 + (TR_H1 + b) % 2, :]
                turn(TR_H1 + b, [(bank[:, c * P:(c + 1) * P], hT[:, c, b * P:(b + 1) * P]) for c in range(DC)])
            pe.wait_ge(att_ready, 1)
            for j in range(NJ):
                bank = ps[0:R, 6 + (TR_ATT + j) % 2, :]
                turn(TR_ATT + j, [(bank[:, i * P:(i + 1) * P], att[:, j * JB + i, :]) for i in range(JB)])

            pe.wait_ge(over_ready, 1)
            n_over = pe.value_load(over[0:1, 0:1], min_val=0, max_val=P)

            def add_rest(layer, j):
                for s in range(NB):
                    n = (layer * NJ + j) * NB + s
                    pe.wait_ge(rest_ready, n + 1)
                    if layer == 0:
                        pe.wait_ge(lo_ready, s + 1)
                    else:
                        pe.wait_ge(lo_ready, NB + s + 1)
                        mm(ps[:, 6 + j % 2, :], ones_r, cf_rest[:, n % 2, :], start=False, stop=False)
                    for m in range(DC):
                        for rows in (rows_hi, rows_lo[layer]):
                            last = mm(ps[:, (j * DC + m) % 6, :], rows[:, s, m * P:(m + 1) * P], cf_rest[:, n % 2, :],
                                      start=False, stop=False)
                    last.then_inc(rest_used, 1)

            def aggregate(layer):
                for j in range(NJ):
                    if layer == 1:
                        if j < 2:
                            pe.wait_ge(tr_sb, TR_X3 + NB)
                        else:
                            pe.wait_ge(deg_read, j - 1)
                    for m in range(DC):
                        t = (layer * NJ + j) * DC + m
                        if t >= 6 and (layer == 0 or j * DC + m >= 6):
                            pe.wait_ge(agg_sb, t - 5)
                    for s in range(NB):
                        n = (layer * NJ + j) * NB + s
                        if s == NB - 1:
                            with pe.If(n_over > 0):
                                add_rest(layer, j)
                        pe.wait_ge(cf_ready, n + 1)
                        if j == 0:
                            pe.wait_ge(lo_ready, layer * NB + s + 1)
                        for m in range(DC):
                            bank = ps[:, (j * DC + m) % 6, :]
                            mm(bank, rows_hi[:, s, m * P:(m + 1) * P], cf[:, n % 3, :], start=(s == 0), stop=False)
                            last = mm(bank, rows_lo[layer][:, s, m * P:(m + 1) * P], cf[:, n % 3, :], start=False,
                                      stop=(layer == 1 and s == NB - 1))
                            if layer == 1 and s == NB - 1:
                                last.then_inc(agg_ps, 1)
                        if layer == 1:
                            last = mm(ps[:, 6 + j % 2, :], ones_r, cf[:, n % 3, :], start=(s == 0),
                                      stop=(s == NB - 1))
                        last.then_inc(cf_used, 1)
                    if layer == 0:
                        for m in range(DC):
                            mm(ps[:, (j * DC + m) % 6, :], img_ctx[0:R, m * P:(m + 1) * P],
                               attT[0:R, j * 512:(j + 1) * 512], start=False, stop=True).then_inc(agg_ps, 1)

            pe.wait_ge(tr_sb, TR_ATT + NJ)
            aggregate(0)

            for b in range(NB):
                if b % JB == 0:
                    pe.wait_ge(agg_sb, DC * (b // JB + 1))
                if b == 0:
                    pe.wait_ge(agg_sb, DC * NJ)
                if b >= 4:
                    pe.wait_ge(out_read, b - 3)
                for k in range(2 * DC):
                    rows = xT[:, k, b * P:(b + 1) * P] if k < DC else hT[:, k - DC, b * P:(b + 1) * P]
                    last = mm(ps[:, b % 4, :], rows, wap_sb[:, k, :], start=(k == 0), stop=(k == 2 * DC - 1))
                last.then_inc(out_ps, 1)

            turn_rows(TR_XF, xn, xn_ready, NB)
            pe.wait_ge(tr_sb, TR_XF + NB)
            pe.wait_ge(out_read, NB)
            for b in range(NB):
                for k in range(DC):
                    last = mm(ps[:, 0, b * NE:(b + 1) * NE], xT[:, k, b * P:(b + 1) * P], rw_sb[:, k, :],
                              start=(k == 0), stop=(k == DC - 1))
            last.then_inc(router_ps, 1)

            pe.wait_ge(sel_ready, 1)
            for s in range(NB):
                mm(ps[:, 1, 0:NB * NE], before_bf[:] if s == 0 else ones_bf[:],
                   sel_bf[:, (NB - 1 - s) * NE:(2 * NB - 1 - s) * NE], start=(s == 0), stop=(s == NB - 1))
            for b in range(NB):
                last = mm(ps[:, 2, 0:NE], ones_bf[:], sel_bf[:, (NB - 1 + b) * NE:(NB + b) * NE],
                          start=(b == 0), stop=(b == NB - 1))
            last.then_inc(pos_ps, 1)

            for n in range(TOPK * NB):
                pe.wait_ge(slot_oh, n + 1)
                mm(ps[:, 3, 0:2 * SW], lo_oh[:, n % 2, :], hi_oh[:, n % 2, :],
                   start=(n == 0), stop=(n == TOPK * NB - 1)).then_inc(slot_ps, 1)

            pe.wait_ge(gatew_ready, 1)
            for j in range(NJ):
                bank = ps[0:NE, 6 + (TR_GATE + j) % 2, :]
                turn(TR_GATE + j, [(bank[:, i * P:(i + 1) * P], gate_w[:, 0, j * JB + i, :]) for i in range(JB)])
            pe.wait_ge(tr_sb, TR_GATE + NJ)
            for b in range(NB):
                if b >= 2:
                    pe.wait_ge(beta_read, b - 1)
                mm(ps[:, 4 + b % 2, :], gate_T[0:NE, b * P:(b + 1) * P], beta_sb[:], start=True,
                   stop=True).then_inc(beta_ps, 1)

            pe.wait_ge(w1_in, 16)
            pe.wait_ge(w2_in, 32)
            pe.wait_ge(tok_ready, 2)
            pe.wait_ge(beta_read, NB)

            def turn_tokens(j, b, half, free):
                pe.wait_ge(xs_in[b], 16 * (half + 1))
                if free is not None:
                    pe.wait_ge(xs_T, free)
                for c in range(DC):
                    last = nc.tensor.transpose(ps[:, 4 + b, c * P:(c + 1) * P], xs[:, b, c * P:(c + 1) * P], ident[:])
                last.then_inc(xs_ps, 1)

            def expert_of(j):
                return pe.value_load(chunk_e[0:1, bass.ds(j, 1)], min_val=0, max_val=NE - 1)

            def hidden(j, b, free):
                e = expert_of(j)
                pe.wait_ge(xs_T, j + 1)
                if free is not None:
                    pe.wait_ge(hid_sb, free)
                for k in range(DC):
                    last = mm(ps[:, b, 0:F], xsT[:, b, k, :], w1_sb[:, bass.ds(e * (DC * F) + k * F, F)],
                              start=(k == 0), stop=(k == DC - 1))
                last.then_inc(hid_ps, 1)

            def turn_hidden(j, b, free):
                pe.wait_ge(hid_sb, j + 1)
                if free is not None:
                    pe.wait_ge(hidT_sb, free)
                for c in range(FC):
                    last = nc.tensor.transpose(ps[:, 6 + b, c * P:(c + 1) * P], hb[:, b, c * P:(c + 1) * P], ident[:])
                last.then_inc(hidT_ps, 1)

            def expert_out(j, b, free):
                e = expert_of(j)
                pe.wait_ge(hidT_sb, j + 1)
                if free is not None:
                    pe.wait_ge(yt_ready, free)
                for k in range(FC):
                    last = mm(ps[:, 2 + b, :], hbT[:, b, k, :], w2_sb[:, bass.ds(e * (FC * D) + k * D, D)],
                              start=(k == 0), stop=(k == FC - 1))
                last.then_inc(y_ps, 1)

            def expert_step(n, u, half, more=True):
                hidden(n + u, u % 2, n + (u - 1))
                if more:
                    turn_tokens(n + (u + 1), 1 - u % 2, half, n + u)
                expert_out(n + (u - 1), 1 - u % 2, n + (u - 2) if u > 1 else None)
                turn_hidden(n + u, u % 2, n + (u - 1))

            turn_tokens(0, 0, 0, None)
            hidden(0, 0, None)
            turn_tokens(1, 1, 0, None)
            turn_hidden(0, 0, None)
            expert_step(0, 1, 1)
            expert_step(0, 2, 1)
            with pe.Fori(0, (NCH - 5) // 2) as i:
                expert_step(2 * i, 3, i + 2)
                expert_step(2 * i, 4, i + 2)
            expert_step(NCH - 5, 3, NCH // 2)
            expert_step(NCH - 5, 4, 0, more=False)
            expert_out(NCH - 1, 0, NCH - 2)

            turn_rows(TR_X3, xn3, xn_ready, 2 * NB)
            pe.wait_ge(yt_ready, NCH)
            pe.wait_ge(ones_r_ready, 1)
            aggregate(1)
            pe.wait_ge(l1w_in, 64)
            pe.wait_ge(agg_sb, 2 * DC * NJ)
            pe.wait_ge(deg_read, NJ)

            def own(b):
                if b >= 8:
                    pe.wait_ge(l1_read, b - 7)
                for k in range(DC):
                    mm(ps[:, b % 8, :], xT[:, k, b * P:(b + 1) * P], ws_sb[:, k, :], start=(k == 0), stop=False)

            for b in range(6):
                own(b)
            pe.wait_ge(wg_in, 16)
            for b in range(NB):
                for k in range(DC):
                    last = mm(ps[:, b % 8, :], hT[:, k, b * P:(b + 1) * P], wg_sb[:, k, :],
                              start=False, stop=(k == DC - 1))
                last.then_inc(l1_ps, 1)
                if b + 6 < NB:
                    own(b + 6)

        @block.scalar
        def _(act):
            def evac(to, fr):
                return nc.scalar.activation(to, fr, ACT.Copy)

            def evac_turned(t0, to, rows=P):
                for b in range(NB):
                    act.wait_ge(tr_ps, t0 + b + 1)
                    evac(to(b), ps[:, 6 + (t0 + b) % 2, :].rearrange("p (c n) -> p c n", c=DC)).then_inc(tr_sb, 1)

            act.wait_ge(img_ps, 2)
            evac(img_ctx[0:R, :], ps[0:R, 1, :]).then_inc(img_ctx_ready, 1)
            evac_turned(TR_X, lambda b: xT[:, :, b * P:(b + 1) * P])
            for t in range(PC * NJ):
                m, j = t // NJ, t % NJ
                act.wait_ge(proj_ps, t + 1)
                evac(node_proj[:, m, j * 512:(j + 1) * 512], ps[:, 2 + t % 4, :]).then_inc(proj_sb, 1)

            act.wait_ge(img_bias_ready, 1)
            act.wait_ge(proj_sb, PC * NJ)

            def tanh_region(r, u, used):
                if used is not None:
                    act.wait_ge(att_ps, used)
                for m in range(PC):
                    nc.scalar.activation(tanh_t[u][:, m, :], node_proj[:, m, :], ACT.Tanh,
                                         bias=img_bias[:, m, bass.ds(r, 1)]).then_inc(tanh_sb, 1)
                act.wait_ge(tanh_sb, PC * r + 1)
                nc.scalar.activation(tanh_t[u][:, 0, :], tanh_t[u][:, 0, :], ACT.Copy,
                                     scale=wa_sb[:, 0:1]).then_inc(scaled_sb, 1)

            for u in range(3):
                tanh_region(u, u, None)
            with act.Fori(0, R // 3 - 1) as i:
                for u in range(3):
                    tanh_region(3 * i + (u + 3), u, 3 * i + (u + 1))
            act.wait_ge(att_ps, R)
            for j in range(NJ):
                evac(logits_T[0:R, j * 512:(j + 1) * 512], ps[0:R, LOGIT_BANKS[j], :]).then_inc(logits_sb, 1)

            def h1_tile(t):
                j, m = t // DC, t % DC
                act.wait_ge(h1_ps, t + 1)
                nc.scalar.activation(hT[:, m, j * 512:(j + 1) * 512], ps[:, 2 + t % 4, :], ACT.Identity,
                                     bias=bn_sb[:, m:m + 1]).then_inc(h1_sb, 1)

            act.wait_ge(gnnw_in, 112)
            for t in range(DC):
                h1_tile(t)
            act.wait_ge(att_shift, 1)
            nc.scalar.activation(att, att, ACT.Exp).then_inc(att_exp, 1)
            for t in range(DC, DC * NJ):
                h1_tile(t)
            evac_turned(TR_H1, lambda b: rows_hi[:, b, :].rearrange("p (c n) -> p c n", c=DC))
            for j in range(NJ):
                t = TR_ATT + j
                act.wait_ge(tr_ps, t + 1)
                evac(attT[0:R, j * 512:(j + 1) * 512], ps[0:R, 6 + t % 2, :]).then_inc(tr_sb, 1)
            for t in range(DC * NJ):
                j, m = t // DC, t % DC
                act.wait_ge(agg_ps, t + 1)
                nc.scalar.activation(xT[:, m, j * 512:(j + 1) * 512], ps[:, (j * DC + m) % 6, :], ACT.Identity,
                                     bias=bim_sb[:, m:m + 1]).then_inc(agg_sb, 1)
            evac_turned(TR_XF, lambda b: xT[:, :, b * P:(b + 1) * P])
            act.wait_ge(gate_diff, 1)
            nc.scalar.activation(gate_e[:], gate_d[:], ACT.Exp).then_inc(gate_exp, 1)
            for j in range(NJ):
                t = TR_GATE + j
                act.wait_ge(tr_ps, t + 1)
                evac(gate_T[0:NE, j * 512:(j + 1) * 512], ps[0:NE, 6 + t % 2, :]).then_inc(tr_sb, 1)

            def tokens_out(j, b, free):
                act.wait_ge(xs_ps, j + 1)
                if free is not None:
                    act.wait_ge(hid_ps, free)
                evac(xsT[:, b], ps[:, 4 + b, :].rearrange("p (c n) -> p c n", c=DC)).then_inc(xs_T, 1)

            def hidden_out(j, b, free):
                act.wait_ge(hidT_ps, j + 1)
                if free is not None:
                    act.wait_ge(y_ps, free)
                nc.scalar.activation(hbT[:, b], ps[:, 6 + b, 0:F].rearrange("p (c n) -> p c n", c=FC),
                                     ACT.Relu).then_inc(hidT_sb, 1)

            def root(j, b):
                act.wait_ge(yv_ready, j + 1)
                nc.scalar.activation(e_mv[:, b, 3:4], e_mv[:, b, 2:3], ACT.Sqrt).then_inc(sd_ready, 1)

            def step(n, u, more=True):
                if more:
                    tokens_out(n + (u + 1), 1 - u % 2, n + u)
                hidden_out(n + u, u % 2, n + (u - 1))
                root(n + (u - 1), 1 - u % 2)

            tokens_out(0, 0, None)
            tokens_out(1, 1, None)
            hidden_out(0, 0, None)
            step(0, 1)
            step(0, 2)
            with act.Fori(0, (NCH - 5) // 2) as i:
                step(2 * i, 3)
                step(2 * i, 4)
            step(NCH - 5, 3)
            step(NCH - 5, 4, more=False)
            root(NCH - 1, 0)

            for b in range(NB):
                act.wait_ge(xn_ready, 2 * NB + b + 1)
                evac(rows_hi[:, b, :], xn3[:, b, :]).then_inc(hi_ready, 1)
                act.wait_ge(tr_ps, TR_X3 + b + 1)
                evac(xT[:, :, b * P:(b + 1) * P], ps[:, 6 + (TR_X3 + b) % 2, :].rearrange(
                    "p (c n) -> p c n", c=DC)).then_inc(tr_sb, 1)

        @block.vector
        def _(dve):
            order = [0]
            v = nc.vector

            def link(ins):
                order[0] += 1
                ins.then_inc(dve_order, 1)
                dve.wait_ge(dve_order, order[0])

            def rsqrt(to, var, tmp):
                link(v.tensor_scalar(tmp.bitcast(I32), var.bitcast(I32), 1, None, ALU.logical_shift_right))
                link(v.tensor_scalar(to.bitcast(I32), tmp.bitcast(I32), -1.0, RSQRT_MAGIC, ALU.mult, ALU.add))
                for _ in range(4):
                    link(v.tensor_tensor(tmp, to, to, ALU.mult))
                    link(v.tensor_tensor(tmp, tmp, var, ALU.mult))
                    link(v.tensor_scalar(tmp, tmp, -0.5, 1.5, ALU.mult, ALU.add))
                    link(v.tensor_tensor(to, to, tmp, ALU.mult))

            def row_scales(g0, g1):
                for b in range(g0, g1):
                    last = v.bn_aggr(mv[:, b, :], stats[:, b, :])
                link(last)
                link(v.tensor_scalar(var_e[:, g0:g1], mv[:, g0:g1, 1], GNN_EPS, None, ALU.add))
                rsqrt(rstd[:, g0:g1], var_e[:, g0:g1], nt_a[:, g0:g1])

            def normalise(g0, g1, to=xn):
                for b in range(g0, g1):
                    last = v.bn_stats(stats[:, b, :], x_sb[:, b, :])
                link(last)
                row_scales(g0, g1)
                for b in range(g0, g1):
                    v.tensor_scalar(to[:, b, :], x_sb[:, b, :], mv[:, b, 0:1], rstd[:, b:b + 1],
                                    ALU.subtract, ALU.mult).then_inc(xn_ready, 1)

            dve.wait_ge(consts_ready, 9)
            v.tensor_copy(iota_f[:], iota_i[:])
            v.tensor_copy(first_key[:], key_i[:])
            v.memset(one_f[:], 1.0)
            v.memset(sel_bf[:], 0.0)
            for b in range(NB):
                v.memset(block_col[:, b:b + 1], float(b))
            link(v.tensor_copy(iota_p[:], iota_pi[:]))

            for g in range(XG):
                dve.wait_ge(x_in[g], 16)
                normalise(g * GB, (g + 1) * GB)

            dve.wait_ge(img_in, 80)
            link(v.tensor_tensor(bfi_sum[:], bfi[:, 0, :], bfi[:, 1, :], ALU.add))
            dve.wait_ge(img_ps, 2)
            for m in range(PC):
                last = v.tensor_scalar(img_bias[:, m, :], ps[:, 0, m * R:(m + 1) * R], bfi_sum[:, m:m + 1], None,
                                       ALU.add)
            last.then_inc(img_bias_ready, 1)

            dve.wait_ge(edges_in, 32)
            v.tensor_copy(dst_f, dst_i).then_inc(edges_f, 1)
            v.tensor_scalar(edge_t.bitcast(I32), src_i, 7, None, ALU.logical_shift_right)
            link(v.tensor_scalar(edge_u.bitcast(I32), src_i, P - 1, None, ALU.bitwise_and))
            link(v.tensor_copy(lo_16[:], edge_u.bitcast(I32)))
            dve.wait_ge(base_ps, 1)
            link(v.tensor_scalar(base_f[:], ps[:, 0, 0:EG], float(N - WIN), None, ALU.min))
            v.tensor_copy(base_i[:], base_f[:])
            dve.wait_ge(edges_f, 1)
            link(v.tensor_tensor(edge_u.rearrange("p (g c) -> p g c", c=GC), dst_f.rearrange("p (g c) -> p g c", c=GC),
                                 base_f[:].unsqueeze(2).to_broadcast([P, EG, GC]), ALU.subtract))
            v.tensor_reduce(outside[:, 0:1], edge_u, AX_X, ALU.max)
            v.tensor_reduce(outside[:, 1:2], edge_u, AX_X, ALU.min)
            link(v.scalar_tensor_tensor(out=win_16[:], in0=edge_t.bitcast(I32), scalar=float(WIN), in1=edge_u,
                                        op0=ALU.mult, op1=ALU.add))
            link(v.tensor_scalar(outside[:, 0:1], outside[:, 0:1], WIN - 0.5, None, ALU.is_gt))
            link(v.tensor_scalar(outside[:, 1:2], outside[:, 1:2], 0.0, None, ALU.is_lt))
            v.tensor_tensor(outside_bf[:], outside[:, 0:1], outside[:, 1:2], ALU.max).then_inc(outside_ready, 1)
            dve.wait_ge(outside_ps, 1)
            v.tensor_copy(loose[:], ps[:, 1, 0:1]).then_inc(loose_ready, 1)

            def window_rows(pair, k):
                for to, num, of in ((oh_lo[k], num_win[:, 0:P, :], lo_16), (oh_win[k], num_win, win_16)):
                    last = v.tensor_tensor(to, num, of[:, bass.ds(OC * pair, OC)].unsqueeze(1).to_broadcast(
                        [P, num.shape[1], OC]), ALU.is_equal)
                last.then_inc(win_oh, 1)

            def window_add(g, u):
                base = dve.value_load(base_i[0:1, bass.ds(g, 1)], min_val=0, max_val=N - WIN)
                dve.wait_ge(win_ps, g + 1)
                dve.wait_ge(win_bank_free, g + 4)
                at_base = counts[:, :, bass.ds(base, WIN)]
                v.tensor_tensor(at_base, at_base, ps[:, 2 + u % 4, 0:WW].rearrange("p (b w) -> p b w", w=WIN),
                                ALU.add).then_inc(win_bank_free, 1)

            def sum_region(r, u):
                v.tensor_scalar(region_col[:, u, :], iota_f[:, 0:R], iota_f[:, bass.ds(r, 1)], None, ALU.is_equal)
                dve.wait_ge(scaled_sb, r + 1)
                v.scalar_tensor_tensor(out=tanh_t[u][:, 1, :], in0=tanh_t[u][:, 1, :], scalar=wa_sb[:, 1:2],
                                       in1=tanh_t[u][:, 0, :], op0=ALU.mult, op1=ALU.add).then_inc(sum_ready, 1)

            dve.wait_ge(counts_zero, 1)
            dve.wait_ge(loose_ready, 1)
            dve.wait_ge(img_ctx_ready, 1)
            dve.wait_ge(proj_sb, PC * NJ)
            v.memset(nt_b[:, 0:1], 0.0).then_inc(win_bank_free, 4)
            for j in range(NJ):
                last = v.memset(ps[0:R, LOGIT_BANKS[j], :], 0.0)
            last.then_inc(logits_zero, 1)
            v.tensor_copy(num_win, iota_n[:, 0:WW].unsqueeze(2).to_broadcast([P, WW, OC])).then_inc(num_ready, 1)
            dve.wait_ge(num_ready, 1)
            window_rows(0, 0)
            sum_region(0, 0)
            window_rows(1, 1)

            def window_turn(i, more=True):
                for u in range(8):
                    if u % 2 == 0 and (more or u < 4):
                        window_rows(4 * i + (u // 2 + 2), (u // 2 + 2) % 4)
                    if u % 3 == 0 and (more or u < 6):
                        sum_region(3 * i + (u // 3 + 1), (u // 3 + 1) % 3)
                    window_add(8 * i + u, u)

            with dve.Fori(0, R // 3 - 1) as i:
                window_turn(i)
            window_turn(R // 3 - 1, more=False)
            dve.wait_ge(win_bank_free, EG + 4)

            def edge_rows(k, c, b):
                v.tensor_scalar(oh_src[:, b, :], iota_n[:, 0:2 * P], src_k[:, bass.ds(c, 1)], None, ALU.is_equal)
                v.tensor_scalar(oh_dst[:, b, :], iota_n, dst_f[:, bass.ds(c, 1)], None,
                                ALU.is_equal).then_inc(edge_oh, 1)

            n_loose = dve.value_load(loose[0:1, 0:1], min_val=0, max_val=P)
            with dve.If(n_loose > 0):
                for k in range(NB // 2):
                    v.tensor_scalar(src_k, src_i, float(-2 * P * k), None, ALU.add).then_inc(src_k_ready, 1)
                    dve.wait_ge(src_k_ready, k + 1)
                    for c in range(2):
                        if k >= 1:
                            dve.wait_ge(edge_oh_used, k * EC + c - 1)
                        edge_rows(k, c, c)
                    with dve.Fori(0, EC // 2 - 1) as c:
                        for i in range(2):
                            dve.wait_ge(edge_oh_used, 2 * c + (k * EC + i + 1))
                            edge_rows(k, 2 * c + (i + 2), i)
                    dve.wait_ge(edge_oh_used, (k + 1) * EC)
                    for s in range(2):
                        last = v.tensor_copy(counts[:, 2 * k + s, :],
                                             ps[:, 2 + s * NJ:2 + (s + 1) * NJ, :].rearrange("p a b -> p (a b)"))
                    last.then_inc(pass_out, 1)
                dve.wait_ge(pass_out, NB // 2)
            v.memset(nt_b[:, 0:1], 0.0).then_inc(counts_ready, 1)

            dve.wait_ge(attw_in, 48)
            dve.wait_ge(logits_turned, 1)
            link(v.tensor_scalar(att, ps[:, 0, 0:NB * R].rearrange("p (b r) -> p b r", b=NB), ba_sb[:, 0:1], None,
                                 ALU.add))
            link(v.tensor_reduce(att_red, att, AX_X, ALU.max))
            v.tensor_tensor(att, att, att_red.unsqueeze(2).to_broadcast([P, NB, R]),
                            ALU.subtract).then_inc(att_shift, 1)
            dve.wait_ge(counts_ready, 1)
            link(v.tensor_reduce(count_max[:], counts[:], mybir.AxisListType.XY, ALU.max))
            v.tensor_scalar(over_bf[:], count_max[:], float(EXACT), None, ALU.is_gt).then_inc(over_flag, 1)
            dve.wait_ge(att_exp, 1)
            link(v.tensor_reduce(att_red, att, AX_X, ALU.add))
            link(v.reciprocal(att_inv, att_red))
            v.tensor_tensor(att, att, att_inv.unsqueeze(2).to_broadcast([P, NB, R]),
                            ALU.mult).then_inc(att_ready, 1)

            dve.wait_ge(over_ps, 1)
            v.tensor_copy(over[:], ps[:, 1, 0:1]).then_inc(over_ready, 1)

            for b in range(NB):
                dve.wait_ge(tr_sb, TR_H1 + b + 1)
                v.tensor_tensor(rows_lo[0][:, b, :], ps[:, 6 + (TR_H1 + b) % 2, :], rows_hi[:, b, :].bitcast(F32),
                                ALU.subtract).then_inc(lo_ready, 1)

            dve.wait_ge(over_ready, 1)
            n_over = dve.value_load(over[0:1, 0:1], min_val=0, max_val=P)

            def rest_tiles(layer, j):
                for s in range(NB):
                    n = (layer * NJ + j) * NB + s
                    span = counts[:, s, j * 512:(j + 1) * 512]
                    if n >= 2:
                        dve.wait_ge(rest_used, n - 1)
                    v.tensor_copy(cf_rest[:, n % 2, :], span).then_inc(rest_rounded, 1)
                    dve.wait_ge(rest_rounded, n + 1)
                    v.tensor_tensor(cf_rest[:, n % 2, :], span, cf_rest[:, n % 2, :].bitcast(F32),
                                    ALU.subtract).then_inc(rest_ready, 1)

            def count_tiles(layer, j, s0, s1):
                for s in range(s0, s1):
                    n = (layer * NJ + j) * NB + s
                    if s == NB - 1:
                        with dve.If(n_over > 0):
                            rest_tiles(layer, j)
                    if n >= 3:
                        dve.wait_ge(cf_used, n - 2)
                    v.tensor_copy(cf[:, n % 3, :], counts[:, s, j * 512:(j + 1) * 512]).then_inc(cf_ready, 1)

            for j in range(NJ):
                count_tiles(0, j, 0, NB)

            dve.wait_ge(gnnw_in, 112)
            for b in range(NB):
                if b % GB == 0:
                    dve.wait_ge(x_again[b // GB], 16)
                dve.wait_ge(out_ps, b + 1)
                v.tensor_tensor(out_t[:, b % 2, :], ps[:, b % 4, :], row_bias[:], ALU.add).then_inc(out_read, 1)
                dve.wait_ge(out_read, b + 1)
                last = v.scalar_tensor_tensor(out=x_sb[:, b, :], in0=out_t[:, b % 2, :], scalar=0.0,
                                              in1=x_sb[:, b, :], op0=ALU.max, op1=ALU.add)
            link(last)
            for g in range(XG):
                normalise(g * GB, (g + 1) * GB)

            dve.wait_ge(router_ps, 1)
            link(v.tensor_copy(logits[:].rearrange("p b e -> p (b e)"), ps[:, 0, 0:NB * NE]))
            for b in range(NB):
                last = v.max(top_v[:, b, :], logits[:, b, :])
            link(last)
            for b in range(NB):
                last = v.max_index(top_i[:, b, :], top_v[:, b, :], logits[:, b, :])
            v.tensor_tensor(gate_d[:], top_v[:, :, 1], top_v[:, :, 0], ALU.subtract).then_inc(gate_diff, 1)
            link(last)
            for k in range(TOPK):
                last = v.tensor_copy(top_f[:, k, :], top_i[:, :, k])
            link(last)
            for k in range(TOPK):
                last = v.tensor_tensor(sel[:, k], iota_f[:, 0:NE].unsqueeze(1).to_broadcast([P, NB, NE]),
                                       top_f[:, k, :].unsqueeze(2).to_broadcast([P, NB, NE]), ALU.is_equal)
            link(last)
            v.tensor_tensor(sel_bf[:, (NB - 1) * NE:].rearrange("p (b e) -> p b e", e=NE), sel[:, 0], sel[:, 1],
                            ALU.add).then_inc(sel_ready, 1)
            dve.wait_ge(gate_exp, 1)
            link(v.tensor_scalar(gate_d[:], gate_e[:], 1.0, None, ALU.add))
            link(v.reciprocal(gates[:, 0, :], gate_d[:]))
            link(v.tensor_tensor(gates[:, 1, :], gates[:, 0, :], gate_e[:], ALU.mult))
            for k in range(TOPK):
                last = v.tensor_tensor(gate_w[:, k], sel[:, k], gates[:, k, :].unsqueeze(2).to_broadcast([P, NB, NE]),
                                       ALU.mult)
            link(last)
            v.tensor_tensor(gate_w[:, 0], gate_w[:, 0], gate_w[:, 1], ALU.add).then_inc(gatew_ready, 1)

            dve.wait_ge(pos_ps, 1)
            link(v.tensor_scalar(cnt_i[:], ps[:, 2, 0:NE], float(P - 1), None, ALU.add))
            link(v.tensor_scalar(cnt_i[:], cnt_i[:], 7, 7, ALU.logical_shift_right, ALU.logical_shift_left))
            link(v.tensor_copy(cnt_f[:], cnt_i[:]))
            link(v.tensor_tensor_scan(end_f[:], one_f[:], cnt_f[:], 0.0, ALU.mult, ALU.add))
            link(v.tensor_tensor(off_f[:], end_f[:], cnt_f[:], ALU.subtract))
            link(v.tensor_tensor(pos[:], ps[:, 1, 0:NB * NE].rearrange("p (b e) -> p b e", e=NE),
                                 off_f[:].unsqueeze(1).to_broadcast([P, NB, NE]), ALU.add))
            for k in range(TOPK):
                link(v.tensor_tensor(pos_t[:], sel[:, k], pos[:], ALU.mult))
                link(v.tensor_reduce(slot_f[:, k, :], pos_t[:], AX_X, ALU.add))
            link(v.tensor_copy(slot_i[:], slot_f[:]))
            v.tensor_scalar(slot_hi[:], slot_i[:], 7, None, ALU.logical_shift_right)
            link(v.tensor_scalar(slot_lo[:], slot_i[:], P - 1, None, ALU.bitwise_and))
            v.tensor_copy(slot_hf[:], slot_hi[:])
            link(v.tensor_copy(slot_lf[:], slot_lo[:]))
            link(v.tensor_scalar(chunk_ef[:], iota_f[:, 0:SW], float(P), None, ALU.mult))
            link(v.tensor_tensor(chunk_ge, chunk_ef[:].unsqueeze(2).to_broadcast([P, SW, NE]),
                                 end_f[:].unsqueeze(1).to_broadcast([P, SW, NE]), ALU.is_ge))
            link(v.tensor_reduce(chunk_ef[:], chunk_ge, AX_X, ALU.add))
            v.tensor_scalar(chunk_e[:], chunk_ef[:], float(NE - 1), None, ALU.min).then_inc(tok_ready, 1)
            for b in range(NB):
                for k in range(TOPK):
                    n = b * TOPK + k
                    if n >= 2:
                        dve.wait_ge(slot_ps, n - 1)
                    v.tensor_scalar(lo_oh[:, n % 2, :], iota_f[:], slot_lf[:, k, b:b + 1], None, ALU.is_equal)
                    v.tensor_scalar(hi_oh[:, n % 2, 0:SW], iota_f[:, 0:SW], slot_hf[:, k, b:b + 1], iota_p[:, 0:1],
                                    ALU.is_equal, ALU.mult)
                    v.tensor_scalar(hi_oh[:, n % 2, SW:2 * SW], iota_f[:, 0:SW], slot_hf[:, k, b:b + 1],
                                    block_col[:, b:b + 1], ALU.is_equal, ALU.mult).then_inc(slot_oh, 1)
            dve.wait_ge(slot_ps, TOPK * NB)
            link(v.tensor_scalar(tok_f[:], ps[:, 3, SW:2 * SW], float(P), None, ALU.mult))
            link(v.tensor_tensor(tok_f[:], tok_f[:], ps[:, 3, 0:SW], ALU.add))
            v.tensor_copy(tok[:], tok_f[:]).then_inc(tok_ready, 1)
            for b in range(NB):
                dve.wait_ge(beta_ps, b + 1)
                v.tensor_tensor(x_sb[:, b, :], x_sb[:, b, :], ps[:, 4 + b % 2, :], ALU.add).then_inc(beta_read, 1)

            def hidden_bias(j, b, free):
                e = dve.value_load(chunk_e[0:1, bass.ds(j, 1)], min_val=0, max_val=NE - 1)
                dve.wait_ge(hid_ps, j + 1)
                if free is not None:
                    dve.wait_ge(hidT_ps, free)
                v.tensor_tensor(hb[:, b, :], ps[:, b, 0:F], b1_row[:, bass.ds(e * F, F)], ALU.add).then_inc(hid_sb, 1)

            def residual(j, b):
                dve.wait_ge(y_ps, j + 1)
                dve.wait_ge(xb_ready, j + 1)
                v.tensor_tensor(yt[:, b, :], ps[:, 2 + b, :], xb[:, b, :], ALU.add).then_inc(yt_ready, 1)
                dve.wait_ge(yt_ready, j + 1)
                v.bn_stats(e_stats[:, b, :], yt[:, b, :]).then_inc(es_ready, 1)
                dve.wait_ge(es_ready, j + 1)
                v.memset(nt_b[:, 0:1], 0.0)
                v.bn_aggr(e_mv[:, b, 0:2], e_stats[:, b, :]).then_inc(em_ready, 1)
                dve.wait_ge(em_ready, j + 1)
                v.tensor_scalar(e_mv[:, b, 2:3], e_mv[:, b, 1:2], EXPERT_EPS, None, ALU.add).then_inc(yv_ready, 1)

            def scaled(j, b, half):
                dve.wait_ge(sd_ready, j + 1)
                v.reciprocal(e_mv[:, b, 4:5], e_mv[:, b, 3:4]).then_inc(er_ready, 1)
                dve.wait_ge(er_ready, 4 * j + 1)
                v.scalar_tensor_tensor(out=e_mv[:, b, 5:6], in0=e_mv[:, b, 4:5], scalar=e_mv[:, b, 4:5],
                                       in1=e_mv[:, b, 2:3], op0=ALU.mult, op1=ALU.mult).then_inc(er_ready, 1)
                dve.wait_ge(er_ready, 4 * j + 2)
                v.tensor_scalar(e_mv[:, b, 6:7], e_mv[:, b, 5:6], -0.5, 1.5, ALU.mult, ALU.add).then_inc(er_ready, 1)
                dve.wait_ge(er_ready, 4 * j + 3)
                v.tensor_tensor(e_mv[:, b, 7:8], e_mv[:, b, 6:7], e_mv[:, b, 4:5], ALU.mult).then_inc(er_ready, 1)
                dve.wait_ge(er_ready, 4 * j + 4)
                if half is not None:
                    dve.wait_ge(y_out[b], 16 * half)
                v.tensor_scalar(yu[:, b, :], yt[:, b, :], e_mv[:, b, 0:1], e_mv[:, b, 7:8],
                                ALU.subtract, ALU.mult).then_inc(yu_ready, 1)

            dve.wait_ge(ffn_rows_in, 48)
            hidden_bias(0, 0, None)
            hidden_bias(1, 1, None)
            residual(0, 0)
            hidden_bias(2, 0, 1)
            scaled(0, 0, None)
            residual(1, 1)
            hidden_bias(3, 1, 2)
            scaled(1, 1, None)
            residual(2, 0)
            with dve.Fori(0, (NCH - 5) // 2) as i:
                for u in range(2):
                    hidden_bias(2 * i + (4 + u), u, 2 * i + (3 + u))
                    scaled(2 * i + (2 + u), u, i + 1)
                    residual(2 * i + (3 + u), 1 - u)
            hidden_bias(NCH - 1, 0, NCH - 2)
            scaled(NCH - 3, 0, (NCH - 3) // 2)
            residual(NCH - 2, 1)
            scaled(NCH - 2, 1, (NCH - 2) // 2)
            residual(NCH - 1, 0)
            scaled(NCH - 1, 0, (NCH - 1) // 2)

            for b in range(NB):
                dve.wait_ge(y_top_in[b], 16 * TOPK)
                for k in range(TOPK):
                    link(v.scalar_tensor_tensor(out=x_sb[:, b, :], in0=y_top[:, k, b, :], scalar=gates[:, k, b:b + 1],
                                                in1=x_sb[:, b, :], op0=ALU.mult, op1=ALU.add))

            for g in range(XG):
                normalise(g * GB, (g + 1) * GB, xn3)

            v.tensor_copy(ones_r, ones_bf[:]).then_inc(ones_r_ready, 1)

            def mean_span(j):
                dve.wait_ge(cf_used, (NJ + j + 1) * NB)
                link(v.tensor_scalar(deg_inv, ps[:, 6 + j % 2, :], 1.0, None, ALU.max))
                v.reciprocal(deg_inv, deg_inv).then_inc(deg_read, 1)
                dve.wait_ge(deg_read, j + 1)
                for m in range(DC):
                    t = (NJ + j) * DC + m
                    dve.wait_ge(agg_ps, t + 1)
                    v.tensor_tensor(hT[:, m, j * 512:(j + 1) * 512], ps[:, (j * DC + m) % 6, :], deg_inv,
                                    ALU.mult).then_inc(agg_sb, 1)

            for j in range(NJ):
                count_tiles(1, j, 0, 3)
                if j >= 1:
                    mean_span(j - 1)
                count_tiles(1, j, 3, NB)
            mean_span(NJ - 1)
            dve.wait_ge(l1w_in, 64)
            for b in range(NB):
                dve.wait_ge(l1_ps, b + 1)
                v.tensor_tensor(xn[:, b, :], ps[:, b % 8, :], row_bias[:], ALU.add).then_inc(l1_read, 1)
                dve.wait_ge(l1_read, b + 1)
                v.bn_stats(stats[:, b, :], xn[:, b, :])
            link(v.memset(nt_b[:], 0.0))
            row_scales(0, NB)
            for b in range(NB):
                link(v.tensor_scalar(h_t, xn[:, b, :], mv[:, b, 0:1], rstd[:, b:b + 1], ALU.subtract, ALU.mult))
                link(v.tensor_tensor(h_t, h_t, l1g_row, ALU.mult))
                link(v.tensor_tensor(h_t, h_t, l1b_row, ALU.add))
                link(v.scalar_tensor_tensor(out=x_sb[:, b, :], in0=h_t, scalar=0.0, in1=x_sb[:, b, :],
                                            op0=ALU.max, op1=ALU.add))
            for g in range(XG):
                normalise(g * GB, (g + 1) * GB)
            dve.wait_ge(xn_ready, 4 * NB)

            link(v.tensor_scalar(hot, xn[:, :, 64:112], 0.5, None, ALU.is_gt))
            link(v.tensor_tensor(hot.rearrange("p b (g i) -> p (b g) i", i=16),
                                 hot.rearrange("p b (g i) -> p (b g) i", i=16),
                                 first_key[:].unsqueeze(1).to_broadcast([P, NB * 3, 16]), ALU.mult))
            nib_f = nib.rearrange("p b c -> p (b c)")
            nib_pf = nib_pos.rearrange("p b c -> p (b c)")
            link(v.tensor_reduce(nib_f, hot.rearrange("p b (g i) -> p (b g) i", i=16), AX_X, ALU.max))
            link(v.tensor_scalar(nib_pf, nib_f, 0.0, None, ALU.is_gt))
            link(v.tensor_scalar(nib_f, nib_f, -1.0, 16.0, ALU.mult, ALU.add))
            link(v.tensor_tensor(nib_f, nib_f, nib_pf, ALU.mult))
            v.tensor_scalar(mark, xn[:, :, 0], 0.5, None, ALU.is_gt)
            v.tensor_scalar(is_shl, xn[:, :, 39], 0.5, None, ALU.is_gt)
            link(v.tensor_scalar(is_shr, xn[:, :, 40], 0.5, None, ALU.is_gt))
            link(v.scalar_tensor_tensor(out=val_f, in0=nib[:, :, 1], scalar=16.0, in1=nib[:, :, 0],
                                        op0=ALU.mult, op1=ALU.add))
            v.tensor_copy(val_i, val_f)
            link(v.tensor_copy(sa_i, nib[:, :, 2]))
            v.tensor_tensor(shl_i, val_i, sa_i, ALU.logical_shift_left)
            link(v.tensor_tensor(shr_i, val_i, sa_i, ALU.logical_shift_right))
            link(v.tensor_scalar(shl_i, shl_i, 255, None, ALU.bitwise_and))
            v.tensor_copy(shl_f, shl_i)
            v.tensor_copy(shr_f, shr_i)
            link(v.tensor_scalar(not_shl, is_shl, -1.0, 1.0, ALU.mult, ALU.add))
            link(v.tensor_tensor(is_shr, is_shr, not_shl, ALU.mult))
            v.tensor_tensor(is_shl, is_shl, mark, ALU.mult)
            link(v.tensor_tensor(is_shr, is_shr, mark, ALU.mult))
            v.tensor_tensor(shl_f, shl_f, is_shl, ALU.mult)
            v.tensor_tensor(shr_f, shr_f, is_shr, ALU.mult)
            link(v.tensor_tensor(amp, is_shl, is_shr, ALU.add))
            v.tensor_scalar(amp, amp, 2.0, None, ALU.mult)
            link(v.tensor_tensor(val_f, shl_f, shr_f, ALU.add))
            link(v.tensor_scalar(val_f, val_f, 0.0, 255.0, ALU.max, ALU.min))
            link(v.tensor_copy(res_i, val_f))
            v.tensor_scalar(out_ni[:, :, 0], res_i, 15, None, ALU.bitwise_and)
            link(v.tensor_scalar(out_ni[:, :, 1], res_i, 4, None, ALU.logical_shift_right))
            link(v.tensor_copy(out_nf, out_ni))
            for k in range(2):
                last = v.tensor_tensor(out_oh[:, :, k, :], iota_f[:, 0:16].unsqueeze(1).to_broadcast([P, NB, 16]),
                                       out_nf[:, :, k].unsqueeze(2).to_broadcast([P, NB, 16]), ALU.is_equal)
            link(last)
            oh = out_oh.rearrange("p b k i -> p b (k i)")
            link(v.tensor_tensor(oh, oh, amp.unsqueeze(2).to_broadcast([P, NB, 32]), ALU.mult))
            link(v.tensor_tensor(xn[:, :, 128:160], xn[:, :, 128:160], oh, ALU.add))
            for b in range(NB):
                v.tensor_tensor(x_sb[:, b, :], x_sb[:, b, :], xn[:, b, :], ALU.add).then_inc(fin_ready, 1)


_OUTS = [((1536, 512), 'float32')]


def kernel(**inputs):
    import numpy as np
    import concourse.bacc as bacc
    from concourse import mybir as mb
    from concourse.bass_utils import run_bass_kernel_spmd as run

    def cols(a):
        return np.asarray(a).reshape(-1, 128).T

    g = {k: np.asarray(v) for k, v in inputs.items()}
    img0 = g['L0_gnn_img_feats'][0]
    laid = {
        'x': g['x'],
        'src': g['src'].reshape(-1, 128).T, 'dst': g['dst'].reshape(-1, 128).T,
        'img': img0.T.reshape(-1, 128, img0.shape[0]).transpose(1, 0, 2),
        'wf': g['L0_gnn_Wf'], 'bf': cols(g['L0_gnn_bf']), 'wi': g['L0_gnn_Wi'], 'bi': cols(g['L0_gnn_bi']),
        'wa': cols(g['L0_gnn_Wa']), 'ba': g['L0_gnn_ba'],
        'wn': g['L0_gnn_Wn'], 'bn': cols(g['L0_gnn_bn']),
        'wim': g['L0_gnn_Wim'], 'bim': cols(g['L0_gnn_bim']),
        'wap': g['L0_gnn_Wap'], 'bap': g['L0_gnn_bap'],
        'router': g['L0_ffn_router_w'], 'w1': g['L0_ffn_w1'], 'b1': g['L0_ffn_b1'].reshape(-1),
        'w2': g['L0_ffn_w2'], 'b2': g['L0_ffn_b2'].reshape(-1),
        'ffn_gamma': g['L0_ffn_gamma'].reshape(-1), 'ffn_beta': g['L0_ffn_beta'],
        'w_self': g['L1_gnn_w_self'].T, 'w_neigh': g['L1_gnn_w_neigh'].T,
        'l1_bias': g['L1_gnn_bias'], 'l1_gamma': g['L1_gnn_gamma'], 'l1_beta': g['L1_gnn_beta'],
    }
    nc = bacc.Bacc("TRN2", target_bir_lowering=False, num_devices=1)
    arrays, args = {}, []
    for name, a in laid.items():
        a = np.ascontiguousarray(a)
        arrays[f"in_{name}_dram"] = a
        args.append(nc.dram_tensor(f"in_{name}_dram", a.shape, mb.dt.from_np(a.dtype), kind="ExternalInput").ap())
    for i, (shape, dtype) in enumerate(_OUTS):
        dt = mb.dt.from_np(np.dtype(dtype))
        args.append(nc.dram_tensor(f"out_{i}_dram", shape, dt, kind="ExternalOutput").ap())
    args.append(nc.dram_tensor("tokens_dram", (1536, 512), mb.dt.float32, kind="Internal").ap())
    args.append(nc.dram_tensor("expert_rows_dram", (31 * 128, 512), mb.dt.float32, kind="Internal").ap())
    gnn_moe_kernel(nc, *args)
    r = run(nc, [arrays], core_ids=[0])
    return r.results[0]["out_0_dram"]
```

```python
from contextlib import ExitStack

import concourse.bass as bass
from concourse import mybir

ALU = mybir.AluOpType
ACT = mybir.ActivationFunctionType
F32 = mybir.dt.float32
F32R = mybir.dt.float32r
BF16 = mybir.dt.bfloat16
I32 = mybir.dt.int32
U32 = mybir.dt.uint32
U16 = mybir.dt.uint16
I16 = mybir.dt.int16
AX_X = mybir.AxisListType.X

P = 128
RSQRT_MAGIC = 1597463007.0
TOPK = 2
EXACT = 4096
GNN_EPS = 1e-5
EXPERT_EPS = 1e-6


def gnn_moe_kernel(nc, x, src, dst, img, wf, bf, wi, bi, wa, ba, wn, bn, wim, bim, wap, bap,
                   router, w1, b1, w2, b2, ffn_gamma, ffn_beta,
                   w_self, w_neigh, l1_bias, l1_gamma, l1_beta, out, xf_dram, y_dram):
    N, D = x.shape
    NB = N // P
    DC = D // P
    NJ = N // 512
    JB = 512 // P
    EC = src.shape[1]
    KI, R = img.shape[1], img.shape[2]
    PJ = wf.shape[1]
    PC = PJ // P
    NE, F = w1.shape[0], w1.shape[2]
    FC = F // P
    NCH = (N * TOPK + NE * (P - 1)) // P
    SW = 32
    LOGIT_BANKS = (0, 1, 6)
    DEG_BANKS = (5, 7, 6)
    L1_BANKS = (0, 1, 7, 2, 3, 4, 5, 6)
    GC = 4
    EG = EC // GC
    WIN = 24
    XG = NJ
    GB = NB // XG
    GROUPS = ((0, 3), (3, 6), (6, 9), (9, 11), (11, 12))
    L3_GROUPS = ((0, 3), (3, 6), (6, 9), (9, 12))
    L1_GROUPS = ((0, 3), (3, 6), (6, 9), (9, 12))
    ALU_GROUPS = ((0, 6), (6, 12))
    assert 3 * EG == 8 * R and R % 3 == 0 and PC == 2 and NCH <= SW and D == 512 and NJ == 3 and NCH == 31

    with ExitStack() as ctx:
        def sb(name, shape, dt=F32):
            return ctx.enter_context(nc.sbuf_tensor(name, shape, dt))

        def sem(name):
            return ctx.enter_context(nc.semaphore(name))

        ps = ctx.enter_context(nc.psum_tensor("ps", [P, 8, 512], F32))

        AX = 0
        AW = AX + NB * D
        AH = AW + NE * DC * F
        AT = AH + NB * D
        AN = AT + NB * D

        def beneath(name, start, size):
            with ExitStack() as place:
                if start:
                    place.enter_context(nc.sbuf_tensor(name + "_before", [P, start], F32))
                return place.enter_context(nc.sbuf_tensor(name, [P, size], F32R))

        rows_hi = beneath("rows_hi", AN, NB * D)[:].rearrange("p (b d) -> p b d", b=NB)
        rows_lo = [beneath(f"rows_lo{k}", a, NB * D)[:].rearrange("p (b d) -> p b d", b=NB)
                   for k, a in enumerate((AX, AW))]
        arena = sb("arena", [P, 4 * NB * D + NE * DC * F])

        def at(start, size):
            return arena[:, start:start + size]

        x_sb = at(AX, NB * D).rearrange("p (b d) -> p b d", b=NB)
        xn = at(AN, NB * D).rearrange("p (b d) -> p b d", b=NB)
        xT = at(AT, NB * D).rearrange("p (c n) -> p c n", c=DC)
        hT = at(AH, NB * D).rearrange("p (c n) -> p c n", c=DC)
        node_proj = at(AX, PC * N).rearrange("p (m n) -> p m n", m=PC)
        tanh_t = [at(AX + PC * N, PC * N).rearrange("p (m n) -> p m n", m=PC)] + [
            at(AN + k * PC * N, PC * N).rearrange("p (m n) -> p m n", m=PC) for k in range(2)]
        wi_sb = at(AH, KI * PJ).rearrange("p (k n) -> p k n", k=KI)
        wim_sb = at(AH + KI * PJ, KI * D).rearrange("p (k n) -> p k n", k=KI)
        wf_sb = at(AW, DC * PJ).rearrange("p (k n) -> p k n", k=DC)
        wn_sb = at(AW + DC * PJ, DC * D).rearrange("p (k n) -> p k n", k=DC)
        wap_sb = at(AW + DC * (PJ + D), 2 * DC * D).rearrange("p (k n) -> p k n", k=2 * DC)
        w1_sb = at(AW, NE * DC * F)
        w2_sb = at(AH, NE * FC * D)
        w1_cut = DC * (PJ + D) // (DC * F)
        w2_cut = NB * D // (FC * D)
        b1_row = at(AH + NE * FC * D, NE * F)
        b2_row = at(AH + NE * FC * D + NE * F, NE * D)
        gamma_row = at(AH + NE * FC * D + NE * F + NE * D, NE * D)
        y_top = [at(a, NB * D).rearrange("p (b d) -> p b d", b=NB) for a in (AH, AN)]
        ws_sb = at(AW + NB * D, DC * D).rearrange("p (k n) -> p k n", k=DC)
        wg_sb = at(AW, DC * D).rearrange("p (k n) -> p k n", k=DC)
        xn3 = at(AW, NB * D).rearrange("p (b d) -> p b d", b=NB)
        assert NB * D + DC * D <= NE * DC * F
        assert AH + NE * FC * D + NE * F + 2 * NE * D <= AN + NB * D

        counts = sb("counts", [P, NB, N], U16)

        work_r = beneath("work_r", 0, 6656)
        work = sb("work", [P, 6656])
        dst_f = work[:, 480:480 + EC]
        src_k = work[:, 864:864 + EC]
        src_i = work[:, 1248:1248 + EC].bitcast(I32)
        dst_i = work[:, 1632:1632 + EC].bitcast(I32)
        oh_dst = work[:, 2016:2016 + N].bitcast(BF16).rearrange("p (b n) -> p b n", b=2)
        oh_src = work[:, 3552:3552 + 2 * P].bitcast(BF16).rearrange("p (b n) -> p b n", b=2)
        iota_n = work[:, 3808:3808 + N // 2].bitcast(I16)
        edge_t = work[:, 2016:2016 + EC]
        edge_u = work[:, 2400:2400 + EC]
        OC = 2 * GC
        WW = NB * WIN

        def pair_rows(start, n):
            return at(start, n * OC // 2).bitcast(I16).rearrange("p (n c) -> p n c", c=OC)

        num_win = pair_rows(AH, WW)
        oh_win = [pair_rows(AH + (k + 1) * WW * OC // 2, WW).bitcast(BF16) for k in range(4)]
        oh_lo = [pair_rows((AW, AH - DC * PJ)[k // 2] + (k % 2) * P * OC // 2, P).bitcast(BF16) for k in range(4)]
        assert P * OC == DC * PJ and 5 * WW * OC // 2 <= NB * D and DC * (2 * PJ + 3 * D) <= NE * DC * F
        att = work[:, 0:NB * R].rearrange("p (b r) -> p b r", b=NB)
        region_col = work[:, 0:3 * R].rearrange("p (b r) -> p b r", b=3)
        logits_T = at(AN, N)
        att_red = work[:, 448:448 + NB]
        att_inv = work[:, 464:464 + NB]
        attT = work[:, 512:512 + N]
        out_t = work[:, 2048:2048 + 2 * D].rearrange("p (b d) -> p b d", b=2)
        gate_T = work_r[:, 2048:2048 + N]
        xs = work[:, 0:1024].rearrange("p (b d) -> p b d", b=2)
        xb = work[:, 1024:2048].rearrange("p (b d) -> p b d", b=2)
        xsT = work[:, 2048:3072].rearrange("p (b c n) -> p b c n", b=2, c=DC)
        hb = work[:, 3072:3072 + 2 * F].rearrange("p (b f) -> p b f", b=2)
        hbT = work[:, 3584:3584 + 2 * F].rearrange("p (b c n) -> p b c n", b=2, c=FC)
        yt = work[:, 4096:5120].rearrange("p (b d) -> p b d", b=2)
        yu = work[:, 5120:6144].rearrange("p (b d) -> p b d", b=2)
        l1g_row = work[:, 0:D]
        l1b_row = work[:, D:2 * D]
        deg_inv = work[:, 3 * D:4 * D]
        hot = work[:, 3072:3072 + NB * 48].rearrange("p (b c) -> p b c", b=NB)
        nib = work[:, 3712:3712 + NB * 3].rearrange("p (b c) -> p b c", b=NB)
        nib_none = work[:, 3776:3776 + NB * 3].rearrange("p (b c) -> p b c", b=NB)
        mark = work[:, 3840:3840 + NB]
        is_op = work[:, 3856:3856 + 2 * NB].rearrange("p (b k) -> p b k", b=NB)
        val_f = work[:, 3904:3904 + NB]
        val_i = work[:, 3920:3920 + NB].bitcast(I32)
        sa_i = work[:, 3936:3936 + NB].bitcast(I32)
        shl_i = work[:, 3952:3952 + NB].bitcast(I32)
        shr_i = work[:, 3968:3968 + NB].bitcast(I32)
        shl_f = work[:, 3984:3984 + NB]
        shr_f = work[:, 4000:4000 + NB]
        res_i = work[:, 4016:4016 + NB].bitcast(I32)
        out_ni = work[:, 4032:4032 + 2 * NB].rearrange("p (b k) -> p b k", b=NB).bitcast(I32)
        out_oh = work[:, 4096:4096 + NB * 32].rearrange("p (b k i) -> p b k i", b=NB, k=2)
        amp = work[:, 4480:4480 + NB]

        ident = sb("ident", [P, P])
        ones_bf = sb("ones_bf", [P, P], BF16)
        before_bf = sb("before_bf", [P, P], BF16)
        row0 = work[:, 128:128 + P]
        lo_16 = sb("lo_16", [P, EC], I16)
        win_16 = sb("win_16", [P, EC], I16)
        base_f = sb("base_f", [P, EG])
        base_i = sb("base_i", [P, EG], I32)
        outside = sb("outside", [P, 2])
        outside_bf = sb("outside_bf", [P, 1], BF16)
        loose = sb("loose", [P, 1], I32)
        iota_i = sb("iota_i", [P, P], I32)
        iota_f = sb("iota_f", [P, P])
        iota_pi = sb("iota_pi", [P, 1], I32)
        iota_p = sb("iota_p", [P, 1])
        key_i = sb("key_i", [P, 16], I32)
        first_key = sb("first_key", [P, 16])
        block_col = sb("block_col", [P, NB])
        img_sb = sb("img_sb", [P, KI, R])
        bfi = sb("bfi", [P, 2, PC])
        bfi_sum = sb("bfi_sum", [P, PC])
        wa_sb = sb("wa_sb", [P, PC])
        ba_sb = sb("ba_sb", [P, 1])
        bn_sb = sb("bn_sb", [P, DC])
        bim_sb = sb("bim_sb", [P, DC])
        row_bias = sb("row_bias", [P, D])
        img_bias = sb("img_bias", [P, PC, R])
        img_ctx = work[:, 4608:4608 + D]
        stats = sb("stats", [P, NB, 6])
        mv = sb("mv", [P, NB, 2])
        var_e = sb("var_e", [P, NB])
        rstd = sb("rstd", [P, NB])
        shift = sb("shift", [P, NB])
        nt_a = sb("nt_a", [P, NB])
        nt_b = sb("nt_b", [P, NB])
        cf = work_r[:, 5120:6656].rearrange("p (b n) -> p b n", b=3)
        cf_rest = work_r[:, 3072:4096].rearrange("p (b n) -> p b n", b=2)
        count_max = sb("count_max", [P, 1])
        over_bf = sb("over_bf", [P, 1], BF16)
        over = sb("over", [P, 1], I32)
        ones_r = work_r[:, 2 * D:2 * D + P]

        rw_sb = sb("rw_sb", [P, DC, NE])
        logits = sb("logits", [P, NB, NE])
        top_v = sb("top_v", [P, NB, 8])
        top_i = sb("top_i", [P, NB, 8], U32)
        top_f = sb("top_f", [P, TOPK, NB])
        gate_d = sb("gate_d", [P, NB])
        gate_e = sb("gate_e", [P, NB])
        gates = sb("gates", [P, TOPK, NB])
        sel = sb("sel", [P, TOPK, NB, NE])
        sel_bf = sb("sel_bf", [P, (2 * NB - 1) * NE], BF16)
        gate_w = sb("gate_w", [P, 2, NB, NE])
        gate_r = work_r[:, 3584:3584 + NB * 4 * NE].rearrange("p (b k e) -> p b k e", b=NB, k=4)
        beta_sb = sb("beta_sb", [4 * NE, D])
        beta_r = sb("beta_r", [4 * NE, D], F32R)
        odd_part = work[:, 4496:4498]
        odd_i = work[:, 4498:4499].bitcast(I32)
        pos = work[:, 5216:5216 + NB * NE].rearrange("p (b e) -> p b e", b=NB)
        pos_t = work[:, 5120:5120 + NB * NE].rearrange("p (b e) -> p b e", b=NB)
        cnt_i = sb("cnt_i", [P, NE], I32)
        cnt_f = sb("cnt_f", [P, NE])
        end_f = sb("end_f", [P, NE])
        off_f = sb("off_f", [P, NE])
        one_f = sb("one_f", [P, NE])
        slot_f = sb("slot_f", [P, TOPK, NB])
        slot_i = sb("slot_i", [P, TOPK, NB], I32)
        slot_hi = sb("slot_hi", [P, TOPK, NB], I32)
        slot_lo = sb("slot_lo", [P, TOPK, NB], I32)
        lo_oh = work[:, 2560:2560 + NB * P].bitcast(BF16).rearrange("p (k b n) -> p k b n", k=TOPK, b=NB)
        hi_oh = work[:, 4096:4096 + NB * 2 * SW].bitcast(BF16).rearrange("p (k b n) -> p k b n", k=TOPK, b=NB)
        iota_b = work[:, 4864:4864 + P // 2].bitcast(BF16)
        slot_lb = work[:, 4928:4928 + NB].bitcast(BF16).rearrange("p (k b) -> p k b", k=TOPK)
        slot_hb = work[:, 4944:4944 + NB].bitcast(BF16).rearrange("p (k b) -> p k b", k=TOPK)
        block_b = work[:, 4960:4960 + NB // 2].bitcast(BF16)
        chunk_ge = work[:, 2048:2048 + SW * NE].rearrange("p (c e) -> p c e", e=NE)
        chunk_ef = sb("chunk_ef", [P, SW])
        chunk_e = sb("chunk_e", [P, SW], I32)
        tok_f = sb("tok_f", [P, SW])
        tok = sb("tok", [P, SW], U32)
        e_mv = sb("e_mv", [P, 2, 8])
        e_stats = sb("e_stats", [P, 2, 6])

        x_in = [sem(f"x_in{g}") for g in range(XG)]
        edges_in = sem("edges_in")
        img_in = sem("img_in")
        wim_in = sem("wim_in")
        attw_in = sem("attw_in")
        gnnw_in = sem("gnnw_in")
        x_again = [sem(f"x_again{g}") for g in range(XG)]
        w1_in = sem("w1_in")
        w2_in = sem("w2_in")
        ffn_rows_in = sem("ffn_rows_in")
        l1w_in = sem("l1w_in")
        xf_out = sem("xf_out")
        consts_ready = sem("consts_ready")
        pool_order = sem("pool_order")
        dve_order = sem("dve_order")
        edge_oh = sem("edge_oh")
        edge_oh_used = sem("edge_oh_used")
        pass_out = sem("pass_out")
        src_k_ready = sem("src_k_ready")
        edges_f = sem("edges_f")
        base_ps = sem("base_ps")
        outside_ready = sem("outside_ready")
        outside_ps = sem("outside_ps")
        loose_ready = sem("loose_ready")
        win_oh = sem("win_oh")
        win_ps = sem("win_ps")
        num_ready = sem("num_ready")
        win_bank_free = sem("win_bank_free")
        counts_zero = sem("counts_zero")
        counts_ready = sem("counts_ready")
        scales_ready = sem("scales_ready")
        var_ready = sem("var_ready")
        root_ready = sem("root_ready")
        xn_ready = sem("xn_ready")
        tr_ps = sem("tr_ps")
        tr_sb = sem("tr_sb")
        img_ps = sem("img_ps")
        img_bias_ready = sem("img_bias_ready")
        img_ctx_ready = sem("img_ctx_ready")
        proj_ps = sem("proj_ps")
        proj_sb = sem("proj_sb")
        tanh_sb = sem("tanh_sb")
        scaled_sb = sem("scaled_sb")
        sum_ready = sem("sum_ready")
        third_scaled = sem("third_scaled")
        third_ready = sem("third_ready")
        att_ps = sem("att_ps")
        logits_zero = sem("logits_zero")
        logits_sb = sem("logits_sb")
        logits_turned = sem("logits_turned")
        att_shift = sem("att_shift")
        att_exp = sem("att_exp")
        att_ready = sem("att_ready")
        h1_ps = sem("h1_ps")
        h1_sb = sem("h1_sb")
        cf_ready = sem("cf_ready")
        cf_used = sem("cf_used")
        rest_rounded = sem("rest_rounded")
        rest_ready = sem("rest_ready")
        rest_used = sem("rest_used")
        ones_r_ready = sem("ones_r_ready")
        over_flag = sem("over_flag")
        over_ps = sem("over_ps")
        over_ready = sem("over_ready")
        lo_ready = sem("lo_ready")
        hi_ready = sem("hi_ready")
        deg_read = sem("deg_read")
        mean_ready = sem("mean_ready")
        wg_in = sem("wg_in")
        agg_ps = sem("agg_ps")
        agg_sb = sem("agg_sb")
        out_ps = sem("out_ps")
        out_read = sem("out_read")
        router_ps = sem("router_ps")
        gate_diff = sem("gate_diff")
        gate_exp = sem("gate_exp")
        sel_ready = sem("sel_ready")
        gatew_ready = sem("gatew_ready")
        pos_ps = sem("pos_ps")
        slot_oh = sem("slot_oh")
        slot_ps = sem("slot_ps")
        tok_ready = sem("tok_ready")
        beta_in = sem("beta_in")
        beta_ready = sem("beta_ready")
        beta_ps = sem("beta_ps")
        beta_read = sem("beta_read")
        xs_in = [sem(f"xs_in{i}") for i in range(2)]
        xs_ps = sem("xs_ps")
        xs_T = sem("xs_T")
        hid_ps = sem("hid_ps")
        hid_sb = sem("hid_sb")
        hidT_ps = sem("hidT_ps")
        hidT_sb = sem("hidT_sb")
        y_ps = sem("y_ps")
        xb_ready = sem("xb_ready")
        yt_ready = sem("yt_ready")
        sd_ready = sem("sd_ready")
        yu_ready = sem("yu_ready")
        yg_ready = sem("yg_ready")
        y_out = [sem(f"y_out{i}") for i in range(2)]
        y_top_in = [sem(f"y_top_in{b}") for b in range(NB)]
        yv_ready = sem("yv_ready")
        es_ready = sem("es_ready")
        em_ready = sem("em_ready")
        er_ready = sem("er_ready")
        l1_ps = sem("l1_ps")
        l1_read = sem("l1_read")
        hn_ready = sem("hn_ready")
        gamma_done = sem("gamma_done")
        beta_done = sem("beta_done")
        added = sem("added")
        fin_ready = sem("fin_ready")
        out_done = sem("out_done")

        TR_X, TR_H1, TR_ATT = 0, NB, 2 * NB
        TR_XF = TR_ATT + NJ
        TR_GATE = TR_XF + NB
        TR_X3 = TR_GATE + NJ

        xb_dram = x.rearrange("(b p) d -> p b d", p=P)
        out_dram = out.rearrange("(b p) d -> p b d", p=P)

        block = ctx.enter_context(nc.Block())

        @block.sync
        def _(sp):
            sp.dma_start(src_i, src).then_inc(edges_in, 16)
            sp.dma_start(dst_i, dst).then_inc(edges_in, 16)
            for g in range(XG):
                sp.dma_start(x_sb[:, g * GB:(g + 1) * GB, :], xb_dram[:, g * GB:(g + 1) * GB, :]).then_inc(x_in[g], 16)
            sp.dma_start(wf_sb, wf.rearrange("(k p) n -> p k n", p=P)).then_inc(attw_in, 16)
            sp.dma_start(wa_sb[:], wa).then_inc(attw_in, 16)
            sp.dma_start(ba_sb[:], ba.partition_broadcast(P)).then_inc(attw_in, 16)
            sp.dma_start(img_sb[:], img).then_inc(img_in, 16)
            sp.dma_start(bfi[:, 0, :], bf).then_inc(img_in, 16)
            sp.dma_start(bfi[:, 1, :], bi).then_inc(img_in, 16)
            sp.dma_start(wi_sb, wi.rearrange("(k p) n -> p k n", p=P)).then_inc(img_in, 16)
            sp.dma_start(wim_sb, wim.rearrange("(k p) n -> p k n", p=P)).then_inc(wim_in, 16)
            sp.dma_start(wn_sb, wn.rearrange("(k p) n -> p k n", p=P)).then_inc(gnnw_in, 16)
            sp.dma_start(wap_sb, wap.rearrange("(k p) n -> p k n", p=P)).then_inc(gnnw_in, 16)
            sp.dma_start(bn_sb[:], bn).then_inc(gnnw_in, 16)
            sp.dma_start(bim_sb[:], bim).then_inc(gnnw_in, 16)
            sp.dma_start(row_bias[:], bap.partition_broadcast(P)).then_inc(gnnw_in, 16)
            sp.dma_start(rw_sb[:], router.rearrange("(k p) n -> p k n", p=P)).then_inc(gnnw_in, 16)
            for k in range(4):
                sp.dma_start(beta_sb[k * NE:(k + 1) * NE, :], ffn_beta).then_inc(beta_in, 16)
            w1v = w1_sb.rearrange("p (e k f) -> p e k f", e=NE, k=DC)
            w1d = w1.rearrange("e (k p) f -> p e k f", p=P)
            w2v = w2_sb.rearrange("p (e k d) -> p e k d", e=NE, k=FC)
            w2d = w2.rearrange("e (k p) d -> p e k d", p=P)
            sp.wait_ge(h1_ps, DC * NJ)
            sp.dma_start(w1v[:, 0:w1_cut], w1d[:, 0:w1_cut]).then_inc(w1_in, 16)
            sp.dma_start(w1v[:, NE - 1:NE], w1d[:, NE - 1:NE]).then_inc(w1_in, 16)
            sp.wait_ge(agg_ps, DC * NJ)
            for g in range(XG):
                sp.dma_start(x_sb[:, g * GB:(g + 1) * GB, :], xb_dram[:, g * GB:(g + 1) * GB, :]).then_inc(
                    x_again[g], 16)

            xf_blocks = xf_dram.rearrange("(b p) d -> p b d", p=P)
            for g0, g1 in GROUPS:
                if g1 == GROUPS[3][1]:
                    sp.wait_ge(out_ps, NB)
                    sp.dma_start(w1v[:, w1_cut:NE - 1], w1d[:, w1_cut:NE - 1]).then_inc(w1_in, 16)
                    sp.dma_start(w2v[:, 0:w2_cut], w2d[:, 0:w2_cut]).then_inc(w2_in, 16)
                sp.wait_ge(xn_ready, NB + g1)
                sp.dma_start(xf_blocks[:, g0:g1, :], xn[:, g0:g1, :]).then_inc(xf_out, 16)
            sp.wait_ge(router_ps, 1)
            sp.dma_start(w2v[:, w2_cut:NE], w2d[:, w2_cut:NE]).then_inc(w2_in, 16)
            sp.dma_start(b1_row, b1.partition_broadcast(P)).then_inc(ffn_rows_in, 16)
            sp.wait_ge(xf_out, 16 * len(GROUPS))
            sp.dma_start(b2_row, b2.partition_broadcast(P)).then_inc(ffn_rows_in, 16)
            sp.dma_start(gamma_row, ffn_gamma.partition_broadcast(P)).then_inc(ffn_rows_in, 16)

            def store(j, b):
                sp.wait_ge(yg_ready, j + 1)
                sp.dma_start(y_dram[bass.ds(j * P, P), :], yu[:, b, :]).then_inc(y_out[b], 16)

            with sp.Fori(0, NCH - 1, 2) as j:
                store(j, 0)
                store(j + 1, 1)
            store(NCH - 1, 0)

            sp.wait_ge(hid_ps, NCH)
            sp.dma_start(ws_sb, w_self.rearrange("(k p) n -> p k n", p=P)).then_inc(l1w_in, 16)
            sp.dma_start(row_bias[:], l1_bias.partition_broadcast(P)).then_inc(l1w_in, 16)
            sp.wait_ge(xs_ps, NCH)
            sp.wait_ge(xb_ready, NCH)
            sp.dma_start(l1g_row, l1_gamma.partition_broadcast(P)).then_inc(l1w_in, 16)
            sp.dma_start(l1b_row, l1_beta.partition_broadcast(P)).then_inc(l1w_in, 16)
            sp.wait_ge(agg_ps, 2 * DC * NJ)
            sp.dma_start(wg_sb, w_neigh.rearrange("(k p) n -> p k n", p=P)).then_inc(wg_in, 16)
            for n, (a0, a1) in enumerate(ALU_GROUPS):
                sp.wait_ge(fin_ready, n + 1)
                sp.dma_start(out_dram[:, a0:a1, :], x_sb[:, a0:a1, :]).then_inc(out_done, 16)
            sp.wait_ge(out_done, 16 * len(ALU_GROUPS))
            for i in range(2):
                sp.wait_ge(y_out[i], 16 * ((NCH + 1 - i) // 2))

        @block.gpsimd
        def _(pool):
            pool.memset(ident[:], 0.0).then_inc(pool_order, 1)
            pool.memset(before_bf[:], 0.0).then_inc(pool_order, 1)
            pool.memset(row0, 0.0).then_inc(pool_order, 1)
            pool.wait_ge(pool_order, 3)
            pool.memset(row0[0:1, :], 1.0).then_inc(consts_ready, 1)
            pool.affine_select(out=ident[:], in_=ident[:], compare_op=ALU.not_equal, fill=1.0, base=0,
                               pattern=[[-1, P]], channel_multiplier=1).then_inc(consts_ready, 1)
            pool.affine_select(out=before_bf[:], in_=before_bf[:], compare_op=ALU.is_ge, fill=1.0, base=0,
                               pattern=[[-1, P]], channel_multiplier=1).then_inc(consts_ready, 1)
            pool.memset(ones_bf[:], 1.0).then_inc(consts_ready, 1)
            pool.memset(count_max[:], 0.0).then_inc(consts_ready, 1)
            pool.iota(iota_n, pattern=[[1, N]], base=0, channel_multiplier=0).then_inc(consts_ready, 1)
            pool.iota(iota_i[:], pattern=[[1, P]], base=0, channel_multiplier=0).then_inc(consts_ready, 1)
            pool.iota(key_i[:], pattern=[[-1, 16]], base=16, channel_multiplier=0).then_inc(consts_ready, 1)
            pool.iota(iota_pi[:], pattern=[[1, 1]], base=0, channel_multiplier=1).then_inc(consts_ready, 1)
            pool.memset(counts[:].rearrange("p b n -> p (b n)").bitcast(F32), 0.0).then_inc(counts_zero, 1)

            def sum_third(i):
                pool.wait_ge(scaled_sb, 3 * i + 3)
                pool.tensor_tensor(tanh_t[2][:, 1, :], tanh_t[2][:, 1, :], wa_sb[:, 1:2].to_broadcast([P, N]),
                                   ALU.mult).then_inc(third_scaled, 1)
                pool.wait_ge(third_scaled, i + 1)
                pool.tensor_tensor(tanh_t[2][:, 1, :], tanh_t[2][:, 1, :], tanh_t[2][:, 0, :],
                                   ALU.add).then_inc(third_ready, 1)

            with pool.Fori(0, R // 3) as i:
                sum_third(i)

            def gather(j):
                if j == 0:
                    pool.wait_ge(tok_ready, 2)
                    pool.wait_ge(xf_out, 16 * len(GROUPS))
                if j >= 2:
                    pool.wait_ge(xs_ps, j - 1)
                    pool.wait_ge(xb_ready, j - 1)
                pool.indirect_dma_start(out=xs[:, j % 2, :], out_offset=None, in_=xf_dram,
                                        in_offset=bass.IndirectOffsetOnAxis(tok[:, j:j + 1], 0)
                                        ).then_inc(xs_in[j % 2], 16)

            def scale(j):
                e = pool.value_load(chunk_e[0:1, j:j + 1], min_val=0, max_val=NE - 1)
                pool.wait_ge(yu_ready, j + 1)
                pool.tensor_tensor(yu[:, j % 2, :], yu[:, j % 2, :], gamma_row[:, bass.ds(e * D, D)],
                                   ALU.mult).then_inc(yg_ready, 1)

            gather(0)
            for j in range(NCH):
                if j + 1 < NCH:
                    gather(j + 1)
                e = pool.value_load(chunk_e[0:1, j:j + 1], min_val=0, max_val=NE - 1)
                if j == 0:
                    pool.wait_ge(ffn_rows_in, 48)
                if j >= 2:
                    pool.wait_ge(yt_ready, j - 1)
                pool.wait_ge(xs_in[j % 2], 16 * (j // 2 + 1))
                pool.tensor_tensor(xb[:, j % 2, :], xs[:, j % 2, :], b2_row[:, bass.ds(e * D, D)],
                                   ALU.add).then_inc(xb_ready, 1)
                if j >= 3:
                    scale(j - 3)
            for j in range(NCH - 3, NCH):
                scale(j)
            for i in range(2):
                pool.wait_ge(y_out[i], 16 * ((NCH + 1 - i) // 2))
            pool.wait_ge(yg_ready, NCH)

            def low_parts(g0, g1):
                for b in range(g0, g1):
                    pool.wait_ge(hi_ready, b + 1)
                    pool.wait_ge(tr_ps, TR_X3 + b + 1)
                    pool.tensor_tensor(rows_lo[1][:, b, :], xn3[:, b, :], rows_hi[:, b, :].bitcast(F32),
                                       ALU.subtract).then_inc(lo_ready, 1)

            for b in range(NB):
                for k in range(TOPK):
                    pool.indirect_dma_start(out=y_top[k][:, b, :], out_offset=None, in_=y_dram,
                                            in_offset=bass.IndirectOffsetOnAxis(slot_i[:, k, b:b + 1].bitcast(U32), 0)
                                            ).then_inc(y_top_in[b], 16)
                if b == L3_GROUPS[2][1] - 1:
                    low_parts(*L3_GROUPS[0])
            for g0, g1 in L3_GROUPS[1:]:
                low_parts(g0, g1)

            pool.wait_ge(l1w_in, 64)
            for g0, g1 in L1_GROUPS:
                for b in range(g0, g1 - 1):
                    pool.wait_ge(gamma_done, b + 1)
                    pool.tensor_tensor(xn[:, b, :], xn[:, b, :], l1b_row, ALU.add).then_inc(beta_done, 1)
                for b in range(g0, g1):
                    pool.wait_ge(xn_ready, 3 * NB + b + 1)
                    pool.tensor_tensor(x_sb[:, b, :], x_sb[:, b, :], xn[:, b, :], ALU.add).then_inc(added, 1)

        @block.tensor
        def _(pe):
            mm = nc.tensor.matmul

            def turn(t, pieces):
                if t >= 2:
                    pe.wait_ge(tr_sb, t - 1)
                if TR_H1 + 2 <= t < TR_ATT + 2:
                    pe.wait_ge(lo_ready, t - TR_H1 - 1)
                for to, fr in pieces:
                    last = nc.tensor.transpose(to, fr, ident[0:fr.shape[0], 0:fr.shape[0]])
                last.then_inc(tr_ps, 1)

            def turn_rows(t0, rows, n0, b0, b1):
                for b in range(b0, b1):
                    pe.wait_ge(xn_ready, n0 + b + 1)
                    bank = ps[:, 6 + (t0 + b) % 2, :]
                    turn(t0 + b, [(bank[:, c * P:(c + 1) * P], rows[:, b, c * P:(c + 1) * P]) for c in range(DC)])

            pe.wait_ge(consts_ready, 9)
            for j in range(NJ):
                turn_rows(TR_X, xn, 0, j * JB, (j + 1) * JB)
                if j == NJ - 1:
                    pe.wait_ge(edges_f, 1)
                    pe.wait_ge(tr_sb, TR_X + NB)
                    mm(ps[:, 7, 0:EG], row0, dst_f[:, 0:EC:GC], start=True, stop=True).then_inc(base_ps, 1)
                    pe.wait_ge(img_in, 64)
                    for m in range(PC):
                        for k in range(KI):
                            last = mm(ps[:, 0, m * R:(m + 1) * R], wi_sb[:, k, m * P:(m + 1) * P], img_sb[:, k, :],
                                      start=(k == 0), stop=(k == KI - 1))
                    last.then_inc(img_ps, 1)
                pe.wait_ge(attw_in, 48)
                pe.wait_ge(tr_sb, TR_X + (j + 1) * JB)
                for m in range(PC):
                    t = j * PC + m
                    if t >= 4:
                        pe.wait_ge(proj_sb, t - 3)
                    for k in range(DC):
                        last = mm(ps[:, 2 + t % 4, :], wf_sb[:, k, m * P:(m + 1) * P], xT[:, k, j * 512:(j + 1) * 512],
                                  start=(k == 0), stop=(k == DC - 1))
                    last.then_inc(proj_ps, 1)

            pe.wait_ge(wim_in, 16)
            for k in range(KI):
                last = mm(ps[0:R, 1, :], img_sb[:, k, :], wim_sb[:, k, :], start=(k == 0), stop=(k == KI - 1))
            last.then_inc(img_ps, 1)

            pe.wait_ge(outside_ready, 1)
            mm(ps[:, 7, EG:EG + 1], ones_bf[:], outside_bf[:], start=True, stop=True).then_inc(outside_ps, 1)
            pe.wait_ge(loose_ready, 1)
            pe.wait_ge(proj_sb, PC * NJ)

            pe.wait_ge(logits_zero, 1)

            def logits_region(i, u):
                if u < 2:
                    pe.wait_ge(sum_ready, 2 * i + (u + 1))
                else:
                    pe.wait_ge(third_ready, i + 1)
                for j in range(NJ):
                    last = mm(ps[0:R, LOGIT_BANKS[j], :], region_col[:, u, :], tanh_t[u][:, 1, j * 512:(j + 1) * 512],
                              start=False, stop=True, skip_group_check=True)
                last.then_inc(att_ps, 1)

            def window_chunk(g, pair, q):
                if q % OC == 0:
                    pe.wait_ge(win_oh, pair + 1)
                if q % GC == 0:
                    pe.wait_ge(win_bank_free, g + 1)
                last = mm(ps[:, 2 + (q // GC) % 4, 0:WW], oh_lo[q // OC][:, :, q % OC],
                          oh_win[q // OC][:, :, q % OC], start=(q % GC == 0), stop=(q % GC == GC - 1))
                if q % GC == GC - 1:
                    last.then_inc(win_ps, 1)

            with pe.Fori(0, R // 3) as i:
                for u in range(3):
                    logits_region(i, u)
                    for q in range(8 * GC * u // 3, 8 * GC * (u + 1) // 3):
                        window_chunk(8 * i + q // GC, 4 * i + q // OC, q)

            def count_chunk(k, c, b, start, stop):
                pe.wait_ge(edge_oh, k * EC + c + 1)
                for s in range(2):
                    for j in range(NJ):
                        last = mm(ps[:, 2 + s * NJ + j, :], oh_src[:, b, s * P:(s + 1) * P],
                                  oh_dst[:, b, j * 512:(j + 1) * 512], start=start, stop=stop)
                last.then_inc(edge_oh_used, 1)

            pe.wait_ge(loose_ready, 1)
            n_loose = pe.value_load(loose[0:1, 0:1], min_val=0, max_val=P)
            with pe.If(n_loose > 0):
                pe.wait_ge(win_bank_free, EG + 4)
                pe.wait_ge(logits_sb, NJ)
                for k in range(NB // 2):
                    if k >= 1:
                        pe.wait_ge(pass_out, k)
                    count_chunk(k, 0, 0, True, False)
                    with pe.Fori(0, EC // 2 - 1) as c:
                        count_chunk(k, 2 * c + 1, 1, False, False)
                        count_chunk(k, 2 * c + 2, 0, False, False)
                    count_chunk(k, EC - 1, 1, False, True)
                pe.wait_ge(pass_out, NB // 2)

            pe.wait_ge(logits_sb, NJ)
            for b in range(NB):
                last = nc.tensor.transpose(ps[:, 0, b * R:(b + 1) * R], logits_T[0:R, b * P:(b + 1) * P],
                                           ident[0:R, 0:R])
            last.then_inc(logits_turned, 1)

            pe.wait_ge(gnnw_in, 96)
            pe.wait_ge(win_bank_free, EG + 4)
            def h1_span(j, m0, m1):
                for m in range(m0, m1):
                    t = j * DC + m
                    if t >= 4:
                        pe.wait_ge(h1_sb, t - 3)
                    for k in range(DC):
                        last = mm(ps[:, 2 + t % 4, :], wn_sb[:, k, m * P:(m + 1) * P], xT[:, k, j * 512:(j + 1) * 512],
                                  start=(k == 0), stop=(k == DC - 1))
                    last.then_inc(h1_ps, 1)

            def turn_h1(j):
                pe.wait_ge(h1_sb, DC * (j + 1))
                for b in range(j * JB, (j + 1) * JB):
                    bank = ps[:, 6 + (TR_H1 + b) % 2, :]
                    turn(TR_H1 + b, [(bank[:, c * P:(c + 1) * P], hT[:, c, b * P:(b + 1) * P]) for c in range(DC)])

            h1_span(0, 0, DC)
            h1_span(1, 0, DC)
            pe.wait_ge(over_flag, 1)
            mm(ps[:, 1, 0:1], ones_bf[:], over_bf[:], start=True, stop=True).then_inc(over_ps, 1)
            turn_h1(0)
            h1_span(2, 0, DC // 2)
            turn_h1(1)
            h1_span(2, DC // 2, DC)
            turn_h1(2)
            pe.wait_ge(att_ready, 1)
            for j in range(NJ):
                bank = ps[0:R, 6 + (TR_ATT + j) % 2, :]
                turn(TR_ATT + j, [(bank[:, i * P:(i + 1) * P], att[:, j * JB + i, :]) for i in range(JB)])

            pe.wait_ge(over_ready, 1)
            n_over = pe.value_load(over[0:1, 0:1], min_val=0, max_val=P)

            def add_rest(layer, j):
                for s in range(NB):
                    n = (layer * NJ + j) * NB + s
                    pe.wait_ge(rest_ready, n + 1)
                    if layer == 0:
                        pe.wait_ge(lo_ready, s + 1)
                    else:
                        pe.wait_ge(lo_ready, NB + s + 1)
                        mm(ps[:, DEG_BANKS[j], :], ones_r, cf_rest[:, n % 2, :], start=False, stop=False)
                    for m in range(DC):
                        for rows in (rows_hi, rows_lo[layer]):
                            last = mm(ps[:, (j * DC + m) % 6, :], rows[:, s, m * P:(m + 1) * P], cf_rest[:, n % 2, :],
                                      start=False, stop=False)
                    last.then_inc(rest_used, 1)

            def aggregate(layer):
                for j in range(NJ):
                    if layer == 1 and j == 1:
                        pe.wait_ge(tr_sb, TR_X3 + NB)
                        pe.wait_ge(deg_read, 1)
                    for m in range(DC):
                        t = (layer * NJ + j) * DC + m
                        if t >= 6 and (layer == 0 or j * DC + m >= 6):
                            pe.wait_ge(agg_sb, t - 5)
                    for s in range(NB):
                        n = (layer * NJ + j) * NB + s
                        for g0, g1 in L3_GROUPS:
                            if layer == 1 and j == 0 and s == g0:
                                turn_rows(TR_X3, xn3, 2 * NB, g0, g1)
                        if s == NB - 1:
                            with pe.If(n_over > 0):
                                add_rest(layer, j)
                        pe.wait_ge(cf_ready, n + 1)
                        if j == 0:
                            pe.wait_ge(lo_ready, layer * NB + s + 1)
                        for m in range(DC):
                            bank = ps[:, (j * DC + m) % 6, :]
                            mm(bank, rows_hi[:, s, m * P:(m + 1) * P], cf[:, n % 3, :], start=(s == 0), stop=False)
                            last = mm(bank, rows_lo[layer][:, s, m * P:(m + 1) * P], cf[:, n % 3, :], start=False,
                                      stop=(layer == 1 and s == NB - 1))
                            if layer == 1 and s == NB - 1:
                                last.then_inc(agg_ps, 1)
                        if layer == 1:
                            last = mm(ps[:, DEG_BANKS[j], :], ones_r, cf[:, n % 3, :], start=(s == 0),
                                      stop=(s == NB - 1))
                        last.then_inc(cf_used, 1)
                    if layer == 0:
                        for m in range(DC):
                            mm(ps[:, (j * DC + m) % 6, :], img_ctx[0:R, m * P:(m + 1) * P],
                               attT[0:R, j * 512:(j + 1) * 512], start=False, stop=True).then_inc(agg_ps, 1)

            pe.wait_ge(tr_sb, TR_ATT + NJ)
            aggregate(0)

            def turn_group(g0, g1):
                turn_rows(TR_XF, xn, NB, g0, g1)

            def route_group(g0, g1):
                for b in range(g0, g1):
                    pe.wait_ge(tr_sb, TR_XF + b + 1)
                    for k in range(DC):
                        last = mm(ps[:, 4, b * NE:(b + 1) * NE], xT[:, k, b * P:(b + 1) * P], rw_sb[:, k, :],
                                  start=(k == 0), stop=(k == DC - 1))
                if g1 == NB:
                    last.then_inc(router_ps, 1)

            pe.wait_ge(agg_sb, DC * NJ)
            for b in range(NB):
                if b >= 4:
                    pe.wait_ge(out_read, b - 3)
                for k in range(2 * DC):
                    rows = xT[:, k, b * P:(b + 1) * P] if k < DC else hT[:, k - DC, b * P:(b + 1) * P]
                    last = mm(ps[:, b % 4, :], rows, wap_sb[:, k, :], start=(k == 0), stop=(k == 2 * DC - 1))
                last.then_inc(out_ps, 1)
                for g0, g1 in GROUPS:
                    if b == g1 + 2:
                        turn_group(g0, g1)
                    if b == g1 + 3:
                        route_group(g0, g1)
            for g0, g1 in GROUPS:
                if g1 + 2 > NB - 1:
                    turn_group(g0, g1)
                if g1 + 3 > NB - 1:
                    route_group(g0, g1)

            pe.wait_ge(sel_ready, 1)
            for s in range(NB):
                mm(ps[:, 1, 0:NB * NE], before_bf[:] if s == 0 else ones_bf[:],
                   sel_bf[:, (NB - 1 - s) * NE:(2 * NB - 1 - s) * NE], start=(s == 0), stop=(s == NB - 1))
            for b in range(NB):
                last = mm(ps[:, 2, 0:NE], ones_bf[:], sel_bf[:, (NB - 1 + b) * NE:(NB + b) * NE],
                          start=(b == 0), stop=(b == NB - 1))
            last.then_inc(pos_ps, 1)

            for k in range(TOPK):
                pe.wait_ge(slot_oh, k + 1)
                for b in range(NB):
                    last = mm(ps[:, 3, 0:2 * SW], lo_oh[:, k, b, :], hi_oh[:, k, b, :],
                              start=(k == 0 and b == 0), stop=(k == TOPK - 1 and b == NB - 1))
            last.then_inc(slot_ps, 1)

            pe.wait_ge(w1_in, 48)
            pe.wait_ge(w2_in, 32)
            pe.wait_ge(tok_ready, 2)

            def turn_tokens(j, b, half, free):
                pe.wait_ge(xs_in[b], 16 * (half + 1))
                if free is not None:
                    pe.wait_ge(xs_T, free)
                for c in range(DC):
                    last = nc.tensor.transpose(ps[:, 4 + b, c * P:(c + 1) * P], xs[:, b, c * P:(c + 1) * P], ident[:])
                last.then_inc(xs_ps, 1)

            def expert_of(j):
                return pe.value_load(chunk_e[0:1, bass.ds(j, 1)], min_val=0, max_val=NE - 1)

            def hidden(j, b, free):
                e = expert_of(j)
                pe.wait_ge(xs_T, j + 1)
                if free is not None:
                    pe.wait_ge(hid_sb, free)
                for k in range(DC):
                    last = mm(ps[:, b, 0:F], xsT[:, b, k, :], w1_sb[:, bass.ds(e * (DC * F) + k * F, F)],
                              start=(k == 0), stop=(k == DC - 1))
                last.then_inc(hid_ps, 1)

            def turn_hidden(j, b, free):
                pe.wait_ge(hid_sb, j + 1)
                if free is not None:
                    pe.wait_ge(hidT_sb, free)
                for c in range(FC):
                    last = nc.tensor.transpose(ps[:, 6 + b, c * P:(c + 1) * P], hb[:, b, c * P:(c + 1) * P], ident[:])
                last.then_inc(hidT_ps, 1)

            def expert_out(j, b, free):
                e = expert_of(j)
                pe.wait_ge(hidT_sb, j + 1)
                if free is not None:
                    pe.wait_ge(yt_ready, free)
                for k in range(FC):
                    last = mm(ps[:, 2 + b, :], hbT[:, b, k, :], w2_sb[:, bass.ds(e * (FC * D) + k * D, D)],
                              start=(k == 0), stop=(k == FC - 1))
                last.then_inc(y_ps, 1)

            def expert_step(n, u, half, more=True):
                hidden(n + u, u % 2, n + (u - 1))
                if more:
                    turn_tokens(n + (u + 1), 1 - u % 2, half, n + u)
                expert_out(n + (u - 1), 1 - u % 2, n + (u - 2) if u > 1 else None)
                turn_hidden(n + u, u % 2, n + (u - 1))

            turn_tokens(0, 0, 0, None)
            hidden(0, 0, None)
            turn_tokens(1, 1, 0, None)
            turn_hidden(0, 0, None)
            expert_step(0, 1, 1)
            expert_step(0, 2, 1)
            with pe.Fori(0, (NCH - 5) // 2) as i:
                expert_step(2 * i, 3, i + 2)
                expert_step(2 * i, 4, i + 2)
            expert_step(NCH - 5, 3, NCH // 2)
            expert_step(NCH - 5, 4, 0, more=False)
            expert_out(NCH - 1, 0, NCH - 2)

            pe.wait_ge(gatew_ready, 1)
            pe.wait_ge(beta_ready, 1)
            pe.wait_ge(hidT_sb, NCH)
            for j in range(NJ):
                bank = ps[0:4 * NE, 6 + (TR_GATE + j) % 2, :]
                turn(TR_GATE + j, [(bank[:, i * P:(i + 1) * P], gate_r[:, j * JB + i].rearrange(
                    "p k e -> p (k e)").bitcast(F32)) for i in range(JB)])
            pe.wait_ge(tr_sb, TR_GATE + NJ)
            pe.wait_ge(yt_ready, NCH)
            for b in range(NB):
                if b >= 6:
                    pe.wait_ge(beta_read, b - 5)
                mm(ps[:, b % 6, :], gate_T[0:4 * NE, b * P:(b + 1) * P], beta_r[:], start=True,
                   stop=True).then_inc(beta_ps, 1)
            pe.wait_ge(beta_read, NB)

            pe.wait_ge(ones_r_ready, 1)
            aggregate(1)
            pe.wait_ge(l1w_in, 64)

            def own(b):
                if b >= 8:
                    pe.wait_ge(l1_read, b - 7)
                elif L1_BANKS[b] in (6, 7):
                    pe.wait_ge(deg_read, NJ - L1_BANKS[b] % 2)
                elif b > 1:
                    pe.wait_ge(agg_sb, 2 * DC * NJ - 5 + L1_BANKS[b])
                for k in range(DC):
                    mm(ps[:, L1_BANKS[b % 8], :], xT[:, k, b * P:(b + 1) * P], ws_sb[:, k, :], start=(k == 0),
                       stop=False)

            pe.wait_ge(agg_sb, 2 * DC * NJ - DC)
            for b in range(6):
                own(b)
            pe.wait_ge(wg_in, 16)
            for b in range(NB):
                pe.wait_ge(mean_ready, DC * (b // JB + 1))
                for k in range(DC):
                    last = mm(ps[:, L1_BANKS[b % 8], :], hT[:, k, b * P:(b + 1) * P], wg_sb[:, k, :],
                              start=False, stop=(k == DC - 1))
                last.then_inc(l1_ps, 1)
                if b + 6 < NB:
                    own(b + 6)

        @block.scalar
        def _(act):
            def evac(to, fr):
                return nc.scalar.activation(to, fr, ACT.Copy)

            def apply_norm(to, fr, b):
                return nc.scalar.activation(to[:, b, :], fr[:, b, :], ACT.Identity, bias=shift[:, b:b + 1],
                                            scale=rstd[:, b:b + 1])

            def turned_out(t0, b, to):
                act.wait_ge(tr_ps, t0 + b + 1)
                evac(to, ps[:, 6 + (t0 + b) % 2, :].rearrange("p (c n) -> p c n", c=DC)).then_inc(tr_sb, 1)

            def norm_span(j):
                act.wait_ge(scales_ready, j + 1)
                for b in range(j * JB, (j + 1) * JB):
                    apply_norm(xn, x_sb, b).then_inc(xn_ready, 1)

            norm_span(0)
            for j in range(NJ):
                for b in range(j * JB, (j + 1) * JB):
                    turned_out(TR_X, b, xT[:, :, b * P:(b + 1) * P])
                if j + 1 < NJ:
                    norm_span(j + 1)
                for m in range(PC):
                    t = j * PC + m
                    act.wait_ge(proj_ps, t + 1)
                    evac(node_proj[:, m, j * 512:(j + 1) * 512], ps[:, 2 + t % 4, :]).then_inc(proj_sb, 1)
            act.wait_ge(img_bias_ready, 1)
            act.wait_ge(proj_sb, PC * NJ)

            def tanh_region(r, u, before):
                def tanh(m):
                    return nc.scalar.activation(tanh_t[u][:, m, :], node_proj[:, m, :], ACT.Tanh,
                                                bias=img_bias[:, m, bass.ds(r, 1)])

                if before is not None:
                    if u < 2:
                        act.wait_ge(sum_ready, 2 * before + (u + 1))
                    else:
                        act.wait_ge(third_ready, before + 1)
                tanh(0).then_inc(tanh_sb, 1)
                act.wait_ge(tanh_sb, r + 1)
                nc.scalar.activation(tanh_t[u][:, 0, :], tanh_t[u][:, 0, :], ACT.Copy, scale=wa_sb[:, 0:1])
                if before is not None:
                    act.wait_ge(att_ps, 3 * before + (u + 1))
                tanh(1).then_inc(scaled_sb, 1)

            tanh_region(0, 0, None)
            act.wait_ge(img_ps, 2)
            evac(img_ctx[0:R, :], ps[0:R, 1, :]).then_inc(img_ctx_ready, 1)
            tanh_region(1, 1, None)
            tanh_region(2, 2, None)
            with act.Fori(0, R // 3 - 1) as i:
                for u in range(3):
                    tanh_region(3 * i + (u + 3), u, i)
            act.wait_ge(att_ps, R)
            for j in range(NJ):
                evac(logits_T[0:R, j * 512:(j + 1) * 512], ps[0:R, LOGIT_BANKS[j], :]).then_inc(logits_sb, 1)

            def h1_tile(t):
                j, m = t // DC, t % DC
                act.wait_ge(h1_ps, t + 1)
                nc.scalar.activation(hT[:, m, j * 512:(j + 1) * 512], ps[:, 2 + t % 4, :], ACT.Identity,
                                     bias=bn_sb[:, m:m + 1]).then_inc(h1_sb, 1)

            act.wait_ge(gnnw_in, 96)
            for t in range(DC):
                h1_tile(t)
            act.wait_ge(att_shift, 1)
            nc.scalar.activation(att, att, ACT.Exp).then_inc(att_exp, 1)
            def h1_high(j):
                for b in range(j * JB, (j + 1) * JB):
                    turned_out(TR_H1, b, rows_hi[:, b, :].rearrange("p (c n) -> p c n", c=DC))

            for j, t0, t1 in ((0, DC, 2 * DC), (1, 2 * DC, 5 * DC // 2), (2, 5 * DC // 2, 3 * DC)):
                for t in range(t0, t1):
                    h1_tile(t)
                h1_high(j)
            for j in range(NJ):
                t = TR_ATT + j
                act.wait_ge(tr_ps, t + 1)
                evac(attT[0:R, j * 512:(j + 1) * 512], ps[0:R, 6 + t % 2, :]).then_inc(tr_sb, 1)
            for t in range(DC * NJ):
                j, m = t // DC, t % DC
                act.wait_ge(agg_ps, t + 1)
                nc.scalar.activation(xT[:, m, j * 512:(j + 1) * 512], ps[:, (j * DC + m) % 6, :], ACT.Identity,
                                     bias=bim_sb[:, m:m + 1]).then_inc(agg_sb, 1)
            for g, (g0, g1) in enumerate(GROUPS):
                act.wait_ge(scales_ready, XG + g + 1)
                for b in range(g0, g1):
                    apply_norm(xn, x_sb, b).then_inc(xn_ready, 1)
                for b in range(g0, g1):
                    turned_out(TR_XF, b, xT[:, :, b * P:(b + 1) * P])
            act.wait_ge(gate_diff, 1)
            nc.scalar.activation(gate_e[:], gate_d[:], ACT.Exp).then_inc(gate_exp, 1)
            def tokens_out(j, b, free):
                act.wait_ge(xs_ps, j + 1)
                if free is not None:
                    act.wait_ge(hid_ps, free)
                evac(xsT[:, b], ps[:, 4 + b, :].rearrange("p (c n) -> p c n", c=DC)).then_inc(xs_T, 1)

            def hidden_out(j, b, free):
                act.wait_ge(hidT_ps, j + 1)
                if free is not None:
                    act.wait_ge(y_ps, free)
                nc.scalar.activation(hbT[:, b], ps[:, 6 + b, 0:F].rearrange("p (c n) -> p c n", c=FC),
                                     ACT.Relu).then_inc(hidT_sb, 1)

            def root(j, b):
                act.wait_ge(yv_ready, j + 1)
                nc.scalar.activation(e_mv[:, b, 3:4], e_mv[:, b, 2:3], ACT.Sqrt).then_inc(sd_ready, 1)

            def step(n, u, more=True):
                if more:
                    tokens_out(n + (u + 1), 1 - u % 2, n + u)
                hidden_out(n + u, u % 2, n + (u - 1))
                root(n + (u - 1), 1 - u % 2)

            tokens_out(0, 0, None)
            tokens_out(1, 1, None)
            hidden_out(0, 0, None)
            step(0, 1)
            step(0, 2)
            with act.Fori(0, (NCH - 5) // 2) as i:
                step(2 * i, 3)
                step(2 * i, 4)
            step(NCH - 5, 3)
            step(NCH - 5, 4, more=False)
            root(NCH - 1, 0)

            for j in range(NJ):
                t = TR_GATE + j
                act.wait_ge(tr_ps, t + 1)
                evac(gate_T[0:4 * NE, j * 512:(j + 1) * 512], ps[0:4 * NE, 6 + t % 2, :]).then_inc(tr_sb, 1)

            def roots(n, g0, g1):
                act.wait_ge(var_ready, n + 1)
                nc.scalar.activation(nt_a[:, g0:g1], var_e[:, g0:g1], ACT.Sqrt).then_inc(root_ready, 1)

            n0 = XG + len(GROUPS)
            for g, (g0, g1) in enumerate(L3_GROUPS):
                roots(g, g0, g1)
                act.wait_ge(scales_ready, n0 + g + 1)
                for b in range(g0, g1):
                    apply_norm(xn3, x_sb, b).then_inc(xn_ready, 1)
                for b in range(g0, g1):
                    apply_norm(rows_hi, x_sb, b).then_inc(hi_ready, 1)
                for b in range(g0, g1):
                    turned_out(TR_X3, b, xT[:, :, b * P:(b + 1) * P])
            for t in range(DC * NJ):
                j, m = t // DC, t % DC
                act.wait_ge(agg_ps, DC * NJ + t + 1)
                evac(hT[:, m, j * 512:(j + 1) * 512], ps[:, (j * DC + m) % 6, :]).then_inc(agg_sb, 1)
            for n, (g0, g1) in enumerate(L1_GROUPS):
                for i, (fr, done) in enumerate(((xn, hn_ready), (x_sb, xn_ready))):
                    m = len(L3_GROUPS) + 2 * n + i
                    roots(m, g0, g1)
                    act.wait_ge(scales_ready, n0 + m + 1)
                    for b in range(g0, g1):
                        apply_norm(xn, fr, b).then_inc(done, 1)

        @block.vector
        def _(dve):
            order = [0]
            v = nc.vector

            def link(ins):
                order[0] += 1
                ins.then_inc(dve_order, 1)
                dve.wait_ge(dve_order, order[0])

            def newton(to, var, tmp):
                link(v.tensor_tensor(tmp, to, to, ALU.mult))
                link(v.scalar_tensor_tensor(out=tmp, in0=tmp, scalar=-0.5, in1=var, op0=ALU.mult, op1=ALU.mult))
                link(v.scalar_tensor_tensor(out=to, in0=tmp, scalar=1.5, in1=to, op0=ALU.add, op1=ALU.mult))

            def rsqrt(to, var, tmp):
                link(v.tensor_scalar(tmp.bitcast(I32), var.bitcast(I32), 1, None, ALU.logical_shift_right))
                link(v.tensor_scalar(to.bitcast(I32), tmp.bitcast(I32), -1.0, RSQRT_MAGIC, ALU.mult, ALU.add))
                for _ in range(3):
                    newton(to, var, tmp)

            roots = [0]

            def row_scales(g0, g1, act_root=False):
                for b in range(g0, g1):
                    last = v.bn_aggr(mv[:, b, :], stats[:, b, :])
                link(last)
                y, t, var = rstd[:, g0:g1], nt_a[:, g0:g1], var_e[:, g0:g1]
                if act_root:
                    roots[0] += 1
                    v.tensor_scalar(var, mv[:, g0:g1, 1], GNN_EPS, None, ALU.add).then_inc(var_ready, 1)
                    dve.wait_ge(root_ready, roots[0])
                    link(v.reciprocal(y, t))
                    newton(y, var, t)
                else:
                    link(v.tensor_scalar(var, mv[:, g0:g1, 1], GNN_EPS, None, ALU.add))
                    rsqrt(y, var, t)
                v.scalar_tensor_tensor(out=shift[:, g0:g1], in0=mv[:, g0:g1, 0], scalar=-1.0, in1=rstd[:, g0:g1],
                                       op0=ALU.mult, op1=ALU.mult).then_inc(scales_ready, 1)

            def row_norms(g0, g1, act_root=False):
                for b in range(g0, g1):
                    last = v.bn_stats(stats[:, b, :], x_sb[:, b, :])
                link(last)
                row_scales(g0, g1, act_root)

            dve.wait_ge(consts_ready, 9)
            v.tensor_copy(iota_f[:], iota_i[:])
            v.tensor_copy(first_key[:], key_i[:])
            v.memset(one_f[:], 1.0)
            v.memset(sel_bf[:], 0.0)
            for b in range(NB):
                v.memset(block_col[:, b:b + 1], float(b))
            link(v.tensor_copy(iota_p[:], iota_pi[:]))

            for g in range(XG):
                dve.wait_ge(x_in[g], 16)
                row_norms(g * GB, (g + 1) * GB)

            dve.wait_ge(edges_in, 32)
            v.tensor_copy(dst_f, dst_i).then_inc(edges_f, 1)
            v.tensor_scalar(edge_t.bitcast(I32), src_i, 7, None, ALU.logical_shift_right)
            link(v.tensor_scalar(edge_u.bitcast(I32), src_i, P - 1, None, ALU.bitwise_and))
            link(v.tensor_copy(lo_16[:], edge_u.bitcast(I32)))
            dve.wait_ge(base_ps, 1)
            link(v.tensor_scalar(base_f[:], ps[:, 7, 0:EG], float(N - WIN), None, ALU.min))
            v.tensor_copy(base_i[:], base_f[:])
            dve.wait_ge(edges_f, 1)
            link(v.tensor_tensor(edge_u.rearrange("p (g c) -> p g c", c=GC), dst_f.rearrange("p (g c) -> p g c", c=GC),
                                 base_f[:].unsqueeze(2).to_broadcast([P, EG, GC]), ALU.subtract))
            v.tensor_reduce(outside[:, 0:1], edge_u, AX_X, ALU.max)
            v.tensor_reduce(outside[:, 1:2], edge_u, AX_X, ALU.min)
            link(v.scalar_tensor_tensor(out=win_16[:], in0=edge_t.bitcast(I32), scalar=float(WIN), in1=edge_u,
                                        op0=ALU.mult, op1=ALU.add))
            link(v.tensor_scalar(outside[:, 0:1], outside[:, 0:1], WIN - 0.5, None, ALU.is_gt))
            link(v.tensor_scalar(outside[:, 1:2], outside[:, 1:2], 0.0, None, ALU.is_lt))
            v.tensor_tensor(outside_bf[:], outside[:, 0:1], outside[:, 1:2], ALU.max).then_inc(outside_ready, 1)
            def window_rows(pair, k):
                for to, num, of in ((oh_lo[k], num_win[:, 0:P, :], lo_16), (oh_win[k], num_win, win_16)):
                    last = v.tensor_tensor(to, num, of[:, bass.ds(OC * pair, OC)].unsqueeze(1).to_broadcast(
                        [P, num.shape[1], OC]), ALU.is_equal)
                last.then_inc(win_oh, 1)

            def window_add(g, u):
                base = dve.value_load(base_i[0:1, bass.ds(g, 1)], min_val=0, max_val=N - WIN)
                dve.wait_ge(win_ps, g + 1)
                dve.wait_ge(win_bank_free, g + 4)
                at_base = counts[:, :, bass.ds(base, WIN)]
                v.tensor_tensor(at_base, at_base, ps[:, 2 + u % 4, 0:WW].rearrange("p (b w) -> p b w", w=WIN),
                                ALU.add).then_inc(win_bank_free, 1)

            def mark_region(r, u):
                v.tensor_scalar(region_col[:, u, :], iota_f[:, 0:R], iota_f[:, bass.ds(r, 1)], None, ALU.is_equal)

            def sum_region(r, u):
                mark_region(r, u)
                dve.wait_ge(scaled_sb, r + 1)
                if u == 1:
                    mark_region(r + 1, 2)
                v.scalar_tensor_tensor(out=tanh_t[u][:, 1, :], in0=tanh_t[u][:, 1, :], scalar=wa_sb[:, 1:2],
                                       in1=tanh_t[u][:, 0, :], op0=ALU.mult, op1=ALU.add).then_inc(sum_ready, 1)

            dve.wait_ge(img_in, 64)
            link(v.tensor_tensor(bfi_sum[:], bfi[:, 0, :], bfi[:, 1, :], ALU.add))
            dve.wait_ge(img_ps, 1)
            for m in range(PC):
                last = v.tensor_scalar(img_bias[:, m, :], ps[:, 0, m * R:(m + 1) * R], bfi_sum[:, m:m + 1], None,
                                       ALU.add)
            last.then_inc(img_bias_ready, 1)

            v.tensor_copy(num_win, iota_n[:, 0:WW].unsqueeze(2).to_broadcast([P, WW, OC])).then_inc(num_ready, 1)
            dve.wait_ge(tr_sb, TR_X + NB)
            dve.wait_ge(img_bias_ready, 1)
            for j in (0, 2, 1):
                if LOGIT_BANKS[j] == 1:
                    sum_region(0, 0)
                    dve.wait_ge(img_ctx_ready, 1)
                last = v.memset(ps[0:R, LOGIT_BANKS[j], :], 0.0)
            last.then_inc(logits_zero, 1)
            dve.wait_ge(outside_ps, 1)
            v.tensor_copy(loose[:], ps[:, 7, EG:EG + 1]).then_inc(loose_ready, 1)

            dve.wait_ge(counts_zero, 1)
            dve.wait_ge(proj_sb, PC * NJ)
            v.memset(nt_b[:, 0:1], 0.0).then_inc(win_bank_free, 4)
            dve.wait_ge(num_ready, 1)
            window_rows(0, 0)
            window_rows(1, 1)
            sum_region(1, 1)

            def window_turn(i, more=True):
                for u in range(8):
                    if u % 2 == 0 and (more or u < 4):
                        window_rows(4 * i + (u // 2 + 2), (u // 2 + 2) % 4)
                    if u == 5 and more:
                        sum_region(3 * i + 3, 0)
                    if u == 7 and more:
                        sum_region(3 * i + 4, 1)
                    window_add(8 * i + u, u)

            with dve.Fori(0, R // 3 - 1) as i:
                window_turn(i)
            window_turn(R // 3 - 1, more=False)
            dve.wait_ge(win_bank_free, EG + 4)

            def edge_rows(k, c, b):
                v.tensor_scalar(oh_src[:, b, :], iota_n[:, 0:2 * P], src_k[:, bass.ds(c, 1)], None, ALU.is_equal)
                v.tensor_scalar(oh_dst[:, b, :], iota_n, dst_f[:, bass.ds(c, 1)], None,
                                ALU.is_equal).then_inc(edge_oh, 1)

            n_loose = dve.value_load(loose[0:1, 0:1], min_val=0, max_val=P)
            with dve.If(n_loose > 0):
                for k in range(NB // 2):
                    v.tensor_scalar(src_k, src_i, float(-2 * P * k), None, ALU.add).then_inc(src_k_ready, 1)
                    dve.wait_ge(src_k_ready, k + 1)
                    for c in range(2):
                        if k >= 1:
                            dve.wait_ge(edge_oh_used, k * EC + c - 1)
                        edge_rows(k, c, c)
                    with dve.Fori(0, EC // 2 - 1) as c:
                        for i in range(2):
                            dve.wait_ge(edge_oh_used, 2 * c + (k * EC + i + 1))
                            edge_rows(k, 2 * c + (i + 2), i)
                    dve.wait_ge(edge_oh_used, (k + 1) * EC)
                    for s in range(2):
                        last = v.tensor_copy(counts[:, 2 * k + s, :],
                                             ps[:, 2 + s * NJ:2 + (s + 1) * NJ, :].rearrange("p a b -> p (a b)"))
                    last.then_inc(pass_out, 1)
                dve.wait_ge(pass_out, NB // 2)
            v.memset(nt_b[:, 0:1], 0.0).then_inc(counts_ready, 1)

            dve.wait_ge(attw_in, 48)
            dve.wait_ge(logits_turned, 1)
            link(v.tensor_scalar(att, ps[:, 0, 0:NB * R].rearrange("p (b r) -> p b r", b=NB), ba_sb[:, 0:1], None,
                                 ALU.add))
            link(v.tensor_reduce(att_red, att, AX_X, ALU.max))
            v.tensor_tensor(att, att, att_red.unsqueeze(2).to_broadcast([P, NB, R]),
                            ALU.subtract).then_inc(att_shift, 1)
            dve.wait_ge(counts_ready, 1)
            link(v.tensor_reduce(count_max[:], counts[:], mybir.AxisListType.XY, ALU.max))
            v.tensor_scalar(over_bf[:], count_max[:], float(EXACT), None, ALU.is_gt).then_inc(over_flag, 1)
            dve.wait_ge(att_exp, 1)
            link(v.tensor_reduce(att_red, att, AX_X, ALU.add))
            link(v.reciprocal(att_inv, att_red))
            v.tensor_tensor(att, att, att_inv.unsqueeze(2).to_broadcast([P, NB, R]),
                            ALU.mult).then_inc(att_ready, 1)

            dve.wait_ge(over_ps, 1)
            v.tensor_copy(over[:], ps[:, 1, 0:1]).then_inc(over_ready, 1)

            for b in range(NB):
                dve.wait_ge(tr_sb, TR_H1 + b + 1)
                v.tensor_tensor(rows_lo[0][:, b, :], ps[:, 6 + (TR_H1 + b) % 2, :], rows_hi[:, b, :].bitcast(F32),
                                ALU.subtract).then_inc(lo_ready, 1)

            dve.wait_ge(over_ready, 1)
            n_over = dve.value_load(over[0:1, 0:1], min_val=0, max_val=P)

            def rest_tiles(layer, j):
                for s in range(NB):
                    n = (layer * NJ + j) * NB + s
                    span = counts[:, s, j * 512:(j + 1) * 512]
                    if n >= 2:
                        dve.wait_ge(rest_used, n - 1)
                    v.tensor_copy(cf_rest[:, n % 2, :], span).then_inc(rest_rounded, 1)
                    dve.wait_ge(rest_rounded, n + 1)
                    v.tensor_tensor(cf_rest[:, n % 2, :], span, cf_rest[:, n % 2, :].bitcast(F32),
                                    ALU.subtract).then_inc(rest_ready, 1)

            def count_tiles(layer, j, s0, s1):
                for s in range(s0, s1):
                    n = (layer * NJ + j) * NB + s
                    if s == NB - 1:
                        with dve.If(n_over > 0):
                            rest_tiles(layer, j)
                    if n >= 3:
                        dve.wait_ge(cf_used, n - 2)
                    v.tensor_copy(cf[:, n % 3, :], counts[:, s, j * 512:(j + 1) * 512]).then_inc(cf_ready, 1)

            for j in range(NJ):
                count_tiles(0, j, 0, NB)

            dve.wait_ge(beta_in, 64)
            v.tensor_scalar(odd_i, iota_pi[:], NE.bit_length() - 1, 1, ALU.logical_shift_right, ALU.bitwise_and)
            link(v.tensor_copy(beta_r[:], beta_sb[:]))
            v.tensor_copy(odd_part[:, 0:1], odd_i)
            link(v.tensor_tensor(beta_sb[:], beta_sb[:], beta_r[:].bitcast(F32), ALU.subtract))
            v.tensor_scalar(odd_part[:, 1:2], odd_part[:, 0:1], -1.0, 1.0, ALU.mult, ALU.add)
            link(v.tensor_scalar(beta_sb[:], beta_sb[:], odd_part[0:4 * NE, 0:1], None, ALU.mult))
            v.scalar_tensor_tensor(out=beta_r[:], in0=beta_r[:].bitcast(F32), scalar=odd_part[0:4 * NE, 1:2],
                                   in1=beta_sb[:], op0=ALU.mult, op1=ALU.add).then_inc(beta_ready, 1)

            dve.wait_ge(gnnw_in, 96)
            for b in range(NB):
                if b % GB == 0:
                    dve.wait_ge(x_again[b // GB], 16)
                dve.wait_ge(out_ps, b + 1)
                v.tensor_tensor(out_t[:, b % 2, :], ps[:, b % 4, :], row_bias[:], ALU.add).then_inc(out_read, 1)
                dve.wait_ge(out_read, b + 1)
                link(v.scalar_tensor_tensor(out=x_sb[:, b, :], in0=out_t[:, b % 2, :], scalar=0.0,
                                            in1=x_sb[:, b, :], op0=ALU.max, op1=ALU.add))
                for g0, g1 in GROUPS:
                    if b == g1 - 1:
                        row_norms(g0, g1)

            dve.wait_ge(router_ps, 1)
            link(v.tensor_copy(logits[:].rearrange("p b e -> p (b e)"), ps[:, 4, 0:NB * NE]))
            for b in range(NB):
                last = v.max(top_v[:, b, :], logits[:, b, :])
            link(last)
            for b in range(NB):
                last = v.max_index(top_i[:, b, :], top_v[:, b, :], logits[:, b, :])
            v.tensor_tensor(gate_d[:], top_v[:, :, 1], top_v[:, :, 0], ALU.subtract).then_inc(gate_diff, 1)
            link(last)
            for k in range(TOPK):
                last = v.tensor_copy(top_f[:, k, :], top_i[:, :, k])
            link(last)
            for k in range(TOPK):
                last = v.tensor_tensor(sel[:, k], iota_f[:, 0:NE].unsqueeze(1).to_broadcast([P, NB, NE]),
                                       top_f[:, k, :].unsqueeze(2).to_broadcast([P, NB, NE]), ALU.is_equal)
            link(last)
            v.tensor_tensor(sel_bf[:, (NB - 1) * NE:].rearrange("p (b e) -> p b e", e=NE), sel[:, 0], sel[:, 1],
                            ALU.add).then_inc(sel_ready, 1)
            dve.wait_ge(gate_exp, 1)
            link(v.tensor_scalar(gate_d[:], gate_e[:], 1.0, None, ALU.add))
            link(v.reciprocal(gates[:, 0, :], gate_d[:]))
            link(v.tensor_tensor(gates[:, 1, :], gates[:, 0, :], gate_e[:], ALU.mult))
            for k in range(TOPK):
                last = v.tensor_tensor(gate_w[:, k], sel[:, k], gates[:, k, :].unsqueeze(2).to_broadcast([P, NB, NE]),
                                       ALU.mult)
            link(last)
            link(v.tensor_tensor(gate_w[:, 0], gate_w[:, 0], gate_w[:, 1], ALU.add))

            dve.wait_ge(pos_ps, 1)
            link(v.tensor_scalar(cnt_i[:], ps[:, 2, 0:NE], float(P - 1), None, ALU.add))
            link(v.tensor_scalar(cnt_i[:], cnt_i[:], 7, 7, ALU.logical_shift_right, ALU.logical_shift_left))
            link(v.tensor_copy(cnt_f[:], cnt_i[:]))
            link(v.tensor_tensor_scan(end_f[:], one_f[:], cnt_f[:], 0.0, ALU.mult, ALU.add))
            link(v.tensor_tensor(off_f[:], end_f[:], cnt_f[:], ALU.subtract))
            link(v.tensor_tensor(pos, ps[:, 1, 0:NB * NE].rearrange("p (b e) -> p b e", e=NE),
                                 off_f[:].unsqueeze(1).to_broadcast([P, NB, NE]), ALU.add))
            for k in range(TOPK):
                link(v.tensor_tensor(pos_t, sel[:, k], pos, ALU.mult))
                link(v.tensor_reduce(slot_f[:, k, :], pos_t, AX_X, ALU.add))
            link(v.tensor_copy(slot_i[:], slot_f[:]))
            v.tensor_scalar(slot_hi[:], slot_i[:], 7, None, ALU.logical_shift_right)
            link(v.tensor_scalar(slot_lo[:], slot_i[:], P - 1, None, ALU.bitwise_and))
            v.tensor_copy(iota_b, iota_f[:])
            v.tensor_copy(block_b, block_col[:])
            v.tensor_copy(slot_hb, slot_hi[:])
            link(v.tensor_copy(slot_lb, slot_lo[:]))
            link(v.tensor_scalar(chunk_ef[:], iota_f[:, 0:SW], float(P), None, ALU.mult))
            link(v.tensor_tensor(chunk_ge, chunk_ef[:].unsqueeze(2).to_broadcast([P, SW, NE]),
                                 end_f[:].unsqueeze(1).to_broadcast([P, SW, NE]), ALU.is_ge))
            link(v.tensor_reduce(chunk_ef[:], chunk_ge, AX_X, ALU.add))
            v.tensor_scalar(chunk_e[:], chunk_ef[:], float(NE - 1), None, ALU.min).then_inc(tok_ready, 1)
            for k in range(TOPK):
                lo, hi = lo_oh[:, k], hi_oh[:, k]
                v.tensor_tensor(hi[:, :, 0:SW], iota_b[:, 0:SW].unsqueeze(1).to_broadcast([P, NB, SW]),
                                slot_hb[:, k, :].unsqueeze(2).to_broadcast([P, NB, SW]), ALU.is_equal)
                link(v.tensor_tensor(lo, iota_b.unsqueeze(1).to_broadcast([P, NB, P]),
                                     slot_lb[:, k, :].unsqueeze(2).to_broadcast([P, NB, P]), ALU.is_equal))
                link(v.tensor_tensor(hi[:, :, SW:2 * SW], hi[:, :, 0:SW],
                                     block_b.unsqueeze(2).to_broadcast([P, NB, SW]), ALU.mult))
                v.tensor_scalar(hi[:, :, 0:SW], hi[:, :, 0:SW], iota_p[:, 0:1], None, ALU.mult).then_inc(slot_oh, 1)
            dve.wait_ge(slot_ps, 1)
            link(v.tensor_scalar(tok_f[:], ps[:, 3, SW:2 * SW], float(P), None, ALU.mult))
            link(v.tensor_tensor(tok_f[:], tok_f[:], ps[:, 3, 0:SW], ALU.add))
            v.tensor_copy(tok[:], tok_f[:]).then_inc(tok_ready, 1)
            def hidden_bias(j, b, free):
                e = dve.value_load(chunk_e[0:1, bass.ds(j, 1)], min_val=0, max_val=NE - 1)
                dve.wait_ge(hid_ps, j + 1)
                if free is not None:
                    dve.wait_ge(hidT_ps, free)
                v.tensor_tensor(hb[:, b, :], ps[:, b, 0:F], b1_row[:, bass.ds(e * F, F)], ALU.add).then_inc(hid_sb, 1)

            def residual(j, b):
                dve.wait_ge(y_ps, j + 1)
                dve.wait_ge(xb_ready, j + 1)
                v.tensor_tensor(yt[:, b, :], ps[:, 2 + b, :], xb[:, b, :], ALU.add).then_inc(yt_ready, 1)
                dve.wait_ge(yt_ready, j + 1)
                v.bn_stats(e_stats[:, b, :], yt[:, b, :]).then_inc(es_ready, 1)
                dve.wait_ge(es_ready, j + 1)
                v.memset(nt_b[:, 0:1], 0.0)
                v.bn_aggr(e_mv[:, b, 0:2], e_stats[:, b, :]).then_inc(em_ready, 1)
                dve.wait_ge(em_ready, j + 1)
                v.tensor_scalar(e_mv[:, b, 2:3], e_mv[:, b, 1:2], EXPERT_EPS, None, ALU.add).then_inc(yv_ready, 1)

            def scaled(j, b, half):
                dve.wait_ge(sd_ready, j + 1)
                v.reciprocal(e_mv[:, b, 4:5], e_mv[:, b, 3:4]).then_inc(er_ready, 1)
                dve.wait_ge(er_ready, 4 * j + 1)
                v.scalar_tensor_tensor(out=e_mv[:, b, 5:6], in0=e_mv[:, b, 4:5], scalar=e_mv[:, b, 4:5],
                                       in1=e_mv[:, b, 2:3], op0=ALU.mult, op1=ALU.mult).then_inc(er_ready, 1)
                dve.wait_ge(er_ready, 4 * j + 2)
                v.tensor_scalar(e_mv[:, b, 6:7], e_mv[:, b, 5:6], -0.5, 1.5, ALU.mult, ALU.add).then_inc(er_ready, 1)
                dve.wait_ge(er_ready, 4 * j + 3)
                v.tensor_tensor(e_mv[:, b, 7:8], e_mv[:, b, 6:7], e_mv[:, b, 4:5], ALU.mult).then_inc(er_ready, 1)
                dve.wait_ge(er_ready, 4 * j + 4)
                if half is not None:
                    dve.wait_ge(y_out[b], 16 * half)
                v.tensor_scalar(yu[:, b, :], yt[:, b, :], e_mv[:, b, 0:1], e_mv[:, b, 7:8],
                                ALU.subtract, ALU.mult).then_inc(yu_ready, 1)

            dve.wait_ge(ffn_rows_in, 48)
            hidden_bias(0, 0, None)
            hidden_bias(1, 1, None)
            residual(0, 0)
            hidden_bias(2, 0, 1)
            scaled(0, 0, None)
            residual(1, 1)
            hidden_bias(3, 1, 2)
            scaled(1, 1, None)
            residual(2, 0)
            with dve.Fori(0, (NCH - 5) // 2) as i:
                for u in range(2):
                    hidden_bias(2 * i + (4 + u), u, 2 * i + (3 + u))
                    scaled(2 * i + (2 + u), u, i + 1)
                    residual(2 * i + (3 + u), 1 - u)
            hidden_bias(NCH - 1, 0, NCH - 2)
            scaled(NCH - 3, 0, (NCH - 3) // 2)
            residual(NCH - 2, 1)
            scaled(NCH - 2, 1, (NCH - 2) // 2)
            residual(NCH - 1, 0)
            scaled(NCH - 1, 0, (NCH - 1) // 2)

            for k in range(2):
                last = v.tensor_copy(gate_r[:, :, k, :], gate_w[:, 0])
            link(last)
            for k in range(2):
                last = v.tensor_tensor(gate_r[:, :, 2 + k, :], gate_w[:, 0], gate_r[:, :, k, :].bitcast(F32),
                                       ALU.subtract)
            last.then_inc(gatew_ready, 1)
            for b in range(NB):
                dve.wait_ge(beta_ps, b + 1)
                last = v.tensor_tensor(x_sb[:, b, :], x_sb[:, b, :], ps[:, b % 6, :], ALU.add)
                last.then_inc(beta_read, 1)
            dve.wait_ge(beta_read, NB)
            v.tensor_copy(ones_r, ones_bf[:]).then_inc(ones_r_ready, 1)
            for g0, g1 in L3_GROUPS:
                for k in range(TOPK):
                    for b in range(g0, g1):
                        if k == 0:
                            dve.wait_ge(y_top_in[b], 16 * TOPK)
                        last = v.scalar_tensor_tensor(out=x_sb[:, b, :], in0=y_top[k][:, b, :],
                                                      scalar=gates[:, k, b:b + 1], in1=x_sb[:, b, :],
                                                      op0=ALU.mult, op1=ALU.add)
                    link(last)
                row_norms(g0, g1, True)
                if g0 > 0:
                    count_tiles(1, 0, *before)
                before = g0, g1
            count_tiles(1, 0, *before)

            def mean_span(j):
                dve.wait_ge(cf_used, (NJ + j + 1) * NB)
                link(v.tensor_scalar(deg_inv, ps[:, DEG_BANKS[j], :], 1.0, None, ALU.max))
                v.reciprocal(deg_inv, deg_inv).then_inc(deg_read, 1)
                dve.wait_ge(deg_read, j + 1)
                for m in range(DC):
                    dve.wait_ge(agg_sb, (NJ + j) * DC + m + 1)
                    part = hT[:, m, j * 512:(j + 1) * 512]
                    v.tensor_tensor(part, part, deg_inv, ALU.mult).then_inc(mean_ready, 1)

            for j in range(1, NJ):
                count_tiles(1, j, 0, 3)
                mean_span(j - 1)
                count_tiles(1, j, 3, NB)
            mean_span(NJ - 1)

            def alu_step(g0, g1):
                n = g1 - g0
                hot_g = hot[:, g0:g1].rearrange("p b (g i) -> p (b g) i", i=16)
                nib_g = nib[:, g0:g1].rearrange("p b c -> p (b c)")
                none_g = nib_none[:, g0:g1].rearrange("p b c -> p (b c)")
                flag_g, mark_g, twice, val_g, left, right, whole, ni_g, oh_g = [
                    t[:, g0:g1] for t in (is_op, mark, amp, val_i, shl_i, shr_i, res_i, out_ni, out_oh)]
                v.tensor_scalar(flag_g, xn[:, g0:g1, 39:41], 0.5, None, ALU.is_gt)
                v.tensor_scalar(mark_g, xn[:, g0:g1, 0], 0.5, None, ALU.is_gt)
                link(v.tensor_scalar(hot[:, g0:g1], xn[:, g0:g1, 64:112], 0.5, None, ALU.is_gt))
                link(v.tensor_tensor(hot_g, hot_g, first_key[:].unsqueeze(1).to_broadcast([P, n * 3, 16]), ALU.mult))
                link(v.tensor_reduce(nib_g, hot_g, AX_X, ALU.max))
                v.scalar_tensor_tensor(out=flag_g[:, :, 1], in0=flag_g[:, :, 0], scalar=0.5, in1=flag_g[:, :, 1],
                                       op0=ALU.is_lt, op1=ALU.mult)
                link(v.tensor_scalar(none_g, nib_g, 0.0, 16.0, ALU.is_gt, ALU.mult))
                v.tensor_tensor(flag_g, flag_g, mark_g.unsqueeze(2).to_broadcast([P, n, 2]), ALU.mult)
                link(v.tensor_tensor(nib_g, none_g, nib_g, ALU.subtract))
                v.scalar_tensor_tensor(out=val_g, in0=nib[:, g0:g1, 1], scalar=16.0, in1=nib[:, g0:g1, 0],
                                       op0=ALU.mult, op1=ALU.add)
                v.tensor_tensor(twice, flag_g[:, :, 0], flag_g[:, :, 1], ALU.add)
                link(v.tensor_copy(sa_i[:, g0:g1], nib[:, g0:g1, 2]))
                v.tensor_tensor(left, val_g, sa_i[:, g0:g1], ALU.logical_shift_left)
                link(v.tensor_tensor(right, val_g, sa_i[:, g0:g1], ALU.logical_shift_right))
                link(v.tensor_scalar(left, left, 255, None, ALU.bitwise_and))
                v.tensor_tensor(shl_f[:, g0:g1], left, flag_g[:, :, 0], ALU.mult)
                link(v.tensor_tensor(shr_f[:, g0:g1], right, flag_g[:, :, 1], ALU.mult))
                link(v.tensor_tensor(val_f[:, g0:g1], shl_f[:, g0:g1], shr_f[:, g0:g1], ALU.add))
                link(v.tensor_scalar(whole, val_f[:, g0:g1], 0.0, 255.0, ALU.max, ALU.min))
                v.tensor_scalar(ni_g[:, :, 0], whole, 15, None, ALU.bitwise_and)
                link(v.tensor_scalar(ni_g[:, :, 1], whole, 4, None, ALU.logical_shift_right))
                link(v.tensor_tensor(oh_g, iota_i[:, 0:16].unsqueeze(1).unsqueeze(1).to_broadcast([P, n, 2, 16]),
                                     ni_g.unsqueeze(3).to_broadcast([P, n, 2, 16]), ALU.is_equal))
                oh = oh_g.rearrange("p b k i -> p b (k i)")
                link(v.scalar_tensor_tensor(out=oh, in0=oh, scalar=2.0, in1=twice.unsqueeze(2).to_broadcast([P, n, 32]),
                                            op0=ALU.mult, op1=ALU.mult))
                dve.wait_ge(added, g1)
                v.tensor_tensor(x_sb[:, g0:g1, 128:160], x_sb[:, g0:g1, 128:160], oh, ALU.add).then_inc(fin_ready, 1)

            dve.wait_ge(l1w_in, 64)
            for n, (g0, g1) in enumerate(L1_GROUPS):
                for b in range(g0, g1):
                    dve.wait_ge(l1_ps, b + 1)
                    v.tensor_tensor(xn[:, b, :], ps[:, L1_BANKS[b % 8], :], row_bias[:], ALU.add).then_inc(l1_read, 1)
                    dve.wait_ge(l1_read, b + 1)
                    last = v.bn_stats(stats[:, b, :], xn[:, b, :])
                link(last)
                row_scales(g0, g1, True)
                for a0, a1 in ALU_GROUPS:
                    if n >= 2 and a1 == L1_GROUPS[n - 2][1]:
                        dve.wait_ge(xn_ready, 3 * NB + a1)
                        alu_step(a0, a1)
                for b in range(g0, g1):
                    dve.wait_ge(hn_ready, b + 1)
                    v.tensor_tensor(xn[:, b, :], xn[:, b, :], l1g_row, ALU.mult).then_inc(gamma_done, 1)
                dve.wait_ge(gamma_done, g1)
                last = v.tensor_tensor(xn[:, g1 - 1, :], xn[:, g1 - 1, :], l1b_row, ALU.add)
                for b in range(g0, g1):
                    if b == g1 - 1:
                        link(last)
                    else:
                        dve.wait_ge(beta_done, b - n + 1)
                    add = v.scalar_tensor_tensor(out=x_sb[:, b, :], in0=xn[:, b, :], scalar=0.0, in1=x_sb[:, b, :],
                                                 op0=ALU.max, op1=ALU.add)
                link(add)
                row_norms(g0, g1, True)
            dve.wait_ge(xn_ready, 4 * NB)
            alu_step(*ALU_GROUPS[-1])


_OUTS = [((1536, 512), 'float32')]


def kernel(**inputs):
    import numpy as np
    import concourse.bacc as bacc
    from concourse import mybir as mb
    from concourse.bass_utils import run_bass_kernel_spmd as run

    def cols(a):
        return np.asarray(a).reshape(-1, 128).T

    g = {k: np.asarray(v) for k, v in inputs.items()}
    img0 = g['L0_gnn_img_feats'][0]
    laid = {
        'x': g['x'],
        'src': g['src'].reshape(-1, 128).T, 'dst': g['dst'].reshape(-1, 128).T,
        'img': img0.T.reshape(-1, 128, img0.shape[0]).transpose(1, 0, 2),
        'wf': g['L0_gnn_Wf'], 'bf': cols(g['L0_gnn_bf']), 'wi': g['L0_gnn_Wi'], 'bi': cols(g['L0_gnn_bi']),
        'wa': cols(g['L0_gnn_Wa']), 'ba': g['L0_gnn_ba'],
        'wn': g['L0_gnn_Wn'], 'bn': cols(g['L0_gnn_bn']),
        'wim': g['L0_gnn_Wim'], 'bim': cols(g['L0_gnn_bim']),
        'wap': g['L0_gnn_Wap'], 'bap': g['L0_gnn_bap'],
        'router': g['L0_ffn_router_w'], 'w1': g['L0_ffn_w1'], 'b1': g['L0_ffn_b1'].reshape(-1),
        'w2': g['L0_ffn_w2'], 'b2': g['L0_ffn_b2'].reshape(-1),
        'ffn_gamma': g['L0_ffn_gamma'].reshape(-1), 'ffn_beta': g['L0_ffn_beta'],
        'w_self': g['L1_gnn_w_self'].T, 'w_neigh': g['L1_gnn_w_neigh'].T,
        'l1_bias': g['L1_gnn_bias'], 'l1_gamma': g['L1_gnn_gamma'], 'l1_beta': g['L1_gnn_beta'],
    }
    nc = bacc.Bacc("TRN2", target_bir_lowering=False, num_devices=1)
    arrays, args = {}, []
    for name, a in laid.items():
        a = np.ascontiguousarray(a)
        arrays[f"in_{name}_dram"] = a
        args.append(nc.dram_tensor(f"in_{name}_dram", a.shape, mb.dt.from_np(a.dtype), kind="ExternalInput").ap())
    for i, (shape, dtype) in enumerate(_OUTS):
        dt = mb.dt.from_np(np.dtype(dtype))
        args.append(nc.dram_tensor(f"out_{i}_dram", shape, dt, kind="ExternalOutput").ap())
    args.append(nc.dram_tensor("tokens_dram", (1536, 512), mb.dt.float32, kind="Internal").ap())
    args.append(nc.dram_tensor("expert_rows_dram", (31 * 128, 512), mb.dt.float32, kind="Internal").ap())
    gnn_moe_kernel(nc, *args)
    r = run(nc, [arrays], core_ids=[0])
    return r.results[0]["out_0_dram"]
```
